# Optimizing a Trainium2 kernel written in Bass

```python
import numpy as np
import jax
import jax.numpy as jnp

def _softmax(x, axis=-1):
    return jax.nn.softmax(x, axis=axis)

def _gelu(x):
    return jax.nn.gelu(x, approximate=True)

def _silu(x):
    return jax.nn.silu(x)

def _sigmoid(x):
    return jax.nn.sigmoid(x)

def _layernorm(x, axis=-1, eps=1e-05):
    m = jnp.mean(x, axis=axis, keepdims=True)
    v = jnp.var(x, axis=axis, keepdims=True)
    return (x - m) / jnp.sqrt(v + eps)

def _scatter_add(tgt, idx, src, axis=0):
    return tgt.at[idx].add(src)

def _segment_sum(src, seg, n):
    return jax.ops.segment_sum(src, seg, n)
kernel_name = 'mk_recurrent_d4_jaxref_r8_51d1ce'

def setup_inputs(seed: int=0):
    np.random.seed(seed)
    _w = jnp.asarray

    def _L0_attn_setup():
        import jax, jax.numpy as jnp
        import numpy as np
        B, S, D, H = (4, 256, 128, 16)
        DH = D // H
        key = jax.random.key(seed)
        ks = jax.random.split(key, 5)
        std = 1.0 / np.sqrt(D)
        return {'x': jax.random.normal(ks[0], (B, S, D), dtype=jnp.float32), 'mask': jnp.ones((S, S), dtype=bool), 'Wq': jax.random.normal(ks[1], (D, D), dtype=jnp.float32) * std, 'Wk': jax.random.normal(ks[2], (D, D), dtype=jnp.float32) * std, 'Wv': jax.random.normal(ks[3], (D, D), dtype=jnp.float32) * std, 'Wout': jax.random.normal(ks[4], (D, D), dtype=jnp.float32) * std}
    _L0_attn_in = _L0_attn_setup()

    def _L0_ffn_setup():
        import jax, jax.numpy as jnp
        import numpy as np
        D_MODEL = 128
        M = 64
        INNER = 16
        key = jax.random.key(seed)
        ks = jax.random.split(key, 9)

        def init(k, shape, fan_in):
            bound = 1.0 / np.sqrt(fan_in)
            return jax.random.uniform(k, shape, jnp.float32, -bound, bound)
        x = jax.random.normal(ks[0], (16, 512, D_MODEL), dtype=jnp.float32)
        Win = init(ks[1], (D_MODEL, M), D_MODEL)
        bin_ = init(ks[2], (M,), D_MODEL)
        W1 = init(ks[3], (M, INNER), 1)
        b1 = init(ks[4], (M, INNER), 1)
        W2 = init(ks[5], (M, INNER), INNER)
        b2 = init(ks[6], (M,), INNER)
        Wout = init(ks[7], (M, D_MODEL), M)
        bout = init(ks[8], (D_MODEL,), M)
        return {'x': x, 'Win': Win, 'bin_': bin_, 'W1': W1, 'b1': b1, 'W2': W2, 'b2': b2, 'Wout': Wout, 'bout': bout}
    _L0_ffn_in = _L0_ffn_setup()

    def _L1_attn_setup():
        import jax, jax.numpy as jnp
        import numpy as np
        EPS = 1e-06
        N_HEADS = 16

        def _heads(t, B, N, H, Dk):
            return t.reshape(B, N, H, Dk).transpose(0, 2, 1, 3)
        key = jax.random.key(seed)
        ks = jax.random.split(key, 5)
        B, N, D = (64, 64, 128)
        x = jax.random.normal(ks[0], (B, N, D), dtype=jnp.float32)
        s = 0.02
        W_q = jax.random.normal(ks[1], (D, D), dtype=jnp.float32) * s
        W_k = jax.random.normal(ks[2], (D, D), dtype=jnp.float32) * s
        W_v = jax.random.normal(ks[3], (D, D), dtype=jnp.float32) * s
        W_o = jax.random.normal(ks[4], (D, D), dtype=jnp.float32) * s
        z = jnp.zeros((D,), dtype=jnp.float32)
        return {'x': x, 'W_q': W_q, 'b_q': z, 'W_k': W_k, 'b_k': z, 'W_v': W_v, 'b_v': z, 'W_o': W_o, 'b_o': z}
    _L1_attn_in = _L1_attn_setup()

    def _L1_ffn_setup():
        import jax, jax.numpy as jnp
        import numpy as np
        B, S, D, E = (2, 512, 128, 8)
        key = jax.random.key(seed)
        ks = jax.random.split(key, 7)
        s = 1.0 / np.sqrt(D)
        return {'x': jax.random.normal(ks[0], (B, S, D), jnp.float32), 'Ws': jax.random.normal(ks[1], (E, D), jnp.float32) * s, 'bs': jax.random.normal(ks[2], (E,), jnp.float32) * s, 'W1': jax.random.normal(ks[3], (E, D, D), jnp.float32) * s, 'b1': jax.random.normal(ks[4], (E, D), jnp.float32) * s, 'W2': jax.random.normal(ks[5], (E, D, D), jnp.float32) * s, 'b2': jax.random.normal(ks[6], (E, D), jnp.float32) * s}
    _L1_ffn_in = _L1_ffn_setup()

    def _L2_attn_setup():
        import jax, jax.numpy as jnp
        import numpy as np
        import math
        D_MODEL, D_STATE, D_CONV = (128, 16, 4)
        D_INNER = 2 * D_MODEL
        DT_RANK = math.ceil(D_MODEL / 16)
        B, L = (4, 256)

        def _layernorm(x, g, b, eps=1e-05):
            m = jnp.mean(x, axis=-1, keepdims=True)
            v = jnp.mean(jnp.square(x - m), axis=-1, keepdims=True)
            return (x - m) * jax.lax.rsqrt(v + eps) * g + b

        def _mamba(xn, W_in, conv_w, conv_b, W_xp, W_dt, dt_bias, A_log, D_skip, W_out):
            xz = xn @ W_in
            xi, z = jnp.split(xz, 2, axis=-1)
            xi_t = jnp.transpose(xi, (0, 2, 1))
            xc = jax.lax.conv_general_dilated(xi_t, conv_w, window_strides=(1,), padding=[(D_CONV - 1, 0)], feature_group_count=D_INNER, dimension_numbers=('NCH', 'OIH', 'NCH'))
            xc = jnp.transpose(xc, (0, 2, 1)) + conv_b
            xc = jax.nn.silu(xc)
            x_dbl = xc @ W_xp
            dt_lo, Bm, Cm = jnp.split(x_dbl, [DT_RANK, DT_RANK + D_STATE], axis=-1)
            delta = jax.nn.softplus(dt_lo @ W_dt + dt_bias)
            A = -jnp.exp(A_log)

            def step(h, inp):
                dt_t, B_t, C_t, u_t = inp
                dA = jnp.exp(dt_t[..., None] * A)
                h = h * dA + (dt_t * u_t)[..., None] * B_t[:, None, :]
                y = jnp.einsum('bdn,bn->bd', h, C_t)
                return (h, y)
            h0 = jnp.zeros((xn.shape[0], D_INNER, D_STATE), xn.dtype)
            inputs = (jnp.transpose(delta, (1, 0, 2)), jnp.transpose(Bm, (1, 0, 2)), jnp.transpose(Cm, (1, 0, 2)), jnp.transpose(xc, (1, 0, 2)))
            _, ys = jax.lax.scan(step, h0, inputs)
            y = jnp.transpose(ys, (1, 0, 2)) + xc * D_skip
            y = y * jax.nn.silu(z)
            return y @ W_out
        key = jax.random.key(seed)
        ks = jax.random.split(key, 10)
        s = 0.02
        x = jax.random.normal(ks[0], (B, L, D_MODEL), dtype=jnp.float32)
        ln_g = jnp.ones((D_MODEL,), jnp.float32)
        ln_b = jnp.zeros((D_MODEL,), jnp.float32)
        W_in = jax.random.normal(ks[1], (D_MODEL, 2 * D_INNER), jnp.float32) * s
        conv_w = jax.random.normal(ks[2], (D_INNER, 1, D_CONV), jnp.float32) * s
        conv_b = jnp.zeros((D_INNER,), jnp.float32)
        W_xp = jax.random.normal(ks[3], (D_INNER, DT_RANK + 2 * D_STATE), jnp.float32) * s
        W_dt = jax.random.normal(ks[4], (DT_RANK, D_INNER), jnp.float32) * DT_RANK ** (-0.5)
        dt_bias = jnp.full((D_INNER,), float(np.log(np.expm1(0.01))), jnp.float32)
        A_log = jnp.log(jnp.broadcast_to(jnp.arange(1, D_STATE + 1, dtype=jnp.float32), (D_INNER, D_STATE)))
        D_skip = jnp.ones((D_INNER,), jnp.float32)
        W_out = jax.random.normal(ks[5], (D_INNER, D_MODEL), jnp.float32) * s
        return dict(x=x, ln_g=ln_g, ln_b=ln_b, W_in=W_in, conv_w=conv_w, conv_b=conv_b, W_xp=W_xp, W_dt=W_dt, dt_bias=dt_bias, A_log=A_log, D_skip=D_skip, W_out=W_out)
    _L2_attn_in = _L2_attn_setup()

    def _L2_ffn_setup():
        import jax, jax.numpy as jnp
        import numpy as np
        D_MODEL = 128
        D_HIDDEN = 512
        NUM_BANKS = 16
        NUM_SELECTED = 2
        key = jax.random.key(seed)
        ks = jax.random.split(key, 7)
        s = 0.02
        return {'tensor': jax.random.normal(ks[0], (4, 128, D_MODEL), dtype=jnp.float32), 'Wr': jax.random.normal(ks[1], (D_MODEL, NUM_BANKS), dtype=jnp.float32) * s, 'br': jnp.zeros((NUM_BANKS,), dtype=jnp.float32), 'W1': jax.random.normal(ks[2], (NUM_BANKS, D_MODEL, D_HIDDEN), dtype=jnp.float32) * s, 'b1': jnp.zeros((NUM_BANKS, D_HIDDEN), dtype=jnp.float32), 'W2': jax.random.normal(ks[3], (NUM_BANKS, D_HIDDEN, D_MODEL), dtype=jnp.float32) * s, 'b2': jnp.zeros((NUM_BANKS, D_MODEL), dtype=jnp.float32)}
    _L2_ffn_in = _L2_ffn_setup()

    def _L3_attn_setup():
        import jax, jax.numpy as jnp
        import numpy as np
        B, S, H = (2, 256, 128)
        NUM_HEADS = 16
        HEAD_DIM = H // NUM_HEADS
        key = jax.random.key(seed)
        ks = jax.random.split(key, 5)
        sc = 1.0 / np.sqrt(H)
        return {'hidden_states': jax.random.normal(ks[0], (B, S, H), jnp.float32), 'Wq': jax.random.normal(ks[1], (H, H), jnp.float32) * sc, 'bq': jnp.zeros((H,), jnp.float32), 'Wk': jax.random.normal(ks[2], (H, H), jnp.float32) * sc, 'bk': jnp.zeros((H,), jnp.float32), 'Wv': jax.random.normal(ks[3], (H, H), jnp.float32) * sc, 'bv': jnp.zeros((H,), jnp.float32), 'Wg': jax.random.normal(ks[4], (H, 1), jnp.float32) * sc, 'bg': jnp.zeros((1,), jnp.float32)}
    _L3_attn_in = _L3_attn_setup()

    def _L3_ffn_setup():
        import jax, jax.numpy as jnp
        import numpy as np
        DIM = 128
        DEPTH = 2
        HEADS = 8
        DIM_HEAD = 64
        WINDOW = 64
        INNER = HEADS * DIM_HEAD
        HID = int(DIM * 4 * 2 / 3)
        B, N = (2, 1024)
        QK_SCALE = 8.0

        def shift_token(t):
            t1, t2 = jnp.split(t, 2, axis=-1)
            t2 = jnp.pad(t2, ((0, 0), (1, 0), (0, 0)))[:, :-1]
            return jnp.concatenate([t1, t2], axis=-1)

        def l2norm(t):
            return t / jnp.clip(jnp.linalg.norm(t, axis=-1, keepdims=True), 1e-12)

        def rotate_half(x):
            x1, x2 = jnp.split(x, 2, axis=-1)
            return jnp.concatenate([-x2, x1], axis=-1)

        def rotary_xpos(q, k):
            n = q.shape[-2]
            half_idx = jnp.arange(0, DIM_HEAD, 2, dtype=jnp.float32)
            inv_freq = 1.0 / 10000.0 ** (half_idx / DIM_HEAD)
            t = jnp.arange(n, dtype=jnp.float32)
            freqs = t[:, None] * inv_freq[None, :]
            freqs = jnp.concatenate([freqs, freqs], axis=-1)
            base = (half_idx + 0.4 * DIM_HEAD) / (1.4 * DIM_HEAD)
            power = (t - n // 2) / float(WINDOW // 2)
            scale = base[None, :] ** power[:, None]
            scale = jnp.concatenate([scale, scale], axis=-1)
            cos, sin = (jnp.cos(freqs), jnp.sin(freqs))
            q = q * cos * scale + rotate_half(q) * sin * scale
            k = k * cos / scale + rotate_half(k) * sin / scale
            return (q, k)

        def local_attention(q, k, v):
            b, h, n, d = q.shape
            w = n // WINDOW
            bq = q.reshape(b, h, w, WINDOW, d) * QK_SCALE
            bk = k.reshape(b, h, w, WINDOW, d)
            bv = v.reshape(b, h, w, WINDOW, d)

            def look_around(t):
                p = jnp.pad(t, ((0, 0), (0, 0), (1, 0), (0, 0), (0, 0)))
                return jnp.concatenate([p[:, :, :w], p[:, :, 1:]], axis=3)
            bk, bv = (look_around(bk), look_around(bv))
            bt = jnp.arange(n).reshape(w, WINDOW)
            btp = jnp.pad(bt, ((1, 0), (0, 0)), constant_values=-1)
            btk = jnp.concatenate([btp[:w], btp[1:]], axis=1)
            sim = jnp.einsum('bhwid,bhwjd->bhwij', bq, bk)
            i = bt[:, :, None]
            j = btk[:, None, :]
            mask = (i < j) | (i > j + WINDOW) | (j == -1)
            sim = jnp.where(mask, -jnp.finfo(sim.dtype).max, sim)
            attn = jax.nn.softmax(sim, axis=-1)
            out = jnp.einsum('bhwij,bhwjd->bhwid', attn, bv)
            return out.reshape(b, h, n, d)

        def _layer(x, wqkv, qs, ksc, wo, lg, lb, w1, b1, w2, b2):
            b, n, _ = x.shape
            h = shift_token(x)
            qkv = h @ wqkv
            q, k, v = jnp.split(qkv, 3, axis=-1)
            to_heads = lambda t: t.reshape(b, n, HEADS, DIM_HEAD).transpose(0, 2, 1, 3)
            q, k, v = (to_heads(q), to_heads(k), to_heads(v))
            q = l2norm(q) * qs
            k = l2norm(k) * ksc
            q, k = rotary_xpos(q, k)
            o = local_attention(q, k, v)
            o = o.transpose(0, 2, 1, 3).reshape(b, n, INNER)
            x = x + o @ wo
            h = shift_token(x)
            mu = h.mean(-1, keepdims=True)
            var = h.var(-1, keepdims=True)
            h = (h - mu) / jnp.sqrt(var + 1e-05) * lg + lb
            h = h @ w1 + b1
            a, g = jnp.split(h, 2, axis=-1)
            h = a * jax.nn.gelu(g, approximate=False)
            x = x + h @ w2 + b2
            return x
        key = jax.random.key(seed)
        ks = jax.random.split(key, 6)
        return {'x': jax.random.normal(ks[0], (B, N, DIM), jnp.float32), 'wqkv': jax.random.normal(ks[1], (DEPTH, DIM, 3 * INNER), jnp.float32) * 0.02, 'q_scale': jnp.ones((DEPTH, DIM_HEAD), jnp.float32), 'k_scale': jnp.ones((DEPTH, DIM_HEAD), jnp.float32), 'wo': jax.random.normal(ks[2], (DEPTH, INNER, DIM), jnp.float32) * 0.02, 'ln_g': jnp.ones((DEPTH, DIM), jnp.float32), 'ln_b': jnp.zeros((DEPTH, DIM), jnp.float32), 'w1': jax.random.normal(ks[3], (DEPTH, DIM, 2 * HID), jnp.float32) * 0.02, 'b1': jnp.zeros((DEPTH, 2 * HID), jnp.float32), 'w2': jax.random.normal(ks[4], (DEPTH, HID, DIM), jnp.float32) * 0.02, 'b2': jnp.zeros((DEPTH, DIM), jnp.float32)}
    _L3_ffn_in = _L3_ffn_setup()
    _d = {'L0_attn_x': _L0_attn_in['x'], 'L0_attn_mask': _L0_attn_in['mask'], 'L0_attn_Wq': _L0_attn_in['Wq'], 'L0_attn_Wk': _L0_attn_in['Wk'], 'L0_attn_Wv': _L0_attn_in['Wv'], 'L0_attn_Wout': _L0_attn_in['Wout'], 'L0_ffn_Win': _L0_ffn_in['Win'], 'L0_ffn_bin_': _L0_ffn_in['bin_'], 'L0_ffn_W1': _L0_ffn_in['W1'], 'L0_ffn_b1': _L0_ffn_in['b1'], 'L0_ffn_W2': _L0_ffn_in['W2'], 'L0_ffn_b2': _L0_ffn_in['b2'], 'L0_ffn_Wout': _L0_ffn_in['Wout'], 'L0_ffn_bout': _L0_ffn_in['bout'], 'L1_attn_W_q': _L1_attn_in['W_q'], 'L1_attn_b_q': _L1_attn_in['b_q'], 'L1_attn_W_k': _L1_attn_in['W_k'], 'L1_attn_b_k': _L1_attn_in['b_k'], 'L1_attn_W_v': _L1_attn_in['W_v'], 'L1_attn_b_v': _L1_attn_in['b_v'], 'L1_attn_W_o': _L1_attn_in['W_o'], 'L1_attn_b_o': _L1_attn_in['b_o'], 'L1_ffn_Ws': _L1_ffn_in['Ws'], 'L1_ffn_bs': _L1_ffn_in['bs'], 'L1_ffn_W1': _L1_ffn_in['W1'], 'L1_ffn_b1': _L1_ffn_in['b1'], 'L1_ffn_W2': _L1_ffn_in['W2'], 'L1_ffn_b2': _L1_ffn_in['b2'], 'L2_attn_ln_g': _L2_attn_in['ln_g'], 'L2_attn_ln_b': _L2_attn_in['ln_b'], 'L2_attn_W_in': _L2_attn_in['W_in'], 'L2_attn_conv_w': _L2_attn_in['conv_w'], 'L2_attn_conv_b': _L2_attn_in['conv_b'], 'L2_attn_W_xp': _L2_attn_in['W_xp'], 'L2_attn_W_dt': _L2_attn_in['W_dt'], 'L2_attn_dt_bias': _L2_attn_in['dt_bias'], 'L2_attn_A_log': _L2_attn_in['A_log'], 'L2_attn_D_skip': _L2_attn_in['D_skip'], 'L2_attn_W_out': _L2_attn_in['W_out'], 'L2_ffn_Wr': _L2_ffn_in['Wr'], 'L2_ffn_br': _L2_ffn_in['br'], 'L2_ffn_W1': _L2_ffn_in['W1'], 'L2_ffn_b1': _L2_ffn_in['b1'], 'L2_ffn_W2': _L2_ffn_in['W2'], 'L2_ffn_b2': _L2_ffn_in['b2'], 'L3_attn_Wq': _L3_attn_in['Wq'], 'L3_attn_bq': _L3_attn_in['bq'], 'L3_attn_Wk': _L3_attn_in['Wk'], 'L3_attn_bk': _L3_attn_in['bk'], 'L3_attn_Wv': _L3_attn_in['Wv'], 'L3_attn_bv': _L3_attn_in['bv'], 'L3_attn_Wg': _L3_attn_in['Wg'], 'L3_attn_bg': _L3_attn_in['bg'], 'L3_ffn_wqkv': _L3_ffn_in['wqkv'], 'L3_ffn_q_scale': _L3_ffn_in['q_scale'], 'L3_ffn_k_scale': _L3_ffn_in['k_scale'], 'L3_ffn_wo': _L3_ffn_in['wo'], 'L3_ffn_ln_g': _L3_ffn_in['ln_g'], 'L3_ffn_ln_b': _L3_ffn_in['ln_b'], 'L3_ffn_w1': _L3_ffn_in['w1'], 'L3_ffn_b1': _L3_ffn_in['b1'], 'L3_ffn_w2': _L3_ffn_in['w2'], 'L3_ffn_b2': _L3_ffn_in['b2']}
    _x0 = _d['L0_attn_x']
    _d['L0_attn_x'] = jax.random.normal(jax.random.fold_in(jax.random.key(seed), 1), (16, 256, 128), dtype=_x0.dtype)
    del _x0
    return _d

def reference(L0_attn_x, L0_attn_mask, L0_attn_Wq, L0_attn_Wk, L0_attn_Wv, L0_attn_Wout, L0_ffn_Win, L0_ffn_bin_, L0_ffn_W1, L0_ffn_b1, L0_ffn_W2, L0_ffn_b2, L0_ffn_Wout, L0_ffn_bout, L1_attn_W_q, L1_attn_b_q, L1_attn_W_k, L1_attn_b_k, L1_attn_W_v, L1_attn_b_v, L1_attn_W_o, L1_attn_b_o, L1_ffn_Ws, L1_ffn_bs, L1_ffn_W1, L1_ffn_b1, L1_ffn_W2, L1_ffn_b2, L2_attn_ln_g, L2_attn_ln_b, L2_attn_W_in, L2_attn_conv_w, L2_attn_conv_b, L2_attn_W_xp, L2_attn_W_dt, L2_attn_dt_bias, L2_attn_A_log, L2_attn_D_skip, L2_attn_W_out, L2_ffn_Wr, L2_ffn_br, L2_ffn_W1, L2_ffn_b1, L2_ffn_W2, L2_ffn_b2, L3_attn_Wq, L3_attn_bq, L3_attn_Wk, L3_attn_bk, L3_attn_Wv, L3_attn_bv, L3_attn_Wg, L3_attn_bg, L3_ffn_wqkv, L3_ffn_q_scale, L3_ffn_k_scale, L3_ffn_wo, L3_ffn_ln_g, L3_ffn_ln_b, L3_ffn_w1, L3_ffn_b1, L3_ffn_w2, L3_ffn_b2):

    def _L0_attn_ref(x, mask, Wq, Wk, Wv, Wout):
        import jax, jax.numpy as jnp
        import numpy as np
        B, S, D, H = (4, 256, 128, 16)
        DH = D // H
        n, s, d = x.shape
        scale = 1.0 / np.sqrt(DH).astype(np.float32)
        q = (x @ Wq).reshape(n, s, H, DH)
        k = (x @ Wk).reshape(n, s, H, DH)
        v = (x @ Wv).reshape(n, s, H, DH)
        attn = jnp.einsum('nqhd,nkhd->nqkh', q, k) * scale
        attn = jax.nn.softmax(attn, axis=-2)
        z = jnp.einsum('nqkh,nkhd->nqhd', attn, v).reshape(n, s, d)
        z = jnp.einsum('nqd,de->nqe', z, Wout)
        return x + z

    def _L0_ffn_ref(x, Win, bin_, W1, b1, W2, b2, Wout, bout):
        import jax, jax.numpy as jnp
        import numpy as np
        D_MODEL = 128
        M = 64
        INNER = 16
        s = jnp.einsum('btd,dm->btm', x, Win) + bin_
        h = jax.nn.relu(s[..., None] * W1 + b1)
        g = jnp.einsum('btmh,mh->btm', h, W2) + b2
        out = jnp.einsum('btm,md->btd', g, Wout) + bout
        return out

    def _L1_attn_ref(x, W_q, b_q, W_k, b_k, W_v, b_v, W_o, b_o):
        import jax, jax.numpy as jnp
        import numpy as np
        EPS = 1e-06
        N_HEADS = 16

        def _heads(t, B, N, H, Dk):
            return t.reshape(B, N, H, Dk).transpose(0, 2, 1, 3)
        B, N, Dm = x.shape
        H = N_HEADS
        Dk = Dm // H
        q = _heads(x @ W_q.T + b_q, B, N, H, Dk)
        k = _heads(x @ W_k.T + b_k, B, N, H, Dk)
        v = _heads(x @ W_v.T + b_v, B, N, H, Dk)
        dec = jnp.exp(-jnp.arange(N, dtype=jnp.float32) / N)[None, None, :, None]
        qf = jax.nn.relu(q) * dec
        kf = jax.nn.relu(k) * dec
        KV = jnp.einsum('bhnd,bhne->bhde', kf, v)
        Ksum = kf.sum(axis=2)
        denom = jnp.einsum('bhnd,bhd->bhn', qf, Ksum) + EPS
        out = jnp.einsum('bhnd,bhde->bhne', qf, KV) / denom[..., None]
        out = out.transpose(0, 2, 1, 3).reshape(B, N, Dm)
        return out @ W_o.T + b_o

    def _L1_ffn_ref(x, Ws, bs, W1, b1, W2, b2):
        import jax, jax.numpy as jnp
        import numpy as np
        B, S, D, E = (2, 512, 128, 8)
        b, s, d = x.shape
        xf = x.reshape(-1, d)
        logits = xf @ Ws.T + bs
        probs = jax.nn.softmax(logits, axis=-1)
        routes = jnp.argmax(probs, axis=-1)
        pmax = jnp.max(probs, axis=-1)
        xf = xf * pmax[:, None]
        perm = jnp.argsort(routes, stable=True)
        xs = xf[perm]
        rs = routes[perm]
        h = jax.nn.relu(jnp.einsum('td,edf->etf', xs, W1) + b1[:, None, :])
        y = jnp.einsum('etf,efd->etd', h, W2) + b2[:, None, :]
        out = y[rs, jnp.arange(rs.shape[0])]
        return out.reshape(b, s, d)

    def _L2_attn_ref(x, ln_g, ln_b, W_in, conv_w, conv_b, W_xp, W_dt, dt_bias, A_log, D_skip, W_out):
        import jax, jax.numpy as jnp
        import numpy as np
        import math
        D_MODEL, D_STATE, D_CONV = (128, 16, 4)
        D_INNER = 2 * D_MODEL
        DT_RANK = math.ceil(D_MODEL / 16)
        B, L = (4, 256)

        def _layernorm(x, g, b, eps=1e-05):
            m = jnp.mean(x, axis=-1, keepdims=True)
            v = jnp.mean(jnp.square(x - m), axis=-1, keepdims=True)
            return (x - m) * jax.lax.rsqrt(v + eps) * g + b

        def _mamba(xn, W_in, conv_w, conv_b, W_xp, W_dt, dt_bias, A_log, D_skip, W_out):
            xz = xn @ W_in
            xi, z = jnp.split(xz, 2, axis=-1)
            xi_t = jnp.transpose(xi, (0, 2, 1))
            xc = jax.lax.conv_general_dilated(xi_t, conv_w, window_strides=(1,), padding=[(D_CONV - 1, 0)], feature_group_count=D_INNER, dimension_numbers=('NCH', 'OIH', 'NCH'))
            xc = jnp.transpose(xc, (0, 2, 1)) + conv_b
            xc = jax.nn.silu(xc)
            x_dbl = xc @ W_xp
            dt_lo, Bm, Cm = jnp.split(x_dbl, [DT_RANK, DT_RANK + D_STATE], axis=-1)
            delta = jax.nn.softplus(dt_lo @ W_dt + dt_bias)
            A = -jnp.exp(A_log)

            def step(h, inp):
                dt_t, B_t, C_t, u_t = inp
                dA = jnp.exp(dt_t[..., None] * A)
                h = h * dA + (dt_t * u_t)[..., None] * B_t[:, None, :]
                y = jnp.einsum('bdn,bn->bd', h, C_t)
                return (h, y)
            h0 = jnp.zeros((xn.shape[0], D_INNER, D_STATE), xn.dtype)
            inputs = (jnp.transpose(delta, (1, 0, 2)), jnp.transpose(Bm, (1, 0, 2)), jnp.transpose(Cm, (1, 0, 2)), jnp.transpose(xc, (1, 0, 2)))
            _, ys = jax.lax.scan(step, h0, inputs)
            y = jnp.transpose(ys, (1, 0, 2)) + xc * D_skip
            y = y * jax.nn.silu(z)
            return y @ W_out
        xn = _layernorm(x, ln_g, ln_b)
        return _mamba(xn, W_in, conv_w, conv_b, W_xp, W_dt, dt_bias, A_log, D_skip, W_out) + x

    def _L2_ffn_ref(tensor, Wr, br, W1, b1, W2, b2):
        import jax, jax.numpy as jnp
        import numpy as np
        D_MODEL = 128
        D_HIDDEN = 512
        NUM_BANKS = 16
        NUM_SELECTED = 2
        logits = jnp.einsum('bsd,de->bse', tensor, Wr) + br
        probs = jax.nn.softmax(logits, axis=-1)
        topv, topi = jax.lax.top_k(probs, NUM_SELECTED)
        gate = jnp.sum(jax.nn.one_hot(topi, NUM_BANKS, dtype=tensor.dtype) * topv[..., None], axis=-2)
        h = jax.nn.relu(jnp.einsum('bsd,edh->bseh', tensor, W1) + b1)
        y = jnp.einsum('bseh,ehm->bsem', h, W2) + b2
        out = jnp.einsum('bse,bsem->bsm', gate, y)
        return out

    def _L3_attn_ref(hidden_states, Wq, bq, Wk, bk, Wv, bv, Wg, bg):
        import jax, jax.numpy as jnp
        import numpy as np
        B, S, H = (2, 256, 128)
        NUM_HEADS = 16
        HEAD_DIM = H // NUM_HEADS
        b, s, h = hidden_states.shape
        g = jax.nn.sigmoid(hidden_states @ Wg + bg)
        Z_I = g
        Z_J = jnp.swapaxes(g, 1, 2)
        res = (1.0 - Z_I) * jnp.maximum(1.0 - Z_I - Z_J, 0.0) + Z_I * jnp.minimum(1.0 - Z_I + Z_J, 1.0)
        idx = jnp.arange(s)
        abs_ij = jnp.abs(idx[:, None] - idx[None, :]).astype(hidden_states.dtype)
        base = jnp.asarray(s - 2, hidden_states.dtype)
        scope = jnp.power(base, 1.0 - g) + 2.0 - abs_ij
        scope = jnp.clip(scope, 1e-32, 1.0)
        penalties = res * scope
        log_pen = jnp.log(jnp.maximum(penalties, 1e-32))

        def split_heads(x):
            return x.reshape(b, s, NUM_HEADS, HEAD_DIM).transpose(0, 2, 1, 3)
        q = split_heads(hidden_states @ Wq + bq)
        k = split_heads(hidden_states @ Wk + bk)
        v = split_heads(hidden_states @ Wv + bv)
        scores = jnp.einsum('bhqd,bhkd->bhqk', q, k) / np.sqrt(HEAD_DIM)
        scores = scores + log_pen[:, None, :, :]
        probs = jax.nn.softmax(scores, axis=-1)
        ctx = jnp.einsum('bhqk,bhkd->bhqd', probs, v)
        ctx = ctx.transpose(0, 2, 1, 3).reshape(b, s, h)
        return ctx

    def _L3_ffn_ref(x, wqkv, q_scale, k_scale, wo, ln_g, ln_b, w1, b1, w2, b2):
        import jax, jax.numpy as jnp
        import numpy as np
        DIM = 128
        DEPTH = 2
        HEADS = 8
        DIM_HEAD = 64
        WINDOW = 64
        INNER = HEADS * DIM_HEAD
        HID = int(DIM * 4 * 2 / 3)
        B, N = (2, 1024)
        QK_SCALE = 8.0

        def shift_token(t):
            t1, t2 = jnp.split(t, 2, axis=-1)
            t2 = jnp.pad(t2, ((0, 0), (1, 0), (0, 0)))[:, :-1]
            return jnp.concatenate([t1, t2], axis=-1)

        def l2norm(t):
            return t / jnp.clip(jnp.linalg.norm(t, axis=-1, keepdims=True), 1e-12)

        def rotate_half(x):
            x1, x2 = jnp.split(x, 2, axis=-1)
            return jnp.concatenate([-x2, x1], axis=-1)

        def rotary_xpos(q, k):
            n = q.shape[-2]
            half_idx = jnp.arange(0, DIM_HEAD, 2, dtype=jnp.float32)
            inv_freq = 1.0 / 10000.0 ** (half_idx / DIM_HEAD)
            t = jnp.arange(n, dtype=jnp.float32)
            freqs = t[:, None] * inv_freq[None, :]
            freqs = jnp.concatenate([freqs, freqs], axis=-1)
            base = (half_idx + 0.4 * DIM_HEAD) / (1.4 * DIM_HEAD)
            power = (t - n // 2) / float(WINDOW // 2)
            scale = base[None, :] ** power[:, None]
            scale = jnp.concatenate([scale, scale], axis=-1)
            cos, sin = (jnp.cos(freqs), jnp.sin(freqs))
            q = q * cos * scale + rotate_half(q) * sin * scale
            k = k * cos / scale + rotate_half(k) * sin / scale
            return (q, k)

        def local_attention(q, k, v):
            b, h, n, d = q.shape
            w = n // WINDOW
            bq = q.reshape(b, h, w, WINDOW, d) * QK_SCALE
            bk = k.reshape(b, h, w, WINDOW, d)
            bv = v.reshape(b, h, w, WINDOW, d)

            def look_around(t):
                p = jnp.pad(t, ((0, 0), (0, 0), (1, 0), (0, 0), (0, 0)))
                return jnp.concatenate([p[:, :, :w], p[:, :, 1:]], axis=3)
            bk, bv = (look_around(bk), look_around(bv))
            bt = jnp.arange(n).reshape(w, WINDOW)
            btp = jnp.pad(bt, ((1, 0), (0, 0)), constant_values=-1)
            btk = jnp.concatenate([btp[:w], btp[1:]], axis=1)
            sim = jnp.einsum('bhwid,bhwjd->bhwij', bq, bk)
            i = bt[:, :, None]
            j = btk[:, None, :]
            mask = (i < j) | (i > j + WINDOW) | (j == -1)
            sim = jnp.where(mask, -jnp.finfo(sim.dtype).max, sim)
            attn = jax.nn.softmax(sim, axis=-1)
            out = jnp.einsum('bhwij,bhwjd->bhwid', attn, bv)
            return out.reshape(b, h, n, d)

        def _layer(x, wqkv, qs, ksc, wo, lg, lb, w1, b1, w2, b2):
            b, n, _ = x.shape
            h = shift_token(x)
            qkv = h @ wqkv
            q, k, v = jnp.split(qkv, 3, axis=-1)
            to_heads = lambda t: t.reshape(b, n, HEADS, DIM_HEAD).transpose(0, 2, 1, 3)
            q, k, v = (to_heads(q), to_heads(k), to_heads(v))
            q = l2norm(q) * qs
            k = l2norm(k) * ksc
            q, k = rotary_xpos(q, k)
            o = local_attention(q, k, v)
            o = o.transpose(0, 2, 1, 3).reshape(b, n, INNER)
            x = x + o @ wo
            h = shift_token(x)
            mu = h.mean(-1, keepdims=True)
            var = h.var(-1, keepdims=True)
            h = (h - mu) / jnp.sqrt(var + 1e-05) * lg + lb
            h = h @ w1 + b1
            a, g = jnp.split(h, 2, axis=-1)
            h = a * jax.nn.gelu(g, approximate=False)
            x = x + h @ w2 + b2
            return x
        for l in range(DEPTH):
            x = _layer(x, wqkv[l], q_scale[l], k_scale[l], wo[l], ln_g[l], ln_b[l], w1[l], b1[l], w2[l], b2[l])
        return x
    x = L0_attn_x
    xn = _layernorm(x, axis=-1)
    s = _L0_attn_ref(xn, L0_attn_mask, L0_attn_Wq, L0_attn_Wk, L0_attn_Wv, L0_attn_Wout)
    g = _silu(_L0_ffn_ref(xn, L0_ffn_Win, L0_ffn_bin_, L0_ffn_W1, L0_ffn_b1, L0_ffn_W2, L0_ffn_b2, L0_ffn_Wout, L0_ffn_bout))
    x = x + s * g
    xn = _layernorm(x, axis=-1)
    s = _L1_attn_ref(xn, L1_attn_W_q, L1_attn_b_q, L1_attn_W_k, L1_attn_b_k, L1_attn_W_v, L1_attn_b_v, L1_attn_W_o, L1_attn_b_o)
    g = _silu(_L1_ffn_ref(xn, L1_ffn_Ws, L1_ffn_bs, L1_ffn_W1, L1_ffn_b1, L1_ffn_W2, L1_ffn_b2))
    x = x + s * g
    xn = _layernorm(x, axis=-1)
    s = _L2_attn_ref(xn, L2_attn_ln_g, L2_attn_ln_b, L2_attn_W_in, L2_attn_conv_w, L2_attn_conv_b, L2_attn_W_xp, L2_attn_W_dt, L2_attn_dt_bias, L2_attn_A_log, L2_attn_D_skip, L2_attn_W_out)
    g = _silu(_L2_ffn_ref(xn, L2_ffn_Wr, L2_ffn_br, L2_ffn_W1, L2_ffn_b1, L2_ffn_W2, L2_ffn_b2))
    x = x + s * g
    xn = _layernorm(x, axis=-1)
    s = _L3_attn_ref(xn, L3_attn_Wq, L3_attn_bq, L3_attn_Wk, L3_attn_bk, L3_attn_Wv, L3_attn_bv, L3_attn_Wg, L3_attn_bg)
    g = _silu(_L3_ffn_ref(xn, L3_ffn_wqkv, L3_ffn_q_scale, L3_ffn_k_scale, L3_ffn_wo, L3_ffn_ln_g, L3_ffn_ln_b, L3_ffn_w1, L3_ffn_b1, L3_ffn_w2, L3_ffn_b2))
    x = x + s * g
    return x

_drawn_inputs = setup_inputs


def setup_inputs(seed=0):
    import zlib

    import numpy as np

    out = dict(_drawn_inputs(seed))
    spreads = {'L1_attn_b_q': (0.0, 0.8),
     'L1_attn_b_k': (0.0, 0.8),
     'L1_attn_b_v': (0.0, 0.8),
     'L1_attn_b_o': (0.0, 0.424),
     'L2_attn_ln_g': (1.0, 0.6),
     'L2_attn_ln_b': (0.0, 0.8),
     'L2_attn_conv_b': (0.0, 0.8),
     'L2_attn_dt_bias': (-4.600165843963623, 0.6),
     'L2_attn_D_skip': (1.0, 0.6),
     'L2_ffn_br': (0.0, 0.8),
     'L2_ffn_b1': (0.0, 0.8),
     'L2_ffn_b2': (0.0, 0.8),
     'L3_attn_bq': (0.0, 2.0),
     'L3_attn_bk': (0.0, 2.0),
     'L3_attn_bv': (0.0, 0.8),
     'L3_ffn_q_scale': (1.0, 0.6),
     'L3_ffn_k_scale': (1.0, 0.6),
     'L3_ffn_ln_g': (1.0, 0.6),
     'L3_ffn_ln_b': (0.0, 2.0),
     'L3_ffn_b1': (0.0, 2.0),
     'L3_ffn_b2': (0.0, 2.0)}
    factors = {'L0_attn_Wq': 2.911,
     'L0_attn_Wk': 2.807,
     'L0_attn_Wv': 2.698,
     'L0_attn_Wout': 2.738,
     'L0_ffn_bin_': 3.719,
     'L1_attn_W_q': 8.0,
     'L1_attn_W_k': 8.0,
     'L1_attn_W_v': 8.0,
     'L1_attn_W_o': 8.0,
     'L1_ffn_Ws': 3.472,
     'L1_ffn_bs': 3.538,
     'L1_ffn_W1': 3.672,
     'L1_ffn_b1': 8.0,
     'L1_ffn_W2': 3.09,
     'L1_ffn_b2': 8.0,
     'L2_attn_W_in': 8.0,
     'L2_attn_conv_w': 8.0,
     'L2_attn_W_xp': 8.0,
     'L2_attn_W_dt': 8.0,
     'L2_attn_A_log': 8.0,
     'L2_attn_W_out': 8.0,
     'L2_ffn_Wr': 6.156,
     'L2_ffn_W1': 8.0,
     'L2_ffn_W2': 8.0,
     'L3_ffn_wqkv': 8.0,
     'L3_ffn_wo': 8.0,
     'L3_ffn_w1': 8.0,
     'L3_ffn_w2': 8.0,
     'L3_attn_Wg': 2.684}
    for name, (base, spread) in spreads.items():
        noise = np.random.default_rng([zlib.crc32(name.encode()), seed]).standard_normal(out[name].shape)
        drawn = base * np.exp(spread * noise) if base else spread * noise
        out[name] = jnp.asarray(drawn.astype(out[name].dtype))
    for name, factor in factors.items():
        out[name] = (out[name] * factor).astype(out[name].dtype)
    return out
```

```python
import concourse.bass as bass
from concourse import mybir
from contextlib import ExitStack
from collections import namedtuple
import numpy as np

F32 = mybir.dt.float32
BF16 = mybir.dt.bfloat16
ALU = mybir.AluOpType
ACT = mybir.ActivationFunctionType
AX = mybir.AxisListType

D = 128
SEQ = 256
NB = 2
T = NB * SEQ
TT = T // 128
NH, DH = 16, 8
NG = 4
E1 = 8
E2, HID2 = 16, 512
DI, NS, DTR, TAPS = 256, 16, 8, 4
DEPTH, LH, LD, WIN = 2, 8, 64, 64
LI = LH * LD
HIDL = int(D * 4 * 2 / 3)
BIG = 3.0e38
PEN_SCALE = 1.0e16
NORM_SCALE = float(2 ** 16)


def record(**fields):
    return namedtuple("Record", list(fields))(**fields)


def columns(parts):
    at, out = 0, {}
    for name, width in parts:
        out[name] = (at, width)
        at += width
    return out, at


CONSTS = [("ident", 128), ("mean", 128), ("ones", 128), ("before", 128), ("sumsel", 128), ("bd8", 128), ("bd64", 128),
          ("unpad", 4 * 128), ("decrow", SEQ), ("dectok", 2), ("rank8", E1), ("rank16", E2),
          ("dist", 2 * SEQ), ("qcos", SEQ), ("qsin", SEQ), ("kcos", SEQ), ("ksin", SEQ), ("rot", 128),
          ("window", 4 * 128), ("eps", 1), ("one", 1), ("kone", 1), ("aeps", 1), ("pow", 1), ("lnpen", 1), ("lnnorm", 1)]
W0 = [("q", 512), ("k", 512), ("v", 128), ("out", 512), ("w1", 1024), ("w2", 1024), ("win", 64), ("w1c", 8),
      ("b1c", 8), ("binc", 8), ("w2c", 8), ("woutm", 128), ("b2m", 1), ("bout", 1)]
W1 = [("q", 128), ("kv", 256), ("o", 128), ("bq", 1), ("bkv", 256), ("bo", 1), ("s", E1), ("bs", E1),
      ("w1", E1 * 128), ("b1", E1), ("w2", E1 * 128), ("b2", 128)]
W2 = [("g", 1), ("b", 1), ("win", 2 * 2 * 128), ("conv", 2 * TAPS), ("cb", 2), ("xp", 2 * (DTR + 2 * NS)), ("dt", DI),
      ("dtb", 2), ("alog", 2 * NS), ("dskip", 2), ("out", 2 * 128), ("r", E2), ("br", E2), ("b1", E2 * 4), ("b2", E2)]
W2F = [("w1", E2 * HID2), ("w2", E2 * 4 * 128)]
W3 = [("q", 512), ("k", 512), ("v", 128), ("bq", 4), ("bk", 4), ("bv", 128), ("gcol", 1), ("grow", 128), ("bg", 1)]
W3F_LAYER = [("qkv", 3 * LI), ("qs", 1), ("ks", 1), ("o", 4 * 128), ("lg", 1), ("lb", 1), ("wa", HIDL), ("wg", HIDL),
       ("ba", 3), ("bgl", 3), ("w2", 3 * 128), ("b2", 1)]
W3F = [(f"{n}{l}", w) for l in range(DEPTH) for n, w in W3F_LAYER]


def view(tensor, parts):
    at, _ = columns(parts)
    return record(**{n: tensor[:, a:a + w] for n, (a, w) in at.items()})


class Link:

    def __init__(self, eng, sem):
        self.eng, self.sem, self.n = eng, sem, 0

    def __call__(self, ins):
        self.n += 1
        ins.then_inc(self.sem, 1)
        self.eng.wait_ge(self.sem, self.n)
        return ins


def semaphores(nc, ctx, names):
    return record(**{n: ctx.enter_context(nc.semaphore(n)) for n in names.split()})


def buffers(nc, ctx, tag, **shapes):
    return record(**{n: ctx.enter_context(nc.sbuf_tensor(f"{tag}_{n}", [128, *s[:-1]] if s[-1] is BF16 else [128, *s],
                                                                  BF16 if s[-1] is BF16 else F32))
                              for n, s in shapes.items()})


def clear(nc, s):
    nums = sorted({x.num for x in s})
    start = nums[0]
    for a, b in zip(nums, nums[1:] + [None]):
        if b != a + 1:
            nc.gpsimd.sem_clear(range(start, a + 1))
            start = b
    nc.all_engine_barrier(sem_only=True)


LN_SEMS = "ln_mean ln_centred ln_square ln_var ln_rstd xn_ready "
GATE_SEMS = "gate_log gate_arg gate_sigmoid "
LINKS = "act_link dve_link pool_link "


def ln_tensor(nc, pe, s, c, src, PB, n=0):
    nc.tensor.matmul(PB[:, 0, :], c.mean, src, start=True, stop=True).then_inc(s.ln_mean, 1)
    pe.wait_ge(s.ln_square, n + 1)
    nc.tensor.matmul(PB[:, 1, :], c.mean, c.lnsq[:], start=True, stop=True).then_inc(s.ln_var, 1)


def ln_scalar(nc, act, s, c, PB, link, n=0):
    act.wait_ge(s.ln_centred, n + 1)
    nc.scalar.activation(c.lnsq[:], c.lnc[:], ACT.Square).then_inc(s.ln_square, 1)
    act.wait_ge(s.ln_var, n + 1)
    link(nc.scalar.activation(c.lnr[:], PB[:, 1, :], ACT.Ln, bias=c.eps))
    nc.scalar.activation(c.lnr[:], c.lnr[:], ACT.Exp, scale=-0.5).then_inc(s.ln_rstd, 1)


def ln_vector(nc, dve, s, c, src, dst, PB, n=0):
    dve.wait_ge(s.ln_mean, n + 1)
    nc.vector.tensor_tensor(c.lnc[:], src, PB[:, 0, :], ALU.subtract).then_inc(s.ln_centred, 1)
    dve.wait_ge(s.ln_centred, n + 1)
    dve.wait_ge(s.ln_rstd, n + 1)
    return nc.vector.tensor_tensor(dst, c.lnc[:], c.lnr[:], ALU.mult)


def gate_scalar(nc, act, s, c, link):
    link(nc.scalar.activation(c.ga[:], c.Y[:], ACT.Abs))
    link(nc.scalar.activation(c.ga[:], c.ga[:], ACT.Exp, scale=-1.0))
    nc.scalar.activation(c.ga[:], c.ga[:], ACT.Ln, bias=c.one).then_inc(s.gate_log, 1)
    act.wait_ge(s.gate_arg, 1)
    nc.scalar.activation(c.gb[:], c.gb[:], ACT.Exp).then_inc(s.gate_sigmoid, 1)


def gate_vector(nc, dve, s, c, link):
    dve.wait_ge(s.gate_log, 1)
    nc.vector.scalar_tensor_tensor(out=c.gb[:], in0=c.Y[:], scalar=0.0, in1=c.ga[:],
                                   op0=ALU.min, op1=ALU.subtract).then_inc(s.gate_arg, 1)
    link(nc.vector.tensor_tensor(c.lnc[:], c.S[:], c.Y[:], ALU.mult))
    dve.wait_ge(s.gate_sigmoid, 1)
    link(nc.vector.tensor_tensor(c.lnc[:], c.lnc[:], c.gb[:], ALU.mult))
    link(nc.vector.tensor_tensor(c.X[:], c.X[:], c.lnc[:], ALU.add))


ATT_SEMS = ("q_ready k_ready v_ready q_copied k_copied v_copied scores_ready max_taken maxT_ready shifted "
            "scoresT_ready exp_done probs_ready ctx_ready ctx_copied den_ready den_taken recip_ready "
            "ctx_scaled att_ready att_done zeroed ")
UNITS = 16
LAG_T, LAG_C, LAG_V, LAG_O, LAG_D = 5, 6, 7, 10, 11


def unit(m):
    return m // 4, m % 4 // 2, m % 2


def att_buffers(nc, ctx, tag, **more):
    return buffers(nc, ctx, tag, QP=[NG, T], KP=[NG, T], VT=[TT, NH, 32], MP=[TT, NG, 4, 32], PT=[2, 2, 2, SEQ],
                   OS=[NG, T], LG=[T], RG=[2, T], Z=[NG, T], **more)


def att_tensor(nc, pe, s, c, w, b, PB, w_out):
    pe.wait_ge(s.xn_ready, 1)
    for g in range(NG):
        nc.tensor.matmul(PB[:, g, :], w.q[:, g * 128:(g + 1) * 128], c.XN[:], start=True, stop=True).then_inc(s.q_ready, 1)
    for g in range(NG):
        nc.tensor.matmul(PB[:, 4 + g, :], w.k[:, g * 128:(g + 1) * 128], c.XN[:], start=True, stop=True).then_inc(s.k_ready, 1)
    pe.wait_ge(s.q_copied, 1)
    for t in range(TT):
        last = nc.tensor.matmul(PB[:, 0, t * 128:(t + 1) * 128], c.XN[:, t * 128:(t + 1) * 128], w.v,
                                start=True, stop=True)
    last.then_inc(s.v_ready, 1)
    pe.wait_ge(s.q_copied, NG)
    pe.wait_ge(s.k_copied, NG)
    pe.wait_ge(s.v_copied, 1)
    for n in range(UNITS + LAG_D - 3):
        if n < UNITS:
            g, sq, jp = unit(n)
            if n:
                pe.wait_ge(s.max_taken, n)
            for j in (2 * jp, 2 * jp + 1):
                for qt in range(2):
                    q0 = sq * SEQ + qt * 128
                    last = nc.tensor.matmul(PB[:, j % 2, qt * SEQ:(qt + 1) * SEQ], b.QP[32 * j:32 * j + 32, g, q0:q0 + 128],
                                            b.KP[32 * j:32 * j + 32, g, sq * SEQ:(sq + 1) * SEQ], start=True, stop=True)
            last.then_inc(s.scores_ready, 1)
        g, r = divmod(n - LAG_T, 4)
        if r == 0 and 0 <= g < NG:
            pe.wait_ge(s.max_taken, 4 * g + 4)
            if g >= 2:
                pe.wait_ge(s.den_taken, g - 1)
            for t in range(TT):
                last = nc.tensor.transpose(PB[:, 6, t * 128:(t + 1) * 128],
                                           b.MP[:, t, g, :, :].rearrange("p j c -> p (j c)"), c.ident)
            last.then_inc(s.maxT_ready, 1)
        m = n - LAG_C
        if 0 <= m < UNITS:
            g, sq, jp = unit(m)
            if m % 4 == 0:
                pe.wait_ge(s.shifted, g + 1)
            if m >= 2:
                pe.wait_ge(s.exp_done, m - 1)
            for kt in range(2):
                for j in (2 * jp, 2 * jp + 1):
                    k0 = sq * SEQ + kt * 128
                    last = nc.tensor.matmul(PB[:, 2 + 2 * (m % 2) + j % 2, kt * SEQ:(kt + 1) * SEQ],
                                            b.KP[32 * j:32 * j + 32, g, k0:k0 + 128],
                                            b.QP[32 * j:32 * j + 32, g, sq * SEQ:(sq + 1) * SEQ], start=True, stop=True)
            last.then_inc(s.scoresT_ready, 1)
        m = n - LAG_V
        if 0 <= m < UNITS:
            g, sq, jp = unit(m)
            pe.wait_ge(s.probs_ready, m + 1)
            if m % 4 == 0 and g:
                pe.wait_ge(s.ctx_copied, g)
            for kt in range(2):
                for j in (2 * jp, 2 * jp + 1):
                    last = nc.tensor.matmul(PB[32 * j:32 * j + 32, 7, sq * SEQ:(sq + 1) * SEQ],
                                            b.VT[:, 2 * sq + kt, 4 * g + j, :], b.PT[:, m % 2, j % 2, kt, :],
                                            start=kt == 0, stop=kt == 1, tile_position=(0, 32 * j))
            last.then_inc(s.ctx_ready, 1)
        g, r = divmod(n - LAG_D, 4)
        if r == 0 and 0 <= g < NG:
            pe.wait_ge(s.ctx_copied, g + 1)
            pe.wait_ge(s.shifted, min(NG, g + 2))
            nc.tensor.matmul(PB[:, 6, :], c.sumsel, b.OS[:, g, :], start=True, stop=True).then_inc(s.den_ready, 1)
    for g in range(NG):
        pe.wait_ge(s.ctx_scaled, g + 1)
        last = nc.tensor.matmul(PB[:, 0, :], w_out[:, g * 128:(g + 1) * 128], b.Z[:, g, :], start=g == 0, stop=g == NG - 1)
    last.then_inc(s.att_ready, 1)


def att_scalar(nc, act, s, c, b, PB, link, bias, masked):
    for g in range(NG):
        act.wait_ge(s.q_ready, g + 1)
        nc.scalar.activation(b.QP[:, g, :], PB[:, g, :], ACT.Identity, scale=float(DH) ** -0.5,
                             bias=bias[:, g:g + 1] if masked else 0.0).then_inc(s.q_copied, 1)
    for n in range(LAG_C, UNITS + LAG_D - 3):
        m = n - LAG_C
        if m < UNITS:
            act.wait_ge(s.scoresT_ready, m + 1)
            if m >= 2:
                act.wait_ge(s.ctx_ready, m - 1)
            k = 2 + 2 * (m % 2)
            nc.scalar.activation(b.PT[:, m % 2].rearrange("p j k q -> p (j k q)"),
                                 PB[:, k:k + 2, :].rearrange("p j q -> p (j q)"), ACT.Exp).then_inc(s.exp_done, 1)
        g, r = divmod(n - LAG_O, 4)
        if r == 0 and 0 <= g < NG:
            act.wait_ge(s.ctx_ready, 4 * g + 4)
            nc.scalar.activation(b.OS[:, g, :], PB[:, 7, :], ACT.Copy).then_inc(s.ctx_copied, 1)
        g, r = divmod(n - LAG_D, 4)
        if r == 0 and 0 <= g < NG:
            act.wait_ge(s.den_ready, g + 1)
            nc.scalar.activation(b.LG[:], PB[:, 6, :], ACT.Ln).then_inc(s.den_taken, 1)
            act.wait_ge(s.den_taken, g + 1)
            if g >= 2:
                act.wait_ge(s.ctx_scaled, g - 1)
            nc.scalar.activation(b.RG[:, g % 2, :], b.LG[:], ACT.Exp, scale=-1.0).then_inc(s.recip_ready, 1)
            act.wait_ge(s.recip_ready, g + 1)


def att_vector(nc, dve, s, c, w, b, PB, link, masked):
    for g in range(NG):
        dve.wait_ge(s.k_ready, g + 1)
        kb = w.bk[:, g:g + 1] if masked else c.kone
        nc.vector.tensor_scalar(b.KP[:, g, :], PB[:, 4 + g, :], kb, None, ALU.add).then_inc(s.k_copied, 1)
    dve.wait_ge(s.zeroed, 1)
    dve.wait_ge(s.v_ready, 1)
    vt = b.VT[:].rearrange("p t h c -> p (t h) c")[:, :, 0:DH]
    vp = PB[:, 0, :].rearrange("p (a c) -> p a c", c=DH)
    if masked:
        for t in range(TT):
            last = nc.vector.tensor_tensor(b.VT[:, t, :, 0:DH], PB[:, 0, t * 128:(t + 1) * 128].rearrange("p (h c) -> p h c", c=DH),
                                           w.bv.rearrange("p (h c) -> p h c", c=DH), ALU.add)
        last.then_inc(s.v_copied, 1)
    else:
        nc.vector.tensor_copy(vt, vp).then_inc(s.v_copied, 1)
    if masked:
        dve.wait_ge(s.logpen_ready, 1)
    for n in range(UNITS + 2):
        if n < UNITS:
            g, sq, jp = unit(n)
            dve.wait_ge(s.scores_ready, n + 1)
            out = b.MP[:, 2 * sq:2 * sq + 2, g, 2 * jp:2 * jp + 2, DH].rearrange("p t j -> p j t")
            src = PB[:, 0:2, :].rearrange("p j (t k) -> p j t k", k=SEQ)
            if masked:
                for j in range(2):
                    last = nc.vector.tensor_tensor(b.TS[:, j, :], PB[:, j, :],
                                                   b.LP[:, 2 * sq:2 * sq + 2, :].rearrange("p t k -> p (t k)"), ALU.add)
                link(last)
                src = b.TS[:].rearrange("p j (t k) -> p j t k", k=SEQ)
            nc.vector.tensor_reduce(out, src, AX.X, ALU.max).then_inc(s.max_taken, 1)
            dve.wait_ge(s.max_taken, n + 1)
        g, r = divmod(n - LAG_T, 4)
        if r == 0 and 0 <= g < NG:
            dve.wait_ge(s.maxT_ready, g + 1)
            nc.vector.tensor_tensor(b.QP[:, g, :], b.QP[:, g, :], PB[:, 6, :], ALU.subtract).then_inc(s.shifted, 1)


def att_gpsimd(nc, pool, s, c, b, link, masked):
    link(nc.gpsimd.memset(b.VT[:], 0.0))
    link(nc.gpsimd.memset(b.MP[:], 0.0))
    nc.gpsimd.memset(b.VT[:, :, :, DH:DH + 1].rearrange("p t h c -> p (t h) c"), 1.0).then_inc(s.zeroed, 1)
    for n in range(LAG_C, UNITS + LAG_D - 3):
        m = n - LAG_C
        if masked and m < UNITS:
            g, sq, jp = unit(m)
            pool.wait_ge(s.exp_done, m + 1)
            pt = b.PT[:, m % 2].rearrange("p j k q -> p j (k q)")
            pen = b.PEN[:, 2 * sq:2 * sq + 2, :].rearrange("p k q -> p (k q)")
            if m == 0:
                pool.wait_ge(s.penT_copied, 1)
            for j in range(2):
                last = nc.gpsimd.tensor_tensor(pt[:, j, :], pt[:, j, :], pen, ALU.mult)
            last.then_inc(s.probs_masked, 1)
        g, r = divmod(n - LAG_D, 4)
        if r == 0 and 0 <= g < NG:
            pool.wait_ge(s.recip_ready, g + 1)
            nc.gpsimd.tensor_tensor(b.Z[:, g, :], b.OS[:, g, :], b.RG[:, g % 2, :], ALU.mult).then_inc(s.ctx_scaled, 1)


L0_SEMS = LN_SEMS + ATT_SEMS + GATE_SEMS + LINKS + "hid_ready hid_done ffn_ready y_ready "


def layer0(nc, c, w, PB):
    with ExitStack() as ctx:
        s = semaphores(nc, ctx, L0_SEMS)
        s = s._replace(probs_ready=s.exp_done)
        b = att_buffers(nc, ctx, "l0", H=[2, T])
        with nc.Block() as block:
            @block.tensor
            def _(pe):
                ln_tensor(nc, pe, s, c, c.X[:], PB)
                att_tensor(nc, pe, s, c, w, b, PB, w.out)
                for i in range(9):
                    if i < 8:
                        if i >= 2:
                            pe.wait_ge(s.hid_done, i - 1)
                        nc.tensor.matmul(PB[:, 1 + i % 2, :], w.w1[:, i * 128:(i + 1) * 128], c.XN[:],
                                         start=True, stop=True).then_inc(s.hid_ready, 1)
                    if i:
                        pe.wait_ge(s.hid_done, i)
                        last = nc.tensor.matmul(PB[:, 3, :], w.w2[:, (i - 1) * 128:i * 128], b.H[:, (i - 1) % 2, :],
                                                start=i == 1, stop=i == 8)
                        if i < 8:
                            last.then_inc(s.ffn_ready, 1)
                last.then_inc(s.ffn_ready, 1)

            @block.scalar
            def _(act):
                link = Link(act, s.act_link)
                ln_scalar(nc, act, s, c, PB, link)
                att_scalar(nc, act, s, c, b, PB, link, None, False)
                for i in range(8):
                    act.wait_ge(s.hid_ready, i + 1)
                    if i >= 2:
                        act.wait_ge(s.ffn_ready, i - 1)
                    nc.scalar.activation(b.H[:, i % 2, :], PB[:, 1 + i % 2, :], ACT.Relu, bias=w.b1c[:, i:i + 1]).then_inc(s.hid_done, 1)
                act.wait_ge(s.y_ready, 1)
                gate_scalar(nc, act, s, c, link)

            @block.vector
            def _(dve):
                link = Link(dve, s.dve_link)
                ln_vector(nc, dve, s, c, c.X[:], c.XN[:], PB).then_inc(s.xn_ready, 1)
                att_vector(nc, dve, s, c, w, b, PB, link, False)
                dve.wait_ge(s.att_ready, 1)
                dve.wait_ge(s.xn_ready, 1)
                link(nc.vector.tensor_tensor(c.S[:], PB[:, 0, :], c.XN[:], ALU.add))
                dve.wait_ge(s.ffn_ready, 8)
                nc.vector.tensor_scalar(c.Y[:], PB[:, 3, :], w.bout, None, ALU.add).then_inc(s.y_ready, 1)
                dve.wait_ge(s.y_ready, 1)
                gate_vector(nc, dve, s, c, link)

            @block.gpsimd
            def _(pool):
                att_gpsimd(nc, pool, s, c, b, Link(pool, s.pool_link), False)
        clear(nc, s)


L1_SEMS = (LN_SEMS + LINKS + "q_ready qf_relu qf_ready kv_ready kv_biased kf_ready kvsum_ready "
           "kvsum_masked num_ready den_ready recip_ready ctx_scaled att_ready att_done ones_set "
           "logits_ready logits_shifted route_exp pmax_ready route_ready pmaxT_ready routeT_ready xp_ready "
           "routeT_copied keep_ready hid_ready hid_done ffn_ready y_ready count_ready count_taken yT_ready saved ")


def layer1(nc, c, w, r, it, x_mid, s_mid, PB):
    with ExitStack() as ctx:
        s = semaphores(nc, ctx, L1_SEMS)
        b = buffers(nc, ctx, "l1", QF=[T], KV=[TT, 257], KM=[NB, 128], KS=[NB, 128], RG=[T], LG=[T], CT=[T],
                    LO=[TT, E1], EX=[TT, E1], OH=[TT, E1], WK=[TT, E1], M1=[TT], SM=[TT], PX=[TT, 128],
                    XP=[T], OT=[T], PEN=[T, BF16], H=[2, T])
        with nc.Block() as block:
            @block.tensor
            def _(pe):
                ln_tensor(nc, pe, s, c, c.X[:], PB)
                pe.wait_ge(s.xn_ready, 1)
                for t in range(TT):
                    last = nc.tensor.matmul(PB[:, 0, t * E1:(t + 1) * E1], c.XN[:, t * 128:(t + 1) * 128], w.s,
                                            start=True, stop=True)
                last.then_inc(s.logits_ready, 1)
                for t in range(TT):
                    last = nc.tensor.matmul(PB[:, 2 + t // 2, t % 2 * 256:t % 2 * 256 + 256],
                                            c.XN[:, t * 128:(t + 1) * 128], w.kv, start=True, stop=True)
                last.then_inc(s.kv_ready, 1)
                nc.tensor.matmul(PB[:, 1, :], w.q, c.XN[:], start=True, stop=True).then_inc(s.q_ready, 1)
                pe.wait_ge(s.kf_ready, 1)
                for sq in range(NB):
                    for t in range(2):
                        last = nc.tensor.matmul(PB[:, 4 + sq, 0:129], b.KV[:, 2 * sq + t, 0:128], b.KV[:, 2 * sq + t, 128:257],
                                                start=t == 0, stop=t == 1)
                last.then_inc(s.kvsum_ready, 1)
                pe.wait_ge(s.pmax_ready, 1)
                pe.wait_ge(s.route_ready, 1)
                for t in range(TT):
                    last = nc.tensor.transpose(PB[:, 0, t * 128:(t + 1) * 128], b.PX[:, t, :], c.ident)
                last.then_inc(s.pmaxT_ready, 1)
                for t in range(TT):
                    last = nc.tensor.transpose(PB[0:E1, 2, t * 128:(t + 1) * 128], b.OH[:, t, :], c.ident)
                last.then_inc(s.routeT_ready, 1)
                pe.wait_ge(s.qf_relu, 1)
                for t in range(TT):
                    o = PB[:, 1, t * E1:(t + 1) * E1]
                    nc.tensor.matmul(o, c.before, b.OH[:, t, :], start=True, stop=t == 0)
                    for u in range(t):
                        nc.tensor.matmul(o, c.ones, b.OH[:, u, :], start=False, stop=u == t - 1)
                for t in range(TT):
                    last = nc.tensor.matmul(PB[:, 1, TT * E1:TT * E1 + E1], c.ones, b.OH[:, t, :], start=t == 0, stop=t == TT - 1)
                last.then_inc(s.count_ready, 1)
                pe.wait_ge(s.kvsum_masked, 1)
                pe.wait_ge(s.qf_ready, 1)
                for sq in range(NB):
                    last = nc.tensor.matmul(PB[:, 6, sq * SEQ:(sq + 1) * SEQ], b.KM[:, sq, :], b.QF[:, sq * SEQ:(sq + 1) * SEQ],
                                            start=True, stop=True)
                last.then_inc(s.num_ready, 1)
                for sq in range(NB):
                    last = nc.tensor.matmul(PB[:, 7, sq * SEQ:(sq + 1) * SEQ], b.KS[:, sq, :], b.QF[:, sq * SEQ:(sq + 1) * SEQ],
                                            start=True, stop=True)
                last.then_inc(s.den_ready, 1)
                pe.wait_ge(s.xp_ready, 1)
                pe.wait_ge(s.keep_ready, 1)
                for e in range(E1 + 1):
                    if e < E1:
                        if e >= 2:
                            pe.wait_ge(s.hid_done, e - 1)
                        nc.tensor.matmul(PB[:, 4 + e % 2, :], w.w1[:, e * 128:(e + 1) * 128], b.XP[:], start=True, stop=False)
                        nc.tensor.matmul(PB[:, 4 + e % 2, :], c.identb[0:E1, e:e + 1].broadcast_to([E1, 128]), b.PEN[0:E1, :],
                                         start=False, stop=True).then_inc(s.hid_ready, 1)
                    if e:
                        pe.wait_ge(s.hid_done, e)
                        nc.tensor.matmul(PB[:, 3, :], w.w2[:, (e - 1) * 128:e * 128], b.H[:, (e - 1) % 2, :],
                                         start=e == 1, stop=False).then_inc(s.ffn_ready, 1)
                nc.tensor.matmul(PB[:, 3, :], w.b2[0:E1, :], b.OT[0:E1, :], start=False, stop=True).then_inc(s.ffn_ready, 1)
                pe.wait_ge(s.ctx_scaled, 1)
                pe.wait_ge(s.count_taken, 1)
                nc.tensor.matmul(PB[:, 1, :], w.o, b.CT[:], start=True, stop=True).then_inc(s.att_ready, 1)
                pe.wait_ge(s.y_ready, 1)
                for t in range(TT):
                    last = nc.tensor.transpose(PB[:, 0, t * 128:(t + 1) * 128], c.Y[:, t * 128:(t + 1) * 128], c.ident)
                last.then_inc(s.yT_ready, 1)

            @block.scalar
            def _(act):
                link = Link(act, s.act_link)
                ln_scalar(nc, act, s, c, PB, link)
                act.wait_ge(s.logits_shifted, 1)
                nc.scalar.activation(b.EX[:], b.LO[:], ACT.Exp).then_inc(s.route_exp, 1)
                act.wait_ge(s.q_ready, 1)
                nc.scalar.activation(b.QF[:], PB[:, 1, :], ACT.Relu, bias=w.bq).then_inc(s.qf_relu, 1)
                act.wait_ge(s.routeT_ready, 1)
                nc.scalar.activation(b.OT[0:E1, :], PB[0:E1, 2, :], ACT.Copy).then_inc(s.routeT_copied, 1)
                act.wait_ge(s.den_ready, 1)
                link(nc.scalar.activation(b.LG[:], PB[:, 7, :], ACT.Ln, bias=c.aeps))
                nc.scalar.activation(b.RG[:], b.LG[:], ACT.Exp, scale=-1.0).then_inc(s.recip_ready, 1)
                for e in range(E1):
                    act.wait_ge(s.hid_ready, e + 1)
                    if e >= 2:
                        act.wait_ge(s.ffn_ready, e - 1)
                    nc.scalar.activation(b.H[:, e % 2, :], PB[:, 4 + e % 2, :], ACT.Relu, bias=w.b1[:, e:e + 1]).then_inc(s.hid_done, 1)

            @block.vector
            def _(dve):
                link = Link(dve, s.dve_link)
                ln_vector(nc, dve, s, c, c.X[:], c.XN[:], PB).then_inc(s.xn_ready, 1)
                dve.wait_ge(s.logits_ready, 1)
                link(nc.vector.tensor_tensor(b.LO[:], PB[:, 0, 0:TT * E1].rearrange("p (t e) -> p t e", e=E1),
                                             w.bs.unsqueeze(1).broadcast_to([128, TT, E1]), ALU.add))
                link(nc.vector.tensor_reduce(b.M1[:], b.LO[:], AX.X, ALU.max))
                nc.vector.tensor_tensor(b.LO[:], b.LO[:], b.M1[:].unsqueeze(2).broadcast_to([128, TT, E1]),
                                        ALU.subtract).then_inc(s.logits_shifted, 1)
                dve.wait_ge(s.logits_shifted, 1)
                link(nc.vector.tensor_scalar(b.OH[:], b.LO[:], 0.0, None, ALU.is_equal))
                link(nc.vector.tensor_tensor(b.WK[:], b.OH[:], c.rank8.unsqueeze(1).broadcast_to([128, TT, E1]), ALU.mult))
                link(nc.vector.tensor_reduce(b.M1[:], b.WK[:], AX.X, ALU.max))
                nc.vector.tensor_tensor(b.OH[:], b.WK[:], b.M1[:].unsqueeze(2).broadcast_to([128, TT, E1]),
                                        ALU.is_equal).then_inc(s.route_ready, 1)
                dve.wait_ge(s.kv_ready, 1)
                dve.wait_ge(s.ones_set, 1)
                link(nc.vector.tensor_tensor(b.KV[:, :, 0:256], PB[:, 2:4, :].rearrange("p a (t k) -> p (a t) k", k=256),
                                             w.bkv.unsqueeze(1).broadcast_to([128, TT, 256]), ALU.add))
                for par in range(2):
                    last = nc.vector.tensor_scalar(b.KV[:, par:TT:2, 0:128], b.KV[:, par:TT:2, 0:128], 0.0,
                                                   c.dectok[:, par:par + 1], ALU.max, ALU.mult)
                last.then_inc(s.kf_ready, 1)
                dve.wait_ge(s.route_exp, 1)
                link(nc.vector.tensor_reduce(b.SM[:], b.EX[:], AX.X, ALU.add))
                link(nc.vector.reciprocal(b.SM[:], b.SM[:]))
                nc.vector.tensor_copy(b.PX[:], b.SM[:].unsqueeze(2).broadcast_to([128, TT, 128])).then_inc(s.pmax_ready, 1)
                dve.wait_ge(s.kvsum_ready, 1)
                for sq in range(NB):
                    nc.vector.tensor_tensor(b.KM[:, sq, :], PB[:, 4 + sq, 0:128], c.bd8, ALU.mult)
                    last = nc.vector.tensor_scalar(b.KS[:, sq, :], c.bd8, PB[:, 4 + sq, 128:129], None, ALU.mult)
                last.then_inc(s.kvsum_masked, 1)
                dve.wait_ge(s.pmaxT_ready, 1)
                nc.vector.tensor_tensor(b.XP[:], c.XN[:], PB[:, 0, :], ALU.mult).then_inc(s.xp_ready, 1)
                dve.wait_ge(s.routeT_copied, 1)
                nc.vector.tensor_scalar(b.PEN[0:E1, :], b.OT[0:E1, :], -1.0, BIG, ALU.add, ALU.mult).then_inc(s.keep_ready, 1)
                dve.wait_ge(s.count_ready, 1)
                link(nc.vector.tensor_tensor(b.WK[:], PB[:, 1, 0:TT * E1].rearrange("p (t e) -> p t e", e=E1),
                                             r.base[:].unsqueeze(1).broadcast_to([128, TT, E1]), ALU.add))
                nc.vector.tensor_tensor(r.base[:], r.base[:], PB[:, 1, TT * E1:TT * E1 + E1], ALU.add).then_inc(s.count_taken, 1)
                link(nc.vector.tensor_tensor(b.WK[:], b.WK[:], b.OH[:], ALU.mult))
                nc.vector.tensor_reduce(r.rank[:, bass.ts(it, TT)], b.WK[:], AX.X, ALU.add)
                nc.vector.tensor_copy(r.route[:, bass.ts(it, TT), :], b.OH[:])
                dve.wait_ge(s.recip_ready, 1)
                dve.wait_ge(s.num_ready, 1)
                nc.vector.tensor_tensor(b.CT[:], PB[:, 6, :], b.RG[:], ALU.mult).then_inc(s.ctx_scaled, 1)
                dve.wait_ge(s.att_ready, 1)
                dve.wait_ge(s.ffn_ready, E1 + 1)
                nc.vector.tensor_copy(c.Y[:], PB[:, 3, :]).then_inc(s.y_ready, 1)
                nc.vector.tensor_scalar(c.S[:], PB[:, 1, :], w.bo, None, ALU.add).then_inc(s.att_done, 1)
                dve.wait_ge(s.yT_ready, 1)
                nc.vector.tensor_copy(r.y[:, bass.ts(it, TT), :], PB[:, 0, :].rearrange("p (t d) -> p t d", d=D))

            @block.sync
            def _(sp):
                sp.dma_start(x_mid[bass.ts(it, 128), :], c.X[:]).then_inc(s.saved, 16)
                sp.wait_ge(s.att_done, 1)
                sp.dma_start(s_mid[bass.ts(it, 128), :], c.S[:]).then_inc(s.saved, 16)
                sp.wait_ge(s.saved, 32)

            @block.gpsimd
            def _(pool):
                nc.gpsimd.memset(b.KV[:, :, 256:257].rearrange("p t o -> p (t o)"), 1.0).then_inc(s.ones_set, 1)
                pool.wait_ge(s.qf_relu, 1)
                nc.gpsimd.tensor_tensor(b.QF[:].rearrange("p (s n) -> p s n", n=SEQ), b.QF[:].rearrange("p (s n) -> p s n", n=SEQ),
                                        c.decrow.unsqueeze(1).broadcast_to([128, NB, SEQ]), ALU.mult).then_inc(s.qf_ready, 1)
        clear(nc, s)


def place_tokens(nc, r, tiles, y_mid):
    with ExitStack() as ctx:
        s = semaphores(nc, ctx, "dve_link places_ready scattered")
        off = ctx.enter_context(nc.sbuf_tensor("off", [128, E1], F32))
        pos = ctx.enter_context(nc.sbuf_tensor("pos", [128, tiles], F32))
        idx = ctx.enter_context(nc.sbuf_tensor("idx", [128, tiles], mybir.dt.int32))
        with nc.Block() as block:
            @block.vector
            def _(dve):
                link = Link(dve, s.dve_link)
                link(nc.vector.memset(off[:, 0:1], 0.0))
                for e in range(1, E1):
                    link(nc.vector.tensor_tensor(off[:, e:e + 1], off[:, e - 1:e], r.base[:, e - 1:e], ALU.add))
                link(nc.vector.tensor_tensor(r.route[:], r.route[:], off[:].unsqueeze(1).broadcast_to([128, tiles, E1]), ALU.mult))
                link(nc.vector.tensor_reduce(pos[:], r.route[:], AX.X, ALU.add))
                nc.vector.tensor_tensor(idx[:], pos[:], r.rank[:], ALU.add).then_inc(s.places_ready, 1)

            @block.gpsimd
            def _(pool):
                pool.wait_ge(s.places_ready, 1)
                for t in range(tiles):
                    pool.indirect_dma_start(out=y_mid, out_offset=bass.IndirectOffsetOnAxis(ap=idx[:, t:t + 1], axis=0),
                                            in_=r.y[:, t, :], in_offset=None).then_inc(s.scattered, 16)
                pool.wait_ge(s.scattered, 16 * tiles)
        clear(nc, s)


L2_SEMS = (LN_SEMS + GATE_SEMS + LINKS + "ln_reused xm_ready xz_ready xi_copied conv_done silu_x silu_z xd_ready dtl_copied "
           "bc_copied dt_ready dt_raw dt_exp dt_u dt_log delta_ready decay_ready b_ready c_ready drive_ready "
           "c_copied state_ready part_ready y_summed y_gated mamba_ready pads_set "
           "logits_ready logits_shifted route_exp gates_ready gate_spread gateT_ready w2_loaded0 w2_loaded1 hid_ready "
           "hid_even hid_odd ffn_ready bank_done weighted acc_done ")
HID_BANKS = (2, 3, 7)
HTILES = HID2 // 128


def layer2(nc, c, w, wf, PB):
    with ExitStack() as ctx:
        s = semaphores(nc, ctx, L2_SEMS)
        b = buffers(nc, ctx, "l2", XM=[T], XI=[2, NB, TAPS - 1 + SEQ], XC=[2, T], ZS=[2, T], DL=[2, T], DU=[2, T],
                    EE=[2, T], UU=[2, T], DTL=[T], BC=[T], CN=[2, T], DA=[2, 2, T], DB=[2, 2, T], ST=[2, 2, T],
                    CH=[2, T], YA=[2, T], H=[4, T], YB=[2, T], GS=[2, TT, 128], WB=[2, 2 * HID2],
                    LO=[TT, E2], EX=[TT, E2], OA=[TT, E2], OB=[TT, E2], WK=[TT, E2], M1=[TT], SM=[TT])
        loaded = (s.w2_loaded0, s.w2_loaded1)

        def hid_wait(eng, k):
            if k % 2:
                eng.wait_ge(s.hid_odd, (k + 1) // 2)
            else:
                eng.wait_ge(s.hid_even, k // 2 + 1)

        with nc.Block() as block:
            @block.sync
            def _(sp):
                for e in range(E2):
                    if e >= 2:
                        sp.wait_ge(s.ffn_ready, HTILES * (e - 1))
                    sp.dma_start(b.WB[:, e % 2, :], wf[e, :, :]).then_inc(loaded[e % 2], 16)

            @block.tensor
            def _(pe):
                ln_tensor(nc, pe, s, c, c.X[:], PB)
                pe.wait_ge(s.xn_ready, 1)
                ln_tensor(nc, pe, s, c, c.XN[:], PB, 1)
                for t in range(TT):
                    last = nc.tensor.matmul(PB[:, 4, t * E2:(t + 1) * E2], c.XN[:, t * 128:(t + 1) * 128], w.r,
                                            start=True, stop=True)
                last.then_inc(s.logits_ready, 1)
                pe.wait_ge(s.xm_ready, 1)
                for k in range(4):
                    nc.tensor.matmul(PB[:, k, :], w.win[:, k * 128:(k + 1) * 128], b.XM[:], start=True, stop=True).then_inc(s.xz_ready, 1)
                pe.wait_ge(s.silu_x, 2)
                for k in range(2):
                    last = nc.tensor.matmul(PB[0:DTR, 5, :], w.xp[:, k * 40:k * 40 + DTR], b.XC[:, k, :], start=k == 0, stop=k == 1)
                for k in range(2):
                    last = nc.tensor.matmul(PB[0:32, 6, :], w.xp[:, k * 40 + DTR:k * 40 + 40], b.XC[:, k, :], start=k == 0, stop=k == 1)
                last.then_inc(s.xd_ready, 1)
                pe.wait_ge(s.dtl_copied, 1)
                pe.wait_ge(s.xi_copied, 1)
                pe.wait_ge(s.silu_z, 2)
                for k in range(2):
                    last = nc.tensor.matmul(PB[:, k, :], w.dt[0:DTR, k * 128:(k + 1) * 128], b.DTL[0:DTR, :], start=True, stop=True)
                last.then_inc(s.dt_ready, 1)
                pe.wait_ge(s.bc_copied, 1)
                pe.wait_ge(s.dt_raw, 1)
                pe.wait_ge(s.gates_ready, 1)
                for n in range(NS):
                    if n:
                        pe.wait_ge(s.drive_ready, n)
                    nc.tensor.matmul(PB[:, 0, :], c.ident[0:32, n:n + 1].broadcast_to([32, 128]),
                                     b.BC[0:32, :], start=True, stop=True).then_inc(s.b_ready, 1)
                    if n:
                        pe.wait_ge(s.c_copied, n)
                    nc.tensor.matmul(PB[:, 1, :], c.ident[0:32, NS + n:NS + n + 1].broadcast_to([32, 128]),
                                     b.BC[0:32, :], start=True, stop=True).then_inc(s.c_ready, 1)
                    for i in range(HTILES + 2):
                        if i < HTILES:
                            k = HTILES * n + i
                            if i == 0:
                                pe.wait_ge(loaded[n % 2], 16 * (n // 2 + 1))
                            if k >= 3:
                                hid_wait(pe, k - 3)
                            nc.tensor.matmul(PB[:, HID_BANKS[k % 3], :], b.WB[:, n % 2, i * 128:(i + 1) * 128], c.XN[:],
                                             start=True, stop=True).then_inc(s.hid_ready, 1)
                        if i >= 2:
                            k = HTILES * n + i - 2
                            hid_wait(pe, k)
                            if i == 2 and n >= 2:
                                pe.wait_ge(s.bank_done, n - 1)
                            nc.tensor.matmul(PB[:, 4 + n % 2, :], b.WB[:, n % 2, HID2 + (i - 2) * 128:HID2 + (i - 1) * 128],
                                             b.H[:, k % 4, :], start=i == 2, stop=i == HTILES + 1).then_inc(s.ffn_ready, 1)
                    pe.wait_ge(s.gate_spread, n + 1)
                    if n:
                        pe.wait_ge(s.weighted, n)
                    for t in range(TT):
                        last = nc.tensor.transpose(PB[:, 6, t * 128:(t + 1) * 128], b.GS[:, n % 2, t, :], c.ident)
                    last.then_inc(s.gateT_ready, 1)
                pe.wait_ge(s.y_gated, 1)
                for k in range(2):
                    last = nc.tensor.matmul(PB[:, 0, :], w.out[:, k * 128:(k + 1) * 128], b.EE[:, k, :], start=k == 0, stop=k == 1)
                last.then_inc(s.mamba_ready, 1)

            @block.scalar
            def _(act):
                link = Link(act, s.act_link)
                ln_scalar(nc, act, s, c, PB, link)
                ln_scalar(nc, act, s, c, PB, link, 1)
                act.wait_ge(s.logits_shifted, 1)
                nc.scalar.activation(b.EX[:], b.LO[:], ACT.Exp).then_inc(s.route_exp, 1)
                for k in range(2):
                    act.wait_ge(s.xz_ready, 3 + k)
                    nc.scalar.activation(b.ZS[:, k, :], PB[:, 2 + k, :], ACT.Silu).then_inc(s.silu_z, 1)
                for k in range(2):
                    act.wait_ge(s.conv_done, k + 1)
                    nc.scalar.activation(b.XC[:, k, :], b.XC[:, k, :], ACT.Silu).then_inc(s.silu_x, 1)
                act.wait_ge(s.xd_ready, 1)
                nc.scalar.activation(b.DTL[0:DTR, :], PB[0:DTR, 5, :], ACT.Copy).then_inc(s.dtl_copied, 1)
                nc.scalar.activation(b.BC[0:32, :], PB[0:32, 6, :], ACT.Copy).then_inc(s.bc_copied, 1)
                act.wait_ge(s.dt_raw, 1)
                link(nc.scalar.activation(b.EE[:], b.DL[:], ACT.Abs))
                nc.scalar.activation(b.EE[:], b.EE[:], ACT.Exp, scale=-1.0).then_inc(s.dt_exp, 1)
                act.wait_ge(s.dt_u, 1)
                nc.scalar.activation(b.DU[:], b.UU[:], ACT.Ln).then_inc(s.dt_log, 1)
                act.wait_ge(s.delta_ready, 1)
                act.wait_ge(s.pads_set, 1)

                def bank_out(e):
                    act.wait_ge(s.ffn_ready, HTILES * (e + 1))
                    if e >= 2:
                        act.wait_ge(s.acc_done, e - 1)
                    nc.scalar.activation(b.YB[:, e % 2, :], PB[:, 4 + e % 2, :], ACT.Identity, bias=w.b2[:, e:e + 1]).then_inc(s.bank_done, 1)

                def hidden(k):
                    act.wait_ge(s.hid_ready, k + 1)
                    if k >= 4:
                        act.wait_ge(s.ffn_ready, k - 3)
                    nc.scalar.activation(b.H[:, k % 4, :], PB[:, HID_BANKS[k % 3], :], ACT.Relu, bias=w.b1[:, k:k + 1]).then_inc(s.hid_even, 1)

                for n in range(NS):
                    if n >= 2:
                        act.wait_ge(s.state_ready, n - 1)
                    for k in range(2):
                        last = nc.scalar.activation(b.DA[:, n % 2, k, :].rearrange("p (s t) -> p s t", t=SEQ)[:, :, 1:SEQ],
                                                    b.DL[:, k, :].rearrange("p (s t) -> p s t", t=SEQ)[:, :, 1:SEQ],
                                                    ACT.Exp, scale=c.aneg[:, k * NS + n:k * NS + n + 1])
                    last.then_inc(s.decay_ready, 1)
                    act.wait_ge(s.c_ready, n + 1)
                    if n >= 2:
                        act.wait_ge(s.part_ready, n - 1)
                    nc.scalar.activation(b.CN[:, n % 2, :], PB[:, 1, :], ACT.Copy).then_inc(s.c_copied, 1)
                    hidden(HTILES * n)
                    hidden(HTILES * n + 2)
                    if n:
                        bank_out(n - 1)
                bank_out(E2 - 1)
                act.wait_ge(s.acc_done, E2)
                gate_scalar(nc, act, s, c, link)

            @block.vector
            def _(dve):
                link = Link(dve, s.dve_link)
                ln_vector(nc, dve, s, c, c.X[:], c.XN[:], PB).then_inc(s.xn_ready, 1)
                dve.wait_ge(s.xn_ready, 1)
                link(ln_vector(nc, dve, s, c, c.XN[:], b.XM[:], PB, 1))
                nc.vector.tensor_scalar(b.XM[:], b.XM[:], w.g, w.b, ALU.mult, ALU.add).then_inc(s.xm_ready, 1)
                dve.wait_ge(s.logits_ready, 1)
                spread = lambda x, k: x.unsqueeze(2).broadcast_to([128, TT, k])
                rank = c.rank16.unsqueeze(1).broadcast_to([128, TT, E2])
                link(nc.vector.tensor_tensor(b.LO[:], PB[:, 4, 0:TT * E2].rearrange("p (t e) -> p t e", e=E2),
                                             w.br.unsqueeze(1).broadcast_to([128, TT, E2]), ALU.add))
                link(nc.vector.tensor_reduce(b.M1[:], b.LO[:], AX.X, ALU.max))
                nc.vector.tensor_tensor(b.LO[:], b.LO[:], spread(b.M1[:], E2), ALU.subtract).then_inc(s.logits_shifted, 1)
                dve.wait_ge(s.logits_shifted, 1)
                dve.wait_ge(s.pads_set, 1)
                dve.wait_ge(s.xz_ready, 2)
                for k in range(2):
                    last = nc.vector.tensor_copy(b.XI[:, k, :, TAPS - 1:], PB[:, k, :].rearrange("p (s t) -> p s t", t=SEQ))
                last.then_inc(s.xi_copied, 1)
                dve.wait_ge(s.xi_copied, 1)
                for k in range(2):
                    xc = b.XC[:, k, :].rearrange("p (s t) -> p s t", t=SEQ)
                    link(nc.vector.tensor_scalar(xc, b.XI[:, k, :, 0:SEQ], w.conv[:, k * TAPS:k * TAPS + 1], w.cb[:, k:k + 1],
                                                 ALU.mult, ALU.add))
                    for tap in range(1, TAPS):
                        last = nc.vector.scalar_tensor_tensor(out=xc, in0=b.XI[:, k, :, tap:tap + SEQ],
                                                              scalar=w.conv[:, k * TAPS + tap:k * TAPS + tap + 1], in1=xc,
                                                              op0=ALU.mult, op1=ALU.add)
                        if tap < TAPS - 1:
                            link(last)
                    last.then_inc(s.conv_done, 1)
                link(nc.vector.tensor_scalar(b.OA[:], b.LO[:], 0.0, None, ALU.is_equal))
                link(nc.vector.tensor_tensor(b.WK[:], b.OA[:], rank, ALU.mult))
                link(nc.vector.tensor_reduce(b.M1[:], b.WK[:], AX.X, ALU.max))
                link(nc.vector.tensor_tensor(b.OA[:], b.WK[:], spread(b.M1[:], E2), ALU.is_equal))
                link(nc.vector.scalar_tensor_tensor(out=b.WK[:], in0=b.OA[:], scalar=-BIG, in1=b.LO[:], op0=ALU.mult, op1=ALU.add))
                link(nc.vector.tensor_reduce(b.M1[:], b.WK[:], AX.X, ALU.max))
                link(nc.vector.tensor_tensor(b.OB[:], b.WK[:], spread(b.M1[:], E2), ALU.is_equal))
                link(nc.vector.tensor_tensor(b.WK[:], b.OB[:], rank, ALU.mult))
                link(nc.vector.tensor_reduce(b.M1[:], b.WK[:], AX.X, ALU.max))
                link(nc.vector.tensor_tensor(b.OB[:], b.WK[:], spread(b.M1[:], E2), ALU.is_equal))
                link(nc.vector.tensor_tensor(b.OA[:], b.OA[:], b.OB[:], ALU.add))
                dve.wait_ge(s.route_exp, 1)
                link(nc.vector.tensor_tensor(b.OA[:], b.OA[:], b.EX[:], ALU.mult))
                link(nc.vector.tensor_reduce(b.SM[:], b.EX[:], AX.X, ALU.add))
                link(nc.vector.reciprocal(b.SM[:], b.SM[:]))
                nc.vector.tensor_tensor(b.OA[:], b.OA[:], spread(b.SM[:], E2), ALU.mult).then_inc(s.gates_ready, 1)
                dve.wait_ge(s.dt_ready, 1)
                for k in range(2):
                    last = nc.vector.tensor_scalar(b.DL[:, k, :], PB[:, k, :], w.dtb[:, k:k + 1], None, ALU.add)
                last.then_inc(s.dt_raw, 1)
                dve.wait_ge(s.dt_raw, 1)
                dve.wait_ge(s.dt_exp, 1)
                nc.vector.tensor_scalar(b.UU[:], b.EE[:], 1.0, None, ALU.add).then_inc(s.dt_u, 1)
                dve.wait_ge(s.dt_u, 1)
                link(nc.vector.scalar_tensor_tensor(out=b.EE[:], in0=b.UU[:], scalar=-1.0, in1=b.EE[:], op0=ALU.add, op1=ALU.subtract))
                dve.wait_ge(s.dt_log, 1)
                link(nc.vector.tensor_tensor(b.EE[:], b.DU[:], b.EE[:], ALU.subtract))
                nc.vector.scalar_tensor_tensor(out=b.DL[:], in0=b.DL[:], scalar=0.0, in1=b.EE[:], op0=ALU.max,
                                               op1=ALU.add).then_inc(s.delta_ready, 1)
                dve.wait_ge(s.delta_ready, 1)
                dve.wait_ge(s.silu_x, 2)
                link(nc.vector.tensor_tensor(b.DU[:], b.DL[:], b.XC[:], ALU.mult))

                def hidden(k):
                    dve.wait_ge(s.hid_ready, k + 1)
                    if k >= 4:
                        dve.wait_ge(s.ffn_ready, k - 3)
                    nc.vector.tensor_scalar(b.H[:, k % 4, :], PB[:, HID_BANKS[k % 3], :], w.b1[:, k:k + 1], 0.0,
                                            ALU.add, ALU.max).then_inc(s.hid_odd, 1)

                def weigh(e):
                    dve.wait_ge(s.bank_done, e + 1)
                    dve.wait_ge(s.gateT_ready, e + 1)
                    nc.vector.tensor_tensor(b.YB[:, e % 2, :], b.YB[:, e % 2, :], PB[:, 6, :], ALU.mult).then_inc(s.weighted, 1)

                for n in range(NS):
                    dve.wait_ge(s.b_ready, n + 1)
                    nc.vector.tensor_tensor(b.DB[:, n % 2, :, :], b.DU[:], PB[:, 0, :].unsqueeze(1).broadcast_to([128, 2, T]),
                                            ALU.mult).then_inc(s.drive_ready, 1)
                    hidden(HTILES * n + 1)
                    dve.wait_ge(s.drive_ready, n + 1)
                    dve.wait_ge(s.decay_ready, n + 1)
                    if n >= 2:
                        dve.wait_ge(s.part_ready, n - 1)
                    nc.vector.tensor_tensor_scan(b.ST[:, n % 2].rearrange("p k t -> p (k t)"), b.DA[:, n % 2].rearrange("p k t -> p (k t)"),
                                                 b.DB[:, n % 2].rearrange("p k t -> p (k t)"), 0.0, ALU.mult, ALU.add).then_inc(s.state_ready, 1)
                    dve.wait_ge(s.state_ready, n + 1)
                    hidden(HTILES * n + 3)
                    if n:
                        weigh(n - 1)
                dve.wait_ge(s.y_summed, 1)
                for k in range(2):
                    last = nc.vector.scalar_tensor_tensor(out=b.YA[:, k, :], in0=b.XC[:, k, :], scalar=w.dskip[:, k:k + 1],
                                                          in1=b.YA[:, k, :], op0=ALU.mult, op1=ALU.add)
                link(last)
                nc.vector.tensor_tensor(b.EE[:], b.YA[:], b.ZS[:], ALU.mult).then_inc(s.y_gated, 1)
                weigh(E2 - 1)
                dve.wait_ge(s.mamba_ready, 1)
                link(nc.vector.tensor_tensor(c.S[:], PB[:, 0, :], c.XN[:], ALU.add))
                dve.wait_ge(s.acc_done, E2)
                gate_vector(nc, dve, s, c, link)

            @block.gpsimd
            def _(pool):
                link = Link(pool, s.pool_link)
                for k in range(2):
                    nc.gpsimd.memset(b.XI[:, k, :, 0:TAPS - 1], 0.0)
                last = nc.gpsimd.memset(b.DA[:].rearrange("p a k (s t) -> p (a k s) t", t=SEQ)[:, :, 0:1], 0.0)
                last.then_inc(s.pads_set, 1)

                def add_bank(e):
                    pool.wait_ge(s.weighted, e + 1)
                    if e == 0:
                        nc.gpsimd.tensor_copy(c.Y[:], b.YB[:, 0, :]).then_inc(s.acc_done, 1)
                    else:
                        nc.gpsimd.tensor_tensor(c.Y[:], c.Y[:], b.YB[:, e % 2, :], ALU.add).then_inc(s.acc_done, 1)
                    pool.wait_ge(s.acc_done, e + 1)

                pool.wait_ge(s.gates_ready, 1)
                for n in range(NS):
                    if n >= 2:
                        pool.wait_ge(s.gateT_ready, n - 1)
                    nc.gpsimd.tensor_copy(b.GS[:, n % 2], b.OA[:, :, n:n + 1].broadcast_to([128, TT, 128])).then_inc(s.gate_spread, 1)
                    pool.wait_ge(s.state_ready, n + 1)
                    pool.wait_ge(s.c_copied, n + 1)
                    cn = b.CN[:, n % 2, :].unsqueeze(1).broadcast_to([128, 2, T])
                    out = b.CH if n else b.YA
                    nc.gpsimd.tensor_tensor(out[:], b.ST[:, n % 2], cn, ALU.mult).then_inc(s.part_ready, 1)
                    pool.wait_ge(s.part_ready, n + 1)
                    if n:
                        last = nc.gpsimd.tensor_tensor(b.YA[:], b.YA[:], b.CH[:], ALU.add)
                        if n < NS - 1:
                            link(last)
                        else:
                            last.then_inc(s.y_summed, 1)
                        add_bank(n - 1)
                add_bank(E2 - 1)
        clear(nc, s)


L3_SEMS = (LN_SEMS + ATT_SEMS + LINKS + "probs_masked logpen_ready penT_copied gate_ready gate_raw gate_exp gate_u "
           "gi_ready penq_ready penT_ready ")


def layer3_attention(nc, c, w, PB):
    with ExitStack() as ctx:
        s = semaphores(nc, ctx, L3_SEMS)
        s = s._replace(probs_ready=s.probs_masked)
        b = att_buffers(nc, ctx, "l3", TS=[2, T], LP=[TT, SEQ], PEN=[TT, SEQ], PQ=[TT, SEQ], T1=[SEQ], T2=[SEQ], GA=[T + TT],
                        GU=[T + TT], GJ=[T], NJ=[T], GI=[TT], AI=[TT], PI=[TT])
        with nc.Block() as block:
            @block.tensor
            def _(pe):
                ln_tensor(nc, pe, s, c, c.X[:], PB)
                pe.wait_ge(s.xn_ready, 1)
                nc.tensor.matmul(PB[:, 2, :], w.grow, c.XN[:], start=True, stop=True)
                for t in range(TT):
                    last = nc.tensor.matmul(PB[:, 3, t:t + 1], c.XN[:, t * 128:(t + 1) * 128], w.gcol, start=True, stop=True)
                last.then_inc(s.gate_ready, 1)
                pe.wait_ge(s.penq_ready, 1)
                for sq in range(NB):
                    for kt in range(2):
                        for qt in range(2):
                            last = nc.tensor.transpose(PB[:, sq, kt * SEQ + qt * 128:kt * SEQ + qt * 128 + 128],
                                                       b.PQ[:, 2 * sq + qt, kt * 128:(kt + 1) * 128], c.ident)
                last.then_inc(s.penT_ready, 1)
                pe.wait_ge(s.penT_copied, 1)
                att_tensor(nc, pe, s, c, w, b, PB, c.unpad)

            @block.scalar
            def _(act):
                link = Link(act, s.act_link)
                ln_scalar(nc, act, s, c, PB, link)
                act.wait_ge(s.gate_raw, 1)
                link(nc.scalar.activation(b.GU[:], b.GA[:], ACT.Abs))
                link(nc.scalar.activation(b.GU[:], b.GU[:], ACT.Exp, scale=-1.0))
                nc.scalar.activation(b.GU[:], b.GU[:], ACT.Ln, bias=c.one).then_inc(s.gate_exp, 1)
                act.wait_ge(s.gate_u, 1)
                link(nc.scalar.activation(b.GJ[:], b.GU[:, 0:T], ACT.Exp))
                nc.scalar.activation(b.GI[:], b.GU[:, T:T + TT], ACT.Exp).then_inc(s.gi_ready, 1)
                act.wait_ge(s.gi_ready, 1)
                link(nc.scalar.activation(b.PI[:], b.GI[:], ACT.Exp, scale=-float(np.log(SEQ - 2)), bias=c.pow))
                act.sem_inc(s.gi_ready, 1)
                act.wait_ge(s.penq_ready, 1)
                link(nc.scalar.activation(b.LP[:], b.PQ[:], ACT.Ln, scale=PEN_SCALE))
                nc.scalar.activation(b.LP[:], b.LP[:], ACT.Identity, bias=c.lnpen).then_inc(s.logpen_ready, 1)
                att_scalar(nc, act, s, c, b, PB, link, c.bqs, True)

            @block.vector
            def _(dve):
                link = Link(dve, s.dve_link)
                ln_vector(nc, dve, s, c, c.X[:], c.XN[:], PB).then_inc(s.xn_ready, 1)
                dve.wait_ge(s.gate_ready, 1)
                nc.vector.tensor_scalar(b.GA[:, 0:T], PB[:, 2, :], w.bg, None, ALU.add)
                nc.vector.tensor_scalar(b.GA[:, T:T + TT], PB[:, 3, 0:TT], w.bg, None, ALU.add).then_inc(s.gate_raw, 1)
                dve.wait_ge(s.gate_raw, 1)
                dve.wait_ge(s.gate_exp, 1)
                nc.vector.scalar_tensor_tensor(out=b.GU[:], in0=b.GA[:], scalar=0.0, in1=b.GU[:], op0=ALU.min,
                                               op1=ALU.subtract).then_inc(s.gate_u, 1)
                dve.wait_ge(s.gi_ready, 2)
                link(nc.vector.tensor_scalar(b.NJ[:], b.GJ[:], -1.0, None, ALU.mult))
                link(nc.vector.tensor_scalar(b.AI[:], b.GI[:], -1.0, 1.0, ALU.mult, ALU.add))
                for t in range(TT):
                    gj = slice(t // 2 * SEQ, (t // 2 + 1) * SEQ)
                    ai, gi, pi = b.AI[:, t:t + 1], b.GI[:, t:t + 1], b.PI[:, t:t + 1]
                    nc.vector.tensor_scalar(b.T2[:], b.GJ[:, gj], ai, 1.0, ALU.add, ALU.min)
                    link(nc.vector.tensor_scalar(b.T1[:], b.NJ[:, gj], ai, 0.0, ALU.add, ALU.max))
                    link(nc.vector.tensor_scalar(b.T1[:], b.T1[:], ai, None, ALU.mult))
                    link(nc.vector.scalar_tensor_tensor(out=b.T1[:], in0=b.T2[:], scalar=gi, in1=b.T1[:], op0=ALU.mult, op1=ALU.add))
                    link(nc.vector.tensor_scalar(b.T2[:], c.dist[:, t % 2 * SEQ:(t % 2 + 1) * SEQ], pi, 1.0, ALU.add, ALU.min))
                    link(nc.vector.scalar_tensor_tensor(out=b.T1[:], in0=b.T2[:], scalar=1e-32, in1=b.T1[:], op0=ALU.max, op1=ALU.mult))
                    last = nc.vector.tensor_scalar(b.PQ[:, t, :], b.T1[:], 1e-32, None, ALU.max)
                    if t < TT - 1:
                        link(last)
                last.then_inc(s.penq_ready, 1)
                dve.wait_ge(s.penT_ready, 1)
                nc.vector.tensor_copy(b.PEN[:].rearrange("p t q -> p (t q)"), PB[:, 0:2, :].rearrange("p a q -> p (a q)")).then_inc(s.penT_copied, 1)
                att_vector(nc, dve, s, c, w, b, PB, link, True)
                dve.wait_ge(s.att_ready, 1)
                link(nc.vector.tensor_copy(c.S[:], PB[:, 0, :]))

            @block.gpsimd
            def _(pool):
                att_gpsimd(nc, pool, s, c, b, Link(pool, s.pool_link), True)
        clear(nc, s)


L3F_SEMS = (LN_SEMS + GATE_SEMS + LINKS + "pad_set shift_done raw_ready raw_copied squared norm_ready norm_taken norm_guarded rot_ready "
            "cos_done sin_done rnorm_ready rot_summed qk_ready v_ready v_copied win_ready win_shifted prob_ready probT_ready "
            "probT_copied ctx_ready ctx_recip ctx_scaled o_ready x_added hn_ready gate_in_ready gelu_done val_ready hid_ready "
            "out_ready layer_done ")
NW = SEQ // WIN
NT = LI // 128
FT = [(0, 128), (128, 128), (256, HIDL - 256)]


def layer3_ffn(nc, c, ws, PB):
    with ExitStack() as ctx:
        s = semaphores(nc, ctx, L3F_SEMS)
        b = buffers(nc, ctx, "l3f", HS=[NB, SEQ], HN=[T], RW=[2, T], SQ=[2, T], C1=[2, T], C2=[2, T], NR=[2, T], RN=[2, T],
                    QK=[2 * NT, T], VL=[NB, 3, LI], MX=[NW], SH=[2, T], PP=[2, T], PT=[2, T], OF=[NT, T], LG=[T],
                    RG=[2, T], G=[3, T], HH=[3, T])
        F = c.XN
        U, A = 2 * NT, NT * NB

        with nc.Block() as block:
            @block.tensor
            def _(pe):
                for l in range(DEPTH):
                    w, u0, a0 = ws[l], l * U, l * A
                    pe.wait_ge(s.shift_done, 2 * l + 1)
                    hs = b.HS[:].rearrange("p s t -> p (s t)")
                    for u in range(U + 1):
                        if u < U:
                            if u >= 2:
                                pe.wait_ge(s.raw_copied, u0 + u - 1)
                            nc.tensor.matmul(PB[:, u % 2, :], w.qkv[:, u * 128:(u + 1) * 128], hs, start=True, stop=True).then_inc(s.raw_ready, 1)
                        if u < NB * 3:
                            sq, o = divmod(u, 3)
                            if u >= 2:
                                pe.wait_ge(s.v_copied, NB * 3 * l + u - 1)
                            t0 = sq * SEQ + o * WIN
                            nc.tensor.matmul(PB[:, 6 + u % 2, :], hs[:, t0:t0 + 128], w.qkv[:, 2 * LI:3 * LI], start=True, stop=True).then_inc(s.v_ready, 1)
                        if u:
                            v = u - 1
                            if v >= 2:
                                pe.wait_ge(s.norm_taken, u0 + v - 1)
                                pe.wait_ge(s.sin_done, u0 + v - 1)
                            pe.wait_ge(s.raw_copied, u0 + v + 1)
                            nc.tensor.matmul(PB[:, 4 + v % 2, :], c.rotq[l] if v < NT else c.rotk[l], b.RW[:, v % 2, :],
                                             start=True, stop=True).then_inc(s.rot_ready, 1)
                            pe.wait_ge(s.squared, u0 + v + 1)
                            nc.tensor.matmul(PB[:, 2 + v % 2, :], c.bd64, b.SQ[:, v % 2, :], start=True, stop=True).then_inc(s.norm_ready, 1)
                    pe.wait_ge(s.v_copied, NB * 3 * (l + 1))
                    pe.wait_ge(s.norm_taken, u0 + U)
                    pe.wait_ge(s.sin_done, u0 + U)
                    pe.wait_ge(s.qk_ready, u0 + U)
                    for m in range(A + 3):
                        if m < A:
                            hp, sq = divmod(m, NB)
                            if m >= 2:
                                pe.wait_ge(s.win_shifted, a0 + m - 1)
                            for win in range(NW):
                                q0 = sq * SEQ + win * WIN
                                k0 = q0 - WIN if win else q0
                                for h in range(2):
                                    r = slice(LD * h, LD * h + LD)
                                    last = nc.tensor.matmul(PB[r, m % 2, win * 128:win * 128 + 2 * WIN], b.QK[r, hp, q0:q0 + WIN],
                                                            b.QK[r, NT + hp, k0:k0 + 2 * WIN], start=win == 0, stop=False,
                                                            skip_group_check=True)
                            last = nc.tensor.matmul(PB[:, m % 2, :], c.identb, c.windowb, start=False, stop=True, skip_group_check=True)
                            last.then_inc(s.win_ready, 1)
                        v = m - 2
                        if 0 <= v < A:
                            pe.wait_ge(s.prob_ready, a0 + v + 1)
                            if v >= 2:
                                pe.wait_ge(s.probT_copied, a0 + v - 1)
                            for win in range(NW):
                                last = nc.tensor.transpose(PB[:, 2 + v % 2, win * 128:(win + 1) * 128],
                                                           b.PP[:, v % 2, win * 128:(win + 1) * 128], c.ident)
                            last.then_inc(s.probT_ready, 1)
                        v = m - 3
                        if 0 <= v < A:
                            hp, sq = divmod(v, NB)
                            if sq == 0 and hp >= 2:
                                pe.wait_ge(s.ctx_scaled, l * NT + hp - 1)
                            pe.wait_ge(s.probT_copied, a0 + v + 1)
                            k = 4 + 2 * (hp % 2)
                            for win in range(NW):
                                o0 = sq * SEQ + win * WIN
                                for h in range(2):
                                    r = slice(LD * h, LD * h + LD)
                                    p = b.PT[:, v % 2, win * 128 + h * WIN:win * 128 + h * WIN + WIN]
                                    f0 = (2 * hp + h) * LD
                                    nc.tensor.matmul(PB[r, k, o0:o0 + WIN], b.VL[:, sq, max(win - 1, 0), f0:f0 + LD], p,
                                                     start=True, stop=True, tile_position=(0, LD * h))
                                    last = nc.tensor.matmul(PB[r, k + 1, o0:o0 + WIN], c.ones[:, 0:LD], p,
                                                            start=True, stop=True, tile_position=(0, LD * h))
                            last.then_inc(s.ctx_ready, 1)
                    for t in range(NT):
                        pe.wait_ge(s.ctx_scaled, l * NT + t + 1)
                        last = nc.tensor.matmul(PB[:, 2, :], w.o[:, t * 128:(t + 1) * 128], b.OF[:, t, :], start=t == 0, stop=t == NT - 1)
                    last.then_inc(s.o_ready, 1)
                    pe.wait_ge(s.shift_done, 2 * l + 2)
                    ln_tensor(nc, pe, s, c, hs, PB, l)
                    pe.wait_ge(s.hn_ready, l + 1)
                    for i, (f0, fn) in enumerate(FT):
                        nc.tensor.matmul(PB[0:fn, 2 + i, :], w.wg[:, f0:f0 + fn], b.HN[:], start=True, stop=True).then_inc(s.gate_in_ready, 1)
                        nc.tensor.matmul(PB[0:fn, 5 + i, :], w.wa[:, f0:f0 + fn], b.HN[:], start=True, stop=True).then_inc(s.val_ready, 1)
                    for i, (f0, fn) in enumerate(FT):
                        pe.wait_ge(s.hid_ready, 3 * l + i + 1)
                        last = nc.tensor.matmul(PB[:, 0, :], w.w2[0:fn, i * 128:(i + 1) * 128], b.HH[0:fn, i, :], start=i == 0, stop=i == 2)
                    last.then_inc(s.out_ready, 1)

            @block.scalar
            def _(act):
                link = Link(act, s.act_link)
                for l in range(DEPTH):
                    w, u0, a0 = ws[l], l * U, l * A
                    for u in range(U + 1):
                        if u < U:
                            act.wait_ge(s.raw_ready, u0 + u + 1)
                            if u >= 2:
                                act.wait_ge(s.squared, u0 + u - 1)
                                act.wait_ge(s.rot_ready, u0 + u - 1)
                                act.wait_ge(s.cos_done, u0 + u - 1)
                            nc.scalar.activation(b.RW[:, u % 2, :], PB[:, u % 2, :], ACT.Copy).then_inc(s.raw_copied, 1)
                        if u < NB * 3:
                            sq, o = divmod(u, 3)
                            act.wait_ge(s.v_ready, NB * 3 * l + u + 1)
                            nc.scalar.activation(b.VL[:, sq, o, :], PB[:, 6 + u % 2, :], ACT.Copy).then_inc(s.v_copied, 1)
                        if u:
                            v = u - 1
                            act.wait_ge(s.norm_guarded, u0 + v + 1)
                            link(nc.scalar.activation(b.NR[:, v % 2, :], b.NR[:, v % 2, :], ACT.Ln, scale=NORM_SCALE))
                            if v >= 2:
                                act.wait_ge(s.qk_ready, u0 + v - 1)
                            nc.scalar.activation(b.RN[:, v % 2, :], b.NR[:, v % 2, :], ACT.Exp, scale=-0.5, bias=c.lnnorm).then_inc(s.rnorm_ready, 1)
                    for m in range(A + 4):
                        if m < A:
                            act.wait_ge(s.win_shifted, a0 + m + 1)
                            if m >= 2:
                                act.wait_ge(s.probT_ready, a0 + m - 1)
                            nc.scalar.activation(b.PP[:, m % 2, :], b.SH[:, m % 2, :], ACT.Exp, scale=8.0).then_inc(s.prob_ready, 1)
                        v = m - 2
                        if 0 <= v < A:
                            act.wait_ge(s.probT_ready, a0 + v + 1)
                            if v >= 2:
                                act.wait_ge(s.ctx_ready, a0 + v - 1)
                            nc.scalar.activation(b.PT[:, v % 2, :], PB[:, 2 + v % 2, :], ACT.Copy).then_inc(s.probT_copied, 1)
                        v = m - 4
                        if 0 <= v and v % NB == NB - 1:
                            hp = v // NB
                            act.wait_ge(s.ctx_ready, a0 + v + 1)
                            link(nc.scalar.activation(b.LG[:], PB[:, 5 + 2 * (hp % 2), :], ACT.Ln))
                            if l or hp >= 2:
                                act.wait_ge(s.ctx_scaled, l * NT + hp - 1)
                            nc.scalar.activation(b.RG[:, hp % 2, :], b.LG[:], ACT.Exp, scale=-1.0).then_inc(s.ctx_recip, 1)
                            act.wait_ge(s.ctx_recip, l * NT + hp + 1)
                    ln_scalar(nc, act, s, c, PB, link, l)
                    for i, (f0, fn) in enumerate(FT):
                        act.wait_ge(s.gate_in_ready, 3 * l + i + 1)
                        nc.scalar.activation(b.G[0:fn, i, :], PB[0:fn, 2 + i, :], ACT.Gelu, bias=w.bgl[0:fn, i:i + 1]).then_inc(s.gelu_done, 1)
                act.wait_ge(s.layer_done, DEPTH)
                gate_scalar(nc, act, s, c, link)

            @block.vector
            def _(dve):
                link = Link(dve, s.dve_link)

                def shift():
                    nc.vector.tensor_copy(b.HS[0:64, :, :], F[0:64, :].rearrange("p (s t) -> p s t", t=SEQ))
                    nc.vector.tensor_copy(b.HS[64:128, :, 1:SEQ],
                                          F[64:128, :].rearrange("p (s t) -> p s t", t=SEQ)[:, :, 0:SEQ - 1]).then_inc(s.shift_done, 1)

                dve.wait_ge(s.pad_set, 1)
                two = lambda x: x.unsqueeze(1).broadcast_to([128, NB, SEQ])
                for l in range(DEPTH):
                    w, u0, a0 = ws[l], l * U, l * A
                    shift()
                    dve.wait_ge(s.shift_done, 2 * l + 1)
                    for u in range(U + 1):
                        seq = lambda x: x.rearrange("p (s t) -> p s t", t=SEQ)
                        if u < U:
                            cos, sin = (c.qcos, c.qsin) if u < NT else (c.kcos, c.ksin)
                            dve.wait_ge(s.raw_copied, u0 + u + 1)
                            if u >= 2:
                                dve.wait_ge(s.rot_summed, u0 + u - 1)
                                dve.wait_ge(s.qk_ready, u0 + u - 1)
                            nc.vector.scalar_tensor_tensor(out=seq(b.C1[:, u % 2, :]), in0=seq(b.RW[:, u % 2, :]),
                                                           scalar=w.qs if u < NT else w.ks, in1=two(cos),
                                                           op0=ALU.mult, op1=ALU.mult).then_inc(s.cos_done, 1)
                            dve.wait_ge(s.rot_ready, u0 + u + 1)
                            nc.vector.tensor_tensor(seq(b.C2[:, u % 2, :]), seq(PB[:, 4 + u % 2, :]), two(sin), ALU.mult).then_inc(s.sin_done, 1)
                            dve.wait_ge(s.norm_ready, u0 + u + 1)
                            if u >= 2:
                                dve.wait_ge(s.rnorm_ready, u0 + u - 1)
                            nc.vector.tensor_scalar(b.NR[:, u % 2, :], PB[:, 2 + u % 2, :], 1e-24, None, ALU.max).then_inc(s.norm_taken, 1)
                            dve.wait_ge(s.norm_taken, u0 + u + 1)
                            dve.sem_inc(s.norm_guarded, 1)
                        if u:
                            v = u - 1
                            dve.wait_ge(s.rnorm_ready, u0 + v + 1)
                            dve.wait_ge(s.rot_summed, u0 + v + 1)
                            nc.vector.tensor_tensor(b.QK[:, v, :], b.C1[:, v % 2, :], b.RN[:, v % 2, :], ALU.mult).then_inc(s.qk_ready, 1)
                    dve.wait_ge(s.qk_ready, u0 + U)
                    for m in range(A + 5):
                        if m < A:
                            dve.wait_ge(s.win_ready, a0 + m + 1)
                            pw = PB[:, m % 2, :].rearrange("p (w k) -> p w k", k=128)
                            link(nc.vector.tensor_reduce(b.MX[:], pw, AX.X, ALU.max))
                            if m >= 2:
                                dve.wait_ge(s.prob_ready, a0 + m - 1)
                            nc.vector.tensor_tensor(b.SH[:, m % 2, :].rearrange("p (w k) -> p w k", k=128), pw,
                                                    b.MX[:].unsqueeze(2).broadcast_to([128, NW, 128]), ALU.subtract).then_inc(s.win_shifted, 1)
                            dve.wait_ge(s.win_shifted, a0 + m + 1)
                        v = m - 5
                        if 0 <= v and v % NB == NB - 1:
                            hp = v // NB
                            dve.wait_ge(s.ctx_recip, l * NT + hp + 1)
                            nc.vector.tensor_tensor(b.OF[:, hp, :], PB[:, 4 + 2 * (hp % 2), :], b.RG[:, hp % 2, :], ALU.mult).then_inc(s.ctx_scaled, 1)
                    dve.wait_ge(s.o_ready, l + 1)
                    link(nc.vector.tensor_tensor(F[:], F[:], PB[:, 2, :], ALU.add))
                    shift()
                    dve.wait_ge(s.shift_done, 2 * l + 2)
                    link(ln_vector(nc, dve, s, c, b.HS[:].rearrange("p s t -> p (s t)"), b.HN[:], PB, l))
                    nc.vector.tensor_scalar(b.HN[:], b.HN[:], w.lg, w.lb, ALU.mult, ALU.add).then_inc(s.hn_ready, 1)
                    for i, (f0, fn) in enumerate(FT):
                        dve.wait_ge(s.gelu_done, 3 * l + i + 1)
                        dve.wait_ge(s.val_ready, 3 * l + i + 1)
                        nc.vector.scalar_tensor_tensor(out=b.HH[0:fn, i, :], in0=PB[0:fn, 5 + i, :], scalar=w.ba[0:fn, i:i + 1],
                                                       in1=b.G[0:fn, i, :], op0=ALU.add, op1=ALU.mult).then_inc(s.hid_ready, 1)
                    dve.wait_ge(s.out_ready, l + 1)
                    out = F if l < DEPTH - 1 else c.Y
                    nc.vector.scalar_tensor_tensor(out=out[:], in0=PB[:, 0, :], scalar=w.b2, in1=F[:],
                                                   op0=ALU.add, op1=ALU.add).then_inc(s.layer_done, 1)
                    dve.wait_ge(s.layer_done, l + 1)
                gate_vector(nc, dve, s, c, link)

            @block.gpsimd
            def _(pool):
                nc.gpsimd.memset(b.HS[64:128, :, 0:1], 0.0).then_inc(s.pad_set, 1)
                for l in range(DEPTH):
                    u0 = l * U
                    for u in range(U):
                        pool.wait_ge(s.raw_copied, u0 + u + 1)
                        if u >= 2:
                            pool.wait_ge(s.norm_ready, u0 + u - 1)
                        nc.gpsimd.tensor_tensor(b.SQ[:, u % 2, :], b.RW[:, u % 2, :], b.RW[:, u % 2, :], ALU.mult).then_inc(s.squared, 1)
                        pool.wait_ge(s.cos_done, u0 + u + 1)
                        pool.wait_ge(s.sin_done, u0 + u + 1)
                        nc.gpsimd.tensor_tensor(b.C1[:, u % 2, :], b.C1[:, u % 2, :], b.C2[:, u % 2, :], ALU.add).then_inc(s.rot_summed, 1)
        clear(nc, s)


def network(nc, x, consts, w0, w1, w2, w2f, w3, w3f, out, layers):
    tokens = x.shape[0]
    chunks = tokens // T
    with ExitStack() as ctx:
        def sb(name, parts):
            return ctx.enter_context(nc.sbuf_tensor(name, [128, columns(parts)[1]], F32))

        pieces = [("consts", CONSTS, consts), ("w0s", W0, w0), ("w1s", W1, w1), ("w2s", W2, w2), ("w3s", W3, w3), ("w3fs", W3F, w3f)]
        tiles = {n: sb(n, parts) for n, parts, _ in pieces}
        c = view(tiles["consts"], CONSTS)
        v0, v1, v2, v3 = view(tiles["w0s"], W0), view(tiles["w1s"], W1), view(tiles["w2s"], W2), view(tiles["w3s"], W3)
        per_layer = columns(W3F)[1] // DEPTH
        ws = [view(tiles["w3fs"][:, l * per_layer:(l + 1) * per_layer], W3F_LAYER) for l in range(DEPTH)]
        keep = buffers(nc, ctx, "keep", X=[T], XN=[T], S=[T], Y=[T], lnc=[T], lnsq=[T], lnr=[T], ga=[T], gb=[T],
                       aneg=[2 * NS], bqs=[4], XI0=[TT, 128])
        identb = ctx.enter_context(nc.sbuf_tensor("identb", [128, 128], BF16))
        windowb = ctx.enter_context(nc.sbuf_tensor("windowb", [128, 512], BF16))
        rots = ctx.enter_context(nc.sbuf_tensor("rots", [128, 2 * DEPTH, 128], F32))
        c = record(**c._asdict(), **keep._asdict(), identb=identb[:], windowb=windowb[:],
                   rotq=[rots[:, 2 * l, :] for l in range(DEPTH)], rotk=[rots[:, 2 * l + 1, :] for l in range(DEPTH)])
        PB = ctx.enter_context(nc.psum_tensor("PB", [128, 8, 512], F32))

        with ExitStack() as pro:
            s = semaphores(nc, pro, "loaded exped folded fold_ready dve_link")
            with nc.Block() as block:
                @block.sync
                def _(sp):
                    for n, _, src in pieces:
                        sp.dma_start(tiles[n][:], src).then_inc(s.loaded, 16)

                @block.scalar
                def _(act):
                    act.wait_ge(s.loaded, 16 * len(pieces))
                    nc.scalar.activation(c.aneg[:], v2.alog, ACT.Exp).then_inc(s.exped, 1)

                @block.tensor
                def _(pe):
                    pe.wait_ge(s.loaded, 16 * len(pieces))
                    nc.tensor.matmul(PB[:, 0, 0:1], v0.woutm[0:64, :], v0.b2m[0:64, :], start=True, stop=True).then_inc(s.folded, 1)

                @block.vector
                def _(dve):
                    link = Link(dve, s.dve_link)
                    dve.wait_ge(s.loaded, 16 * len(pieces))
                    win = v0.win.unsqueeze(2).broadcast_to([128, 64, 16])
                    w1 = v0.w1.rearrange("p (m h) -> p m h", h=16)
                    nc.vector.tensor_tensor(w1, w1, win, ALU.mult)
                    w2 = v0.w2.rearrange("p (i d) -> p i d", d=128)
                    nc.vector.tensor_tensor(w2, w2, v0.w2c.unsqueeze(2).broadcast_to([128, 8, 128]), ALU.mult)
                    link(nc.vector.tensor_tensor(v0.w1c, v0.w1c, v0.binc, ALU.mult))
                    nc.vector.tensor_tensor(v0.b1c, v0.b1c, v0.w1c, ALU.add)
                    dve.wait_ge(s.folded, 1)
                    nc.vector.tensor_tensor(v0.bout, v0.bout, PB[:, 0, 0:1], ALU.add)
                    dve.wait_ge(s.exped, 1)
                    nc.vector.tensor_scalar(c.aneg[:], c.aneg[:], -1.0, None, ALU.mult)
                    nc.vector.tensor_scalar(c.bqs[:], v3.bq, float(DH) ** -0.5, None, ALU.mult)
                    nc.vector.tensor_copy(c.identb, c.ident)
                    nc.vector.tensor_copy(c.windowb, c.window)
                    for l in range(DEPTH):
                        nc.vector.tensor_scalar(c.rotq[l], c.rot, ws[l].qs, None, ALU.mult)
                        nc.vector.tensor_scalar(c.rotk[l], c.rot, ws[l].ks, None, ALU.mult)
            clear(nc, s)

        x_mid = nc.dram_tensor("x_mid", (chunks * 128, T), F32, kind="Internal").ap()
        s_mid = nc.dram_tensor("s_mid", (chunks * 128, T), F32, kind="Internal").ap()
        y_mid = nc.dram_tensor("y_mid", (tokens, D), F32, kind="Internal").ap()

        with ExitStack() as first:
            r = record(base=first.enter_context(nc.sbuf_tensor("base", [128, E1], F32)),
                                rank=first.enter_context(nc.sbuf_tensor("rank", [128, tokens // 128], F32)),
                                route=first.enter_context(nc.sbuf_tensor("route", [128, tokens // 128, E1], F32)),
                                y=first.enter_context(nc.sbuf_tensor("y", [128, tokens // 128, D], F32)))
            with nc.Block() as block:
                @block.vector
                def _(dve):
                    nc.vector.memset(r.base[:], 0.0)
            with nc.Fori(0, chunks) as it:
                with ExitStack() as io:
                    s = semaphores(nc, io, "x_loaded xT_ready ")
                    with nc.Block() as block:
                        @block.sync
                        def _(sp):
                            sp.dma_start(c.XI0[:], x[bass.ts(it, T), :].rearrange("(t p) d -> p t d", p=128)).then_inc(s.x_loaded, 16)

                        @block.tensor
                        def _(pe):
                            pe.wait_ge(s.x_loaded, 16)
                            for t in range(TT):
                                last = nc.tensor.transpose(PB[:, 0, t * 128:(t + 1) * 128], c.XI0[:, t, :], c.ident)
                            last.then_inc(s.xT_ready, 1)

                        @block.vector
                        def _(dve):
                            dve.wait_ge(s.xT_ready, 1)
                            nc.vector.tensor_copy(c.X[:], PB[:, 0, :])
                    clear(nc, s)
                layer0(nc, c, v0, PB)
                layer1(nc, c, v1, r, it, x_mid, s_mid, PB)
            place_tokens(nc, r, tokens // 128, y_mid)

        with nc.Fori(0, chunks) as it:
            with ExitStack() as io:
                s = semaphores(nc, io, GATE_SEMS + "x_loaded s_loaded y_loaded yT_ready y_ready act_link dve_link ")
                with nc.Block() as block:
                    @block.sync
                    def _(sp):
                        sp.dma_start(c.XI0[:], y_mid[bass.ts(it, T), :].rearrange("(t p) d -> p t d", p=128)).then_inc(s.y_loaded, 16)
                        sp.dma_start(c.S[:], s_mid[bass.ts(it, 128), :]).then_inc(s.s_loaded, 16)
                        sp.dma_start(c.X[:], x_mid[bass.ts(it, 128), :]).then_inc(s.x_loaded, 16)

                    @block.tensor
                    def _(pe):
                        pe.wait_ge(s.y_loaded, 16)
                        for t in range(TT):
                            last = nc.tensor.transpose(PB[:, 0, t * 128:(t + 1) * 128], c.XI0[:, t, :], c.ident)
                        last.then_inc(s.yT_ready, 1)

                    @block.scalar
                    def _(act):
                        act.wait_ge(s.y_ready, 1)
                        gate_scalar(nc, act, s, c, Link(act, s.act_link))

                    @block.vector
                    def _(dve):
                        dve.wait_ge(s.yT_ready, 1)
                        nc.vector.tensor_copy(c.Y[:], PB[:, 0, :]).then_inc(s.y_ready, 1)
                        dve.wait_ge(s.y_ready, 1)
                        dve.wait_ge(s.s_loaded, 16)
                        dve.wait_ge(s.x_loaded, 16)
                        gate_vector(nc, dve, s, c, Link(dve, s.dve_link))
                clear(nc, s)
            if layers > 2:
                layer2(nc, c, v2, w2f, PB)
            if layers > 3:
                layer3_attention(nc, c, v3, PB)
                layer3_ffn(nc, c, ws, PB)
            with ExitStack() as io:
                s = semaphores(nc, io, "xT_ready x_copied x_stored")
                with nc.Block() as block:
                    @block.tensor
                    def _(pe):
                        for t in range(TT):
                            last = nc.tensor.transpose(PB[:, 0, t * 128:(t + 1) * 128], c.X[:, t * 128:(t + 1) * 128], c.ident)
                        last.then_inc(s.xT_ready, 1)

                    @block.vector
                    def _(dve):
                        dve.wait_ge(s.xT_ready, 1)
                        nc.vector.tensor_copy(c.XI0[:].rearrange("p t d -> p (t d)"), PB[:, 0, :]).then_inc(s.x_copied, 1)

                    @block.sync
                    def _(sp):
                        sp.wait_ge(s.x_copied, 1)
                        sp.dma_start(out[bass.ts(it, T), :].rearrange("(t p) d -> p t d", p=128), c.XI0[:]).then_inc(s.x_stored, 16)
                        sp.wait_ge(s.x_stored, 16)
                clear(nc, s)


def constants():
    p = np.arange(128)
    k = {}
    k["ident"] = np.eye(128)
    k["mean"] = np.full((128, 128), 1.0 / D)
    k["ones"] = np.ones((128, 128))
    k["before"] = p[:, None] < p[None, :]
    k["sumsel"] = (p[:, None] == p[None, :] // 32 * 32 + DH)
    k["bd8"] = p[:, None] // DH == p[None, :] // DH
    k["bd64"] = p[:, None] // LD == p[None, :] // LD
    un = np.zeros((128, 4, 128))
    for g in range(4):
        for j in range(4):
            for d in range(DH):
                un[32 * j + d, g, (4 * g + j) * DH + d] = 1
    k["unpad"] = un.reshape(128, 512)
    dec = np.exp(-np.arange(SEQ, dtype=np.float32) / np.float32(SEQ))
    k["decrow"] = np.broadcast_to(dec, (128, SEQ))
    k["dectok"] = dec.reshape(2, 128).T
    k["rank8"] = np.broadcast_to(np.arange(E1, 0, -1), (128, E1))
    k["rank16"] = np.broadcast_to(np.arange(E2, 0, -1), (128, E2))
    q = np.arange(2)[None, :, None] * 128 + p[:, None, None]
    k["dist"] = (2.0 - np.abs(q - np.arange(SEQ)[None, None, :])).reshape(128, 2 * SEQ)
    f = np.float32
    half = np.arange(0, LD, 2, dtype=f)
    inv = f(1.0) / f(10000.0) ** (half / f(LD))
    t = np.arange(SEQ, dtype=f)
    fr = (t[:, None] * inv[None, :]).astype(f)
    base = (half + f(0.4 * LD)) / f(1.4 * LD)
    scale = base[None, :] ** ((t - SEQ // 2) / f(WIN // 2))[:, None]
    rep = lambda a: np.tile(a.T, (4, 1))
    cos, sin = np.cos(fr), np.sin(fr)
    k["qcos"], k["qsin"], k["kcos"], k["ksin"] = rep(cos * scale), rep(sin * scale), rep(cos / scale), rep(sin / scale)
    rot = np.zeros((128, 128))
    for m in range(128):
        if m % LD < LD // 2:
            rot[m + LD // 2, m] = -1
        else:
            rot[m - LD // 2, m] = 1
    k["rot"] = rot
    a, cc, win = p[:, None, None] % WIN, np.arange(128)[None, None, :], np.arange(NW)[None, :, None]
    ok = np.where(win == 0, (cc < WIN) & (cc <= a), (cc - WIN <= a) & (a <= cc))
    k["window"] = np.where(ok, 0.0, -1.0e30).reshape(128, NW * 128)
    one = np.ones((128, 1))
    k["eps"], k["one"], k["aeps"] = one * 1e-5, one, one * 1e-6
    k["kone"] = (p % 32 == DH)[:, None]
    k["pow"] = one * np.log(SEQ - 2)
    k["lnpen"] = one * -np.log(PEN_SCALE)
    k["lnnorm"] = one * 0.5 * np.log(NORM_SCALE)
    return pack(CONSTS, k)


def pack(parts, arrays):
    at, width = columns(parts)
    out = np.zeros((128, width), np.float32)
    for n, (a, w) in at.items():
        out[:arrays[n].shape[0], a:a + w] = arrays[n]
    return out


def heads_apart(a):
    out = np.zeros((a.shape[0], NG, 4, 32), a.dtype)
    out[:, :, :, :DH] = a.reshape(a.shape[0], NG, 4, DH)
    return out.reshape(a.shape[0], 512)


def layouts(i):
    rep = lambda a: np.broadcast_to(a, (128, a.size))
    cols = lambda a: a.reshape(-1, 128).T
    out0 = heads_apart(i["L0_attn_Wout"].T).reshape(D, NG, 128).transpose(2, 1, 0).reshape(128, 512)
    w0 = dict(q=heads_apart(i["L0_attn_Wq"]), k=heads_apart(i["L0_attn_Wk"]), v=i["L0_attn_Wv"], out=out0,
              w1=rep(i["L0_ffn_W1"].reshape(-1)), win=i["L0_ffn_Win"],
              w2=np.repeat(i["L0_ffn_Wout"], 16, axis=0).reshape(8, 128, 128).transpose(1, 0, 2).reshape(128, 1024),
              w1c=cols(i["L0_ffn_W1"]), b1c=cols(i["L0_ffn_b1"]), binc=cols(np.repeat(i["L0_ffn_bin_"], 16)),
              w2c=cols(i["L0_ffn_W2"]), woutm=i["L0_ffn_Wout"], b2m=i["L0_ffn_b2"][:, None], bout=i["L0_ffn_bout"][:, None])
    side = lambda a: a.transpose(1, 0, 2).reshape(a.shape[1], -1)
    w1 = dict(q=i["L1_attn_W_q"].T, kv=np.concatenate([i["L1_attn_W_k"].T, i["L1_attn_W_v"].T], 1), o=i["L1_attn_W_o"].T,
              bq=i["L1_attn_b_q"][:, None], bkv=rep(np.concatenate([i["L1_attn_b_k"], i["L1_attn_b_v"]])),
              bo=i["L1_attn_b_o"][:, None], s=i["L1_ffn_Ws"].T, bs=rep(i["L1_ffn_bs"]), w1=side(i["L1_ffn_W1"]),
              b1=i["L1_ffn_b1"].T, w2=side(i["L1_ffn_W2"]), b2=i["L1_ffn_b2"])
    halves = lambda a: side(a.reshape(2, 128, -1))
    w2 = dict(g=i["L2_attn_ln_g"][:, None], b=i["L2_attn_ln_b"][:, None], win=i["L2_attn_W_in"],
              conv=halves(i["L2_attn_conv_w"]), cb=cols(i["L2_attn_conv_b"]), xp=halves(i["L2_attn_W_xp"]), dt=i["L2_attn_W_dt"],
              dtb=cols(i["L2_attn_dt_bias"]), alog=halves(i["L2_attn_A_log"]), dskip=cols(i["L2_attn_D_skip"]),
              out=halves(i["L2_attn_W_out"]), r=i["L2_ffn_Wr"], br=rep(i["L2_ffn_br"]), b1=cols(i["L2_ffn_b1"]), b2=i["L2_ffn_b2"].T)
    w2f = np.concatenate([i["L2_ffn_W1"], i["L2_ffn_W2"].reshape(E2, 4, 128, D).transpose(0, 2, 1, 3).reshape(E2, 128, 512)], 2)
    w3 = dict(q=heads_apart(i["L3_attn_Wq"]), k=heads_apart(i["L3_attn_Wk"]), v=i["L3_attn_Wv"], bv=rep(i["L3_attn_bv"]),
              bq=heads_apart(i["L3_attn_bq"][None]).reshape(NG, 128).T, bk=heads_apart(i["L3_attn_bk"][None]).reshape(NG, 128).T.copy(),
              gcol=i["L3_attn_Wg"], grow=np.broadcast_to(i["L3_attn_Wg"], (D, 128)), bg=rep(i["L3_attn_bg"]))
    w3["bk"][DH::32, :] = 1.0
    w3f = {}
    for l in range(DEPTH):
        p = lambda n: i["L3_ffn_" + n][l]
        tail = lambda a: np.concatenate([a, np.zeros((384 - HIDL, *a.shape[1:]), a.dtype)])
        w3f |= {f"qkv{l}": p("wqkv"), f"qs{l}": np.tile(p("q_scale"), 2)[:, None], f"ks{l}": np.tile(p("k_scale"), 2)[:, None],
                f"o{l}": side(p("wo").reshape(NT, 128, D)), f"lg{l}": p("ln_g")[:, None], f"lb{l}": p("ln_b")[:, None],
                f"wa{l}": p("w1")[:, :HIDL], f"wg{l}": p("w1")[:, HIDL:], f"ba{l}": cols(tail(p("b1")[:HIDL])),
                f"bgl{l}": cols(tail(p("b1")[HIDL:])), f"w2{l}": side(tail(p("w2")).reshape(3, 128, D)), f"b2{l}": p("b2")[:, None]}
    return dict(x=i["L0_attn_x"].reshape(-1, D), consts=constants(), w0=pack(W0, w0), w1=pack(W1, w1), w2=pack(W2, w2), w2f=w2f,
                w3=pack(W3, w3), w3f=pack(W3F, w3f))


LAYERS = 4


def kernel(**inputs):
    import concourse.bacc as _bacc
    from concourse.bass_utils import run_bass_kernel_spmd as _run

    nc = _bacc.Bacc("TRN2", target_bir_lowering=False, num_devices=1)
    i = {n: np.asarray(a) for n, a in inputs.items()}
    shape = i["L0_attn_x"].shape
    arrays, args = {}, []
    for name, a in layouts(i).items():
        a = np.ascontiguousarray(a)
        arrays[f"in_{name}_dram"] = a
        args.append(nc.dram_tensor(f"in_{name}_dram", a.shape, mybir.dt.from_np(a.dtype), kind="ExternalInput").ap())
    out = nc.dram_tensor("out_0_dram", (shape[0] * shape[1], D), F32, kind="ExternalOutput").ap()
    network(nc, *args, out, LAYERS)
    r = _run(nc, [arrays], core_ids=[0])
    return r.results[0]["out_0_dram"].reshape(shape)
```

```python
import concourse.bass as bass
from concourse import mybir
from contextlib import ExitStack
from collections import namedtuple
import numpy as np

F32 = mybir.dt.float32
BF16 = mybir.dt.bfloat16
ALU = mybir.AluOpType
ACT = mybir.ActivationFunctionType
AX = mybir.AxisListType

D = 128
SEQ = 256
NB = 2
T = NB * SEQ
TT = T // 128
NH, DH = 16, 8
NG = 4
E1 = 8
E2, HID2 = 16, 512
DI, NS, DTR, TAPS = 256, 16, 8, 4
DEPTH, LH, LD, WIN = 2, 8, 64, 64
LI = LH * LD
HIDL = int(D * 4 * 2 / 3)
BIG = 3.0e38
EXP_LN = "natural_log_exp_and_others"
LN = "natural_log"
PEN_SCALE = 1.0e16
NORM_SCALE = float(2 ** 16)


def record(**fields):
    return namedtuple("Record", list(fields))(**fields)


def columns(parts):
    at, out = 0, {}
    for name, width in parts:
        out[name] = (at, width)
        at += width
    return out, at


CONSTS = [("ident", 128), ("mean", 128), ("ones", 128), ("before", 128), ("sumsel", 128), ("bd8", 128), ("bd64", 128),
          ("unpad", 4 * 128), ("decrow", SEQ), ("dectok", 2), ("rank8", E1), ("rank16", E2),
          ("dist", 2 * SEQ), ("qcos", SEQ), ("qsin", SEQ), ("kcos", SEQ), ("ksin", SEQ), ("rot", 128),
          ("window", 4 * 128), ("eps", 1), ("one", 1), ("kone", 1), ("aeps", 1), ("pow", 1), ("lnpen", 1), ("lnnorm", 1)]
W0 = [("q", 512), ("k", 512), ("v", 128), ("out", 512), ("w1", 1024), ("w2", 1024), ("win", 64), ("w1c", 8),
      ("b1c", 8), ("binc", 8), ("w2c", 8), ("woutm", 128), ("b2m", 1), ("bout", 1)]
W1 = [("q", 128), ("kv", 256), ("o", 128), ("bq", 1), ("bkv", 256), ("bo", 1), ("s", E1), ("bs", E1),
      ("w1", E1 * 128), ("b1", E1), ("w2", E1 * 128), ("b2", 128)]
W2 = [("g", 1), ("b", 1), ("win", 2 * 2 * 128), ("conv", 2 * TAPS), ("cb", 2), ("xp", 2 * (DTR + 2 * NS)), ("dt", DI),
      ("dtb", 2), ("alog", 2 * NS), ("dskip", 2), ("out", 2 * 128), ("r", E2), ("br", E2), ("b1", E2 * 4), ("b2", E2)]
W2F = [("w1", E2 * HID2), ("w2", E2 * 4 * 128)]
W3 = [("q", 512), ("k", 512), ("v", 128), ("bq", 4), ("bk", 4), ("bv", 128), ("gcol", 1), ("grow", 128), ("bg", 1)]
W3F_LAYER = [("qkv", 3 * LI), ("qs", 1), ("ks", 1), ("o", 4 * 128), ("lg", 1), ("lb", 1), ("wa", HIDL), ("wg", HIDL),
       ("ba", 3), ("bgl", 3), ("w2", 3 * 128), ("b2", 1)]
W3F = [(f"{n}{l}", w) for l in range(DEPTH) for n, w in W3F_LAYER]


def view(tensor, parts):
    at, _ = columns(parts)
    return record(**{n: tensor[:, a:a + w] for n, (a, w) in at.items()})


class Link:

    def __init__(self, eng, sem):
        self.eng, self.sem, self.n = eng, sem, 0

    def __call__(self, ins):
        self.n += 1
        ins.then_inc(self.sem, 1)
        self.eng.wait_ge(self.sem, self.n)
        return ins


def semaphores(nc, ctx, names):
    return record(**{n: ctx.enter_context(nc.semaphore(n)) for n in names.split()})


def buffers(nc, ctx, tag, **shapes):
    return record(**{n: ctx.enter_context(nc.sbuf_tensor(f"{tag}_{n}", [128, *s[:-1]] if s[-1] is BF16 else [128, *s],
                                                                  BF16 if s[-1] is BF16 else F32))
                              for n, s in shapes.items()})


def clear(nc, s):
    nums = sorted({x.num for x in s})
    start = nums[0]
    for a, b in zip(nums, nums[1:] + [None]):
        if b != a + 1:
            nc.gpsimd.sem_clear(range(start, a + 1))
            start = b
    nc.all_engine_barrier(sem_only=True)


LN_SEMS = "ln_mean ln_centred ln_square ln_var ln_rstd xn_ready "
GATE_SEMS = "gate_log gate_arg gate_sigmoid "
LINKS = "act_link dve_link pool_link "


def ln_tensor(nc, pe, s, c, src, PB, n=0):
    nc.tensor.matmul(PB[:, 0, :], c.mean, src, start=True, stop=True).then_inc(s.ln_mean, 1)
    pe.wait_ge(s.ln_square, n + 1)
    nc.tensor.matmul(PB[:, 1, :], c.mean, c.lnsq[:], start=True, stop=True).then_inc(s.ln_var, 1)


def ln_scalar(nc, act, s, c, PB, link, n=0):
    act.wait_ge(s.ln_centred, n + 1)
    nc.scalar.activation(c.lnsq[:], c.lnc[:], ACT.Square).then_inc(s.ln_square, 1)
    act.wait_ge(s.ln_var, n + 1)
    link(nc.scalar.activation(c.lnr[:], PB[:, 1, :], ACT.Ln, bias=c.eps))
    nc.scalar.activation(c.lnr[:], c.lnr[:], ACT.Exp, scale=-0.5).then_inc(s.ln_rstd, 1)


def ln_vector(nc, dve, s, c, src, dst, PB, link, n=0):
    dve.wait_ge(s.ln_mean, n + 1)
    nc.vector.tensor_tensor(c.lnc[:], src, PB[:, 0, :], ALU.subtract).then_inc(s.ln_centred, 1)
    dve.wait_ge(s.ln_centred, n + 1)
    dve.wait_ge(s.ln_rstd, n + 1)
    link(nc.vector.tensor_tensor(c.lnt[:], c.lnr[:], c.lnr[:], ALU.mult))
    link(nc.vector.scalar_tensor_tensor(out=c.lnt[:], in0=PB[:, 1, :], scalar=c.eps, in1=c.lnt[:], op0=ALU.add, op1=ALU.mult))
    link(nc.vector.scalar_tensor_tensor(out=c.lnt[:], in0=c.lnt[:], scalar=-3.0, in1=c.lnr[:], op0=ALU.add, op1=ALU.mult))
    return nc.vector.scalar_tensor_tensor(out=dst, in0=c.lnc[:], scalar=-0.5, in1=c.lnt[:], op0=ALU.mult, op1=ALU.mult)


def divide(nc, dst, num, den, recip, tmp, link):
    link(nc.vector.tensor_tensor(tmp, den, recip, ALU.mult))
    link(nc.vector.scalar_tensor_tensor(out=tmp, in0=tmp, scalar=-2.0, in1=recip, op0=ALU.add, op1=ALU.mult))
    return nc.vector.scalar_tensor_tensor(out=dst, in0=num, scalar=-1.0, in1=tmp, op0=ALU.mult, op1=ALU.mult)


def gate_scalar(nc, act, s, c, link):
    link(nc.scalar.activation(c.ga[:], c.Y[:], ACT.Abs))
    link(nc.scalar.activation(c.ga[:], c.ga[:], ACT.Exp, scale=-1.0))
    nc.scalar.activation(c.ga[:], c.ga[:], ACT.Ln, bias=c.one).then_inc(s.gate_log, 1)
    act.wait_ge(s.gate_arg, 1)
    nc.scalar.activation(c.gb[:], c.gb[:], ACT.Exp).then_inc(s.gate_sigmoid, 1)


def gate_vector(nc, dve, s, c, link):
    dve.wait_ge(s.gate_log, 1)
    nc.vector.scalar_tensor_tensor(out=c.gb[:], in0=c.Y[:], scalar=0.0, in1=c.ga[:],
                                   op0=ALU.min, op1=ALU.subtract).then_inc(s.gate_arg, 1)
    link(nc.vector.tensor_tensor(c.lnc[:], c.S[:], c.Y[:], ALU.mult))
    dve.wait_ge(s.gate_sigmoid, 1)
    link(nc.vector.tensor_tensor(c.lnc[:], c.lnc[:], c.gb[:], ALU.mult))
    link(nc.vector.tensor_tensor(c.X[:], c.X[:], c.lnc[:], ALU.add))


ATT_SEMS = ("scores_read q_ready k_ready v_ready q_copied k_copied v_copied scores_ready scores_masked max_taken exp_done "
            "probT_ready probT_copied ctx_ready ctx_copied den_ready den_logged den_taken recip_ready "
            "ctx_scaled att_ready att_done zeroed ")
UNITS = NH * NB
GU = UNITS // NG
LAG_T, LAG_P, LAG_V, LAG_O, LAG_D = 4, 5, 7, GU + 6, GU + 9
STEPS = UNITS - GU + LAG_D + 1
SBANKS, TBANKS = 4, 2
BUFS = 4
TBUFS = 3


def unit(m):
    return m // GU, m % GU // 4, m % 4


def group_at(i, lag):
    g, r = divmod(i - lag, GU)
    return g if r == 0 and 0 <= g < NG else None


def att_buffers(nc, ctx, tag, **more):
    return buffers(nc, ctx, tag, QP=[NG, T], KP=[NG, T], VT=[TT, NH, 32], MX=[BUFS, 2], PP=[BUFS, 2, SEQ], PT=[BUFS, 2, SEQ],
                   OS=[2, T], LG=[T], RG=[2, T], DT=[T], Z=[NG, T], **more)


def att_tensor(nc, pe, s, c, w, b, PB, w_out, fill=None):
    pe.wait_ge(s.xn_ready, 1)
    for g in range(NG):
        nc.tensor.matmul(PB[:, g, :], w.q[:, g * 128:(g + 1) * 128], c.XN[:], start=True, stop=True).then_inc(s.q_ready, 1)
    for g in range(NG):
        nc.tensor.matmul(PB[:, 4 + g, :], w.k[:, g * 128:(g + 1) * 128], c.XN[:], start=True, stop=True).then_inc(s.k_ready, 1)
    pe.wait_ge(s.q_copied, 1)
    for t in range(TT):
        last = nc.tensor.matmul(PB[:, 0, t * 128:(t + 1) * 128], c.XN[:, t * 128:(t + 1) * 128], w.v,
                                start=True, stop=True)
    last.then_inc(s.v_ready, 1)
    pe.wait_ge(s.q_copied, NG)
    pe.wait_ge(s.k_copied, NG)
    pe.wait_ge(s.v_copied, 1)
    for i in range(STEPS):
        if i < UNITS and i % 2 == 0:
            if i + 2 > SBANKS:
                pe.wait_ge(s.scores_read, i + 2 - SBANKS)
            for qt in range(2):
                for u in (i, i + 1):
                    g, sq, j = unit(u)
                    q0 = sq * SEQ + qt * 128
                    last = nc.tensor.matmul(PB[:, u % SBANKS, qt * SEQ:(qt + 1) * SEQ], b.QP[32 * j:32 * j + 32, g, q0:q0 + 128],
                                            b.KP[32 * j:32 * j + 32, g, sq * SEQ:(sq + 1) * SEQ], start=True, stop=True)
            last.then_inc(s.scores_ready, 2)
        m = i - LAG_T
        if 0 <= m < UNITS:
            pe.wait_ge(s.exp_done, m + 1)
            if m >= TBANKS:
                pe.wait_ge(s.probT_copied, m - TBANKS + 1)
            for kt in range(2):
                for qt in range(2):
                    last = nc.tensor.transpose(PB[:, SBANKS + m % TBANKS, kt * SEQ + qt * 128:kt * SEQ + qt * 128 + 128],
                                               b.PP[:, m % BUFS, qt, kt * 128:(kt + 1) * 128], c.ident)
            last.then_inc(s.probT_ready, 1)
        m = i - LAG_V
        if 0 <= m < UNITS and m % 2 == 0:
            pe.wait_ge(s.probT_copied, m + 2)
            if m % GU == 0 and m:
                pe.wait_ge(s.ctx_copied, m // GU)
            for kt in range(2):
                for u in (m, m + 1):
                    g, sq, j = unit(u)
                    last = nc.tensor.matmul(PB[32 * j:32 * j + 32, 7, sq * SEQ:(sq + 1) * SEQ],
                                            b.VT[:, 2 * sq + kt, 4 * g + j, :], b.PT[:, u % BUFS, kt, :],
                                            start=kt == 0, stop=kt == 1, tile_position=(0, 32 * j))
            last.then_inc(s.ctx_ready, 2)
        g = group_at(i, LAG_D)
        if g is not None:
            pe.wait_ge(s.ctx_copied, g + 1)
            if g:
                pe.wait_ge(s.den_taken, g)
            nc.tensor.matmul(PB[:, 6, :], c.sumsel, b.OS[:, g % 2, :], start=True, stop=True).then_inc(s.den_ready, 1)
        if fill and i >= UNITS + LAG_T:
            fill(i - UNITS - LAG_T)
    if fill:
        for k in range(STEPS - UNITS - LAG_T, 9):
            fill(k)
    for g in range(NG):
        pe.wait_ge(s.ctx_scaled, g + 1)
        last = nc.tensor.matmul(PB[:, 0, :], w_out[:, g * 128:(g + 1) * 128], b.Z[:, g, :], start=g == 0, stop=g == NG - 1)
    last.then_inc(s.att_ready, 1)


def att_scalar(nc, act, s, c, b, PB, link, bias, masked, fill=None):
    for g in range(NG):
        act.wait_ge(s.q_ready, g + 1)
        nc.scalar.activation(b.QP[:, g, :], PB[:, g, :], ACT.Identity, scale=float(DH) ** -0.5,
                             bias=bias[:, g:g + 1] if masked else 0.0).then_inc(s.q_copied, 1)
    for i in range(STEPS):
        m = i - LAG_P
        if masked and 0 <= m < UNITS:
            act.wait_ge(s.probT_ready, m + 1)
            if m >= BUFS:
                act.wait_ge(s.ctx_ready, m - BUFS + 1)
            nc.scalar.activation(b.PT[:, m % BUFS].rearrange("p k q -> p (k q)"), PB[:, SBANKS + m % TBANKS, :],
                                 ACT.Copy).then_inc(s.probT_copied, 1)
        if i < UNITS:
            act.wait_ge(s.max_taken, i + 1)
            if i >= BUFS:
                act.wait_ge(s.probT_ready, i - BUFS + 1)
            for qt in range(2):
                src = b.TS[:, i % TBUFS, qt, :] if masked else PB[:, i % SBANKS, qt * SEQ:(qt + 1) * SEQ]
                last = nc.scalar.activation(b.PP[:, i % BUFS, qt, :], src, ACT.Exp, scale=-1.0, bias=b.MX[:, i % BUFS, qt:qt + 1])
            last.then_inc(s.exp_done, 1)
        g = group_at(i, LAG_O)
        if g is not None:
            act.wait_ge(s.ctx_ready, GU * (g + 1))
            if g >= 2:
                act.wait_ge(s.ctx_scaled, g - 1)
            nc.scalar.activation(b.OS[:, g % 2, :], PB[:, 7, :], ACT.Copy).then_inc(s.ctx_copied, 1)
        g = group_at(i, LAG_D)
        if g is not None:
            act.wait_ge(s.den_ready, g + 1)
            nc.scalar.activation(b.LG[:], PB[:, 6, :], ACT.Ln).then_inc(s.den_logged, 1)
            act.wait_ge(s.den_logged, g + 1)
            if g >= 2:
                act.wait_ge(s.ctx_scaled, g - 1)
            nc.scalar.activation(b.RG[:, g % 2, :], b.LG[:], ACT.Exp, scale=-1.0).then_inc(s.recip_ready, 1)
            act.wait_ge(s.recip_ready, g + 1)
        if fill and i >= UNITS + LAG_T:
            fill(i - UNITS - LAG_T)
    if fill:
        for k in range(STEPS - UNITS - LAG_T, 9):
            fill(k)


def att_vector(nc, dve, s, c, w, b, PB, link, masked):
    for g in range(NG):
        dve.wait_ge(s.k_ready, g + 1)
        if masked:
            nc.vector.tensor_scalar(b.KP[:, g, :], PB[:, 4 + g, :], w.bk[:, g:g + 1], -1.0, ALU.add, ALU.mult).then_inc(s.k_copied, 1)
        else:
            nc.vector.tensor_scalar(b.KP[:, g, :], PB[:, 4 + g, :], -1.0, None, ALU.mult).then_inc(s.k_copied, 1)
    dve.wait_ge(s.zeroed, 1)
    dve.wait_ge(s.v_ready, 1)
    vt = b.VT[:].rearrange("p t h c -> p (t h) c")[:, :, 0:DH]
    vp = PB[:, 0, :].rearrange("p (a c) -> p a c", c=DH)
    if masked:
        for t in range(TT):
            last = nc.vector.tensor_tensor(b.VT[:, t, :, 0:DH], PB[:, 0, t * 128:(t + 1) * 128].rearrange("p (h c) -> p h c", c=DH),
                                           w.bv.rearrange("p (h c) -> p h c", c=DH), ALU.add)
        last.then_inc(s.v_copied, 1)
    else:
        nc.vector.tensor_copy(vt, vp).then_inc(s.v_copied, 1)
    if masked:
        dve.wait_ge(s.logpen_ready, 1)
    for i in range(STEPS + 1):
        m = i - LAG_P
        if not masked and 0 <= m < UNITS:
            dve.wait_ge(s.probT_ready, m + 1)
            if m >= BUFS:
                dve.wait_ge(s.ctx_ready, m - BUFS + 1)
            nc.vector.tensor_copy(b.PT[:, m % BUFS].rearrange("p k q -> p (k q)"),
                                  PB[:, SBANKS + m % TBANKS, :]).then_inc(s.probT_copied, 1)
        if i < UNITS:
            g, sq, j = unit(i)
            dve.wait_ge(s.scores_ready, i + 1)
            src = PB[:, i % SBANKS, :].rearrange("p (t k) -> p t k", k=SEQ)
            if masked:
                if i >= TBUFS:
                    dve.wait_ge(s.exp_done, i - TBUFS + 1)
                nc.vector.tensor_tensor(b.TS[:, i % TBUFS], src, b.LP[:, 2 * sq:2 * sq + 2, :], ALU.subtract).then_inc(s.scores_masked, 1)
                dve.wait_ge(s.scores_masked, i + 1)
                src = b.TS[:, i % TBUFS]
            nc.vector.tensor_reduce(b.MX[:, i % BUFS, :], src, AX.X, ALU.min).then_inc(s.max_taken, 1)
        g = group_at(i, LAG_D + 1)
        if g is not None:
            dve.wait_ge(s.recip_ready, g + 1)
            r, dt = b.RG[:, g % 2, :], b.DT[:]
            nc.vector.tensor_tensor(dt, PB[:, 6, :], r, ALU.mult).then_inc(s.den_taken, 1)
            dve.wait_ge(s.den_taken, g + 1)
            link(nc.vector.scalar_tensor_tensor(out=dt, in0=dt, scalar=-2.0, in1=r, op0=ALU.add, op1=ALU.mult))
            nc.vector.scalar_tensor_tensor(out=b.Z[:, g, :], in0=b.OS[:, g % 2, :], scalar=-1.0, in1=dt,
                                           op0=ALU.mult, op1=ALU.mult).then_inc(s.ctx_scaled, 1)
            dve.wait_ge(s.ctx_scaled, g + 1)


def att_gpsimd(nc, pool, s, b, link):
    link(nc.gpsimd.memset(b.VT[:], 0.0))
    nc.gpsimd.memset(b.VT[:, :, :, DH:DH + 1].rearrange("p t h c -> p (t h) c"), 1.0).then_inc(s.zeroed, 1)


L0_SEMS = LN_SEMS + ATT_SEMS + GATE_SEMS + LINKS + "hid_ready hid_done ffn_ready y_ready "


def layer0(nc, c, w, PB):
    with ExitStack() as ctx:
        s = semaphores(nc, ctx, L0_SEMS)
        s = s._replace(scores_read=s.exp_done)
        b = att_buffers(nc, ctx, "l0", H=[2, T])
        with nc.Block() as block:
            @block.tensor
            def _(pe):
                ln_tensor(nc, pe, s, c, c.X[:], PB)

                def hidden_layer(i):
                    if i > 8:
                        return
                    if i < 8:
                        if i >= 2:
                            pe.wait_ge(s.hid_done, i - 1)
                        else:
                            pe.wait_ge(s.exp_done, UNITS)
                        nc.tensor.matmul(PB[:, 2 + i % 2, :], w.w1[:, i * 128:(i + 1) * 128], c.XN[:],
                                         start=True, stop=True).then_inc(s.hid_ready, 1)
                    if i:
                        pe.wait_ge(s.hid_done, i)
                        nc.tensor.matmul(PB[:, 1, :], w.w2[:, (i - 1) * 128:i * 128], b.H[:, (i - 1) % 2, :],
                                         start=i == 1, stop=i == 8).then_inc(s.ffn_ready, 1)

                att_tensor(nc, pe, s, c, w, b, PB, w.out, hidden_layer)

            @block.scalar
            def _(act):
                link = Link(act, s.act_link)
                act.preload_act_table_set(EXP_LN)
                ln_scalar(nc, act, s, c, PB, link)

                def hidden_layer(i):
                    if i < 8:
                        act.wait_ge(s.hid_ready, i + 1)
                        if i >= 2:
                            act.wait_ge(s.ffn_ready, i - 1)
                        nc.scalar.activation(b.H[:, i % 2, :], PB[:, 2 + i % 2, :], ACT.Relu, bias=w.b1c[:, i:i + 1]).then_inc(s.hid_done, 1)

                att_scalar(nc, act, s, c, b, PB, link, None, False, hidden_layer)
                act.wait_ge(s.y_ready, 1)
                gate_scalar(nc, act, s, c, link)

            @block.vector
            def _(dve):
                link = Link(dve, s.dve_link)
                ln_vector(nc, dve, s, c, c.X[:], c.XN[:], PB, link).then_inc(s.xn_ready, 1)
                att_vector(nc, dve, s, c, w, b, PB, link, False)
                dve.wait_ge(s.att_ready, 1)
                dve.wait_ge(s.xn_ready, 1)
                link(nc.vector.tensor_tensor(c.S[:], PB[:, 0, :], c.XN[:], ALU.add))
                dve.wait_ge(s.ffn_ready, 8)
                nc.vector.tensor_scalar(c.Y[:], PB[:, 1, :], w.bout, None, ALU.add).then_inc(s.y_ready, 1)
                dve.wait_ge(s.y_ready, 1)
                gate_vector(nc, dve, s, c, link)

            @block.gpsimd
            def _(pool):
                att_gpsimd(nc, pool, s, b, Link(pool, s.pool_link))
        clear(nc, s)


L1_SEMS = (LN_SEMS + LINKS + "q_ready qf_relu qf_ready kv_ready kv_biased kf_ready kvsum_ready "
           "kvsum_masked num_ready den_ready recip_ready ctx_scaled att_ready att_done ones_set "
           "logits_ready logits_shifted route_exp pmax_ready route_ready pmaxT_ready routeT_ready xp_ready "
           "routeT_copied keep_ready hid_ready hid_done ffn_ready y_ready count_ready count_taken yT_ready saved ")


def layer1(nc, c, w, r, it, x_mid, s_mid, PB):
    with ExitStack() as ctx:
        s = semaphores(nc, ctx, L1_SEMS)
        b = buffers(nc, ctx, "l1", QF=[T], KV=[TT, 257], KM=[NB, 128], KS=[NB, 128], RG=[T], LG=[T], CT=[T], DN=[T],
                    LO=[TT, E1], EX=[TT, E1], OH=[TT, E1], WK=[TT, E1], M1=[TT], SM=[TT], PX=[TT, 128],
                    XP=[T], OT=[T], PEN=[T, BF16], H=[2, T])
        with nc.Block() as block:
            @block.tensor
            def _(pe):
                ln_tensor(nc, pe, s, c, c.X[:], PB)
                pe.wait_ge(s.xn_ready, 1)
                for t in range(TT):
                    last = nc.tensor.matmul(PB[:, 0, t * E1:(t + 1) * E1], c.XN[:, t * 128:(t + 1) * 128], w.s,
                                            start=True, stop=True)
                last.then_inc(s.logits_ready, 1)
                for t in range(TT):
                    last = nc.tensor.matmul(PB[:, 2 + t // 2, t % 2 * 256:t % 2 * 256 + 256],
                                            c.XN[:, t * 128:(t + 1) * 128], w.kv, start=True, stop=True)
                last.then_inc(s.kv_ready, 1)
                nc.tensor.matmul(PB[:, 1, :], w.q, c.XN[:], start=True, stop=True).then_inc(s.q_ready, 1)
                pe.wait_ge(s.kf_ready, 1)
                for sq in range(NB):
                    for t in range(2):
                        last = nc.tensor.matmul(PB[:, 4 + sq, 0:129], b.KV[:, 2 * sq + t, 0:128], b.KV[:, 2 * sq + t, 128:257],
                                                start=t == 0, stop=t == 1)
                last.then_inc(s.kvsum_ready, 1)
                pe.wait_ge(s.pmax_ready, 1)
                pe.wait_ge(s.route_ready, 1)
                for t in range(TT):
                    last = nc.tensor.transpose(PB[:, 0, t * 128:(t + 1) * 128], b.PX[:, t, :], c.ident)
                last.then_inc(s.pmaxT_ready, 1)
                for t in range(TT):
                    last = nc.tensor.transpose(PB[0:E1, 2, t * 128:(t + 1) * 128], b.OH[:, t, :], c.ident)
                last.then_inc(s.routeT_ready, 1)
                pe.wait_ge(s.qf_relu, 1)
                for t in range(TT):
                    o = PB[:, 1, t * E1:(t + 1) * E1]
                    nc.tensor.matmul(o, c.before, b.OH[:, t, :], start=True, stop=t == 0)
                    for u in range(t):
                        nc.tensor.matmul(o, c.ones, b.OH[:, u, :], start=False, stop=u == t - 1)
                for t in range(TT):
                    last = nc.tensor.matmul(PB[:, 1, TT * E1:TT * E1 + E1], c.ones, b.OH[:, t, :], start=t == 0, stop=t == TT - 1)
                last.then_inc(s.count_ready, 1)
                pe.wait_ge(s.kvsum_masked, 1)
                pe.wait_ge(s.qf_ready, 1)
                for sq in range(NB):
                    last = nc.tensor.matmul(PB[:, 6, sq * SEQ:(sq + 1) * SEQ], b.KM[:, sq, :], b.QF[:, sq * SEQ:(sq + 1) * SEQ],
                                            start=True, stop=True)
                last.then_inc(s.num_ready, 1)
                for sq in range(NB):
                    last = nc.tensor.matmul(PB[:, 7, sq * SEQ:(sq + 1) * SEQ], b.KS[:, sq, :], b.QF[:, sq * SEQ:(sq + 1) * SEQ],
                                            start=True, stop=True)
                last.then_inc(s.den_ready, 1)
                pe.wait_ge(s.xp_ready, 1)
                pe.wait_ge(s.keep_ready, 1)
                for e in range(E1 + 1):
                    if e < E1:
                        if e >= 2:
                            pe.wait_ge(s.hid_done, e - 1)
                        nc.tensor.matmul(PB[:, 4 + e % 2, :], w.w1[:, e * 128:(e + 1) * 128], b.XP[:], start=True, stop=False)
                        nc.tensor.matmul(PB[:, 4 + e % 2, :], c.identb[0:E1, e:e + 1].broadcast_to([E1, 128]), b.PEN[0:E1, :],
                                         start=False, stop=True).then_inc(s.hid_ready, 1)
                    if e:
                        pe.wait_ge(s.hid_done, e)
                        nc.tensor.matmul(PB[:, 3, :], w.w2[:, (e - 1) * 128:e * 128], b.H[:, (e - 1) % 2, :],
                                         start=e == 1, stop=False).then_inc(s.ffn_ready, 1)
                nc.tensor.matmul(PB[:, 3, :], w.b2[0:E1, :], b.OT[0:E1, :], start=False, stop=True).then_inc(s.ffn_ready, 1)
                pe.wait_ge(s.ctx_scaled, 1)
                pe.wait_ge(s.count_taken, 1)
                nc.tensor.matmul(PB[:, 1, :], w.o, b.CT[:], start=True, stop=True).then_inc(s.att_ready, 1)
                pe.wait_ge(s.y_ready, 1)
                for t in range(TT):
                    last = nc.tensor.transpose(PB[:, 0, t * 128:(t + 1) * 128], c.Y[:, t * 128:(t + 1) * 128], c.ident)
                last.then_inc(s.yT_ready, 1)

            @block.scalar
            def _(act):
                link = Link(act, s.act_link)
                act.preload_act_table_set(EXP_LN)
                ln_scalar(nc, act, s, c, PB, link)
                act.wait_ge(s.logits_shifted, 1)
                nc.scalar.activation(b.EX[:], b.LO[:], ACT.Exp).then_inc(s.route_exp, 1)
                act.wait_ge(s.q_ready, 1)
                nc.scalar.activation(b.QF[:], PB[:, 1, :], ACT.Relu, bias=w.bq).then_inc(s.qf_relu, 1)
                act.wait_ge(s.routeT_ready, 1)
                nc.scalar.activation(b.OT[0:E1, :], PB[0:E1, 2, :], ACT.Copy).then_inc(s.routeT_copied, 1)
                act.wait_ge(s.den_ready, 1)
                link(nc.scalar.activation(b.LG[:], PB[:, 7, :], ACT.Ln, bias=c.aeps))
                nc.scalar.activation(b.RG[:], b.LG[:], ACT.Exp, scale=-1.0).then_inc(s.recip_ready, 1)
                for e in range(E1):
                    act.wait_ge(s.hid_ready, e + 1)
                    if e >= 2:
                        act.wait_ge(s.ffn_ready, e - 1)
                    nc.scalar.activation(b.H[:, e % 2, :], PB[:, 4 + e % 2, :], ACT.Relu, bias=w.b1[:, e:e + 1]).then_inc(s.hid_done, 1)

            @block.vector
            def _(dve):
                link = Link(dve, s.dve_link)
                ln_vector(nc, dve, s, c, c.X[:], c.XN[:], PB, link).then_inc(s.xn_ready, 1)
                dve.wait_ge(s.logits_ready, 1)
                link(nc.vector.tensor_tensor(b.LO[:], PB[:, 0, 0:TT * E1].rearrange("p (t e) -> p t e", e=E1),
                                             w.bs.unsqueeze(1).broadcast_to([128, TT, E1]), ALU.add))
                link(nc.vector.tensor_reduce(b.M1[:], b.LO[:], AX.X, ALU.max))
                nc.vector.tensor_tensor(b.LO[:], b.LO[:], b.M1[:].unsqueeze(2).broadcast_to([128, TT, E1]),
                                        ALU.subtract).then_inc(s.logits_shifted, 1)
                dve.wait_ge(s.logits_shifted, 1)
                link(nc.vector.tensor_scalar(b.OH[:], b.LO[:], 0.0, None, ALU.is_equal))
                link(nc.vector.tensor_tensor(b.WK[:], b.OH[:], c.rank8.unsqueeze(1).broadcast_to([128, TT, E1]), ALU.mult))
                link(nc.vector.tensor_reduce(b.M1[:], b.WK[:], AX.X, ALU.max))
                nc.vector.tensor_tensor(b.OH[:], b.WK[:], b.M1[:].unsqueeze(2).broadcast_to([128, TT, E1]),
                                        ALU.is_equal).then_inc(s.route_ready, 1)
                dve.wait_ge(s.kv_ready, 1)
                dve.wait_ge(s.ones_set, 1)
                link(nc.vector.tensor_tensor(b.KV[:, :, 0:256], PB[:, 2:4, :].rearrange("p a (t k) -> p (a t) k", k=256),
                                             w.bkv.unsqueeze(1).broadcast_to([128, TT, 256]), ALU.add))
                for par in range(2):
                    last = nc.vector.tensor_scalar(b.KV[:, par:TT:2, 0:128], b.KV[:, par:TT:2, 0:128], 0.0,
                                                   c.dectok[:, par:par + 1], ALU.max, ALU.mult)
                last.then_inc(s.kf_ready, 1)
                dve.wait_ge(s.route_exp, 1)
                link(nc.vector.tensor_reduce(b.SM[:], b.EX[:], AX.X, ALU.add))
                link(nc.vector.reciprocal(b.SM[:], b.SM[:]))
                nc.vector.tensor_copy(b.PX[:], b.SM[:].unsqueeze(2).broadcast_to([128, TT, 128])).then_inc(s.pmax_ready, 1)
                dve.wait_ge(s.kvsum_ready, 1)
                for sq in range(NB):
                    nc.vector.tensor_tensor(b.KM[:, sq, :], PB[:, 4 + sq, 0:128], c.bd8, ALU.mult)
                    last = nc.vector.tensor_scalar(b.KS[:, sq, :], c.bd8, PB[:, 4 + sq, 128:129], None, ALU.mult)
                last.then_inc(s.kvsum_masked, 1)
                dve.wait_ge(s.pmaxT_ready, 1)
                nc.vector.tensor_tensor(b.XP[:], c.XN[:], PB[:, 0, :], ALU.mult).then_inc(s.xp_ready, 1)
                dve.wait_ge(s.routeT_copied, 1)
                nc.vector.tensor_scalar(b.PEN[0:E1, :], b.OT[0:E1, :], -1.0, BIG, ALU.add, ALU.mult).then_inc(s.keep_ready, 1)
                dve.wait_ge(s.count_ready, 1)
                link(nc.vector.tensor_tensor(b.WK[:], PB[:, 1, 0:TT * E1].rearrange("p (t e) -> p t e", e=E1),
                                             r.base[:].unsqueeze(1).broadcast_to([128, TT, E1]), ALU.add))
                nc.vector.tensor_tensor(r.base[:], r.base[:], PB[:, 1, TT * E1:TT * E1 + E1], ALU.add).then_inc(s.count_taken, 1)
                link(nc.vector.tensor_tensor(b.WK[:], b.WK[:], b.OH[:], ALU.mult))
                nc.vector.tensor_reduce(r.rank[:, bass.ts(it, TT)], b.WK[:], AX.X, ALU.add)
                nc.vector.tensor_copy(r.route[:, bass.ts(it, TT), :], b.OH[:])
                dve.wait_ge(s.recip_ready, 1)
                dve.wait_ge(s.num_ready, 1)
                link(nc.vector.tensor_scalar(b.DN[:], PB[:, 7, :], c.aeps, None, ALU.add))
                divide(nc, b.CT[:], PB[:, 6, :], b.DN[:], b.RG[:], b.LG[:], link).then_inc(s.ctx_scaled, 1)
                dve.wait_ge(s.att_ready, 1)
                dve.wait_ge(s.ffn_ready, E1 + 1)
                nc.vector.tensor_copy(c.Y[:], PB[:, 3, :]).then_inc(s.y_ready, 1)
                nc.vector.tensor_scalar(c.S[:], PB[:, 1, :], w.bo, None, ALU.add).then_inc(s.att_done, 1)
                dve.wait_ge(s.yT_ready, 1)
                nc.vector.tensor_copy(r.y[:, bass.ts(it, TT), :], PB[:, 0, :].rearrange("p (t d) -> p t d", d=D))

            @block.sync
            def _(sp):
                sp.dma_start(x_mid[bass.ts(it, 128), :], c.X[:]).then_inc(s.saved, 16)
                sp.wait_ge(s.att_done, 1)
                sp.dma_start(s_mid[bass.ts(it, 128), :], c.S[:]).then_inc(s.saved, 16)
                sp.wait_ge(s.saved, 32)

            @block.gpsimd
            def _(pool):
                nc.gpsimd.memset(b.KV[:, :, 256:257].rearrange("p t o -> p (t o)"), 1.0).then_inc(s.ones_set, 1)
                pool.wait_ge(s.qf_relu, 1)
                nc.gpsimd.tensor_tensor(b.QF[:].rearrange("p (s n) -> p s n", n=SEQ), b.QF[:].rearrange("p (s n) -> p s n", n=SEQ),
                                        c.decrow.unsqueeze(1).broadcast_to([128, NB, SEQ]), ALU.mult).then_inc(s.qf_ready, 1)
        clear(nc, s)


def place_tokens(nc, r, tiles, y_mid):
    with ExitStack() as ctx:
        s = semaphores(nc, ctx, "dve_link places_ready scattered")
        off = ctx.enter_context(nc.sbuf_tensor("off", [128, E1], F32))
        pos = ctx.enter_context(nc.sbuf_tensor("pos", [128, tiles], F32))
        idx = ctx.enter_context(nc.sbuf_tensor("idx", [128, tiles], mybir.dt.int32))
        with nc.Block() as block:
            @block.vector
            def _(dve):
                link = Link(dve, s.dve_link)
                link(nc.vector.memset(off[:, 0:1], 0.0))
                for e in range(1, E1):
                    link(nc.vector.tensor_tensor(off[:, e:e + 1], off[:, e - 1:e], r.base[:, e - 1:e], ALU.add))
                link(nc.vector.tensor_tensor(r.route[:], r.route[:], off[:].unsqueeze(1).broadcast_to([128, tiles, E1]), ALU.mult))
                link(nc.vector.tensor_reduce(pos[:], r.route[:], AX.X, ALU.add))
                nc.vector.tensor_tensor(idx[:], pos[:], r.rank[:], ALU.add).then_inc(s.places_ready, 1)

            @block.gpsimd
            def _(pool):
                pool.wait_ge(s.places_ready, 1)
                for t in range(tiles):
                    pool.indirect_dma_start(out=y_mid, out_offset=bass.IndirectOffsetOnAxis(ap=idx[:, t:t + 1], axis=0),
                                            in_=r.y[:, t, :], in_offset=None).then_inc(s.scattered, 16)
                pool.wait_ge(s.scattered, 16 * tiles)
        clear(nc, s)


L2_SEMS = (LN_SEMS + GATE_SEMS + LINKS + "ln_reused xm_ready xz_ready xi_copied conv_done silu_x silu_z xd_ready dtl_copied "
           "bc_copied dt_ready dt_raw dt_exp dt_u dt_log delta_ready decay_ready b_ready c_ready drive_ready "
           "c_copied state_ready part_ready y_summed y_gated mamba_ready pads_set "
           "logits_ready logits_shifted route_exp gates_ready gate_spread gateT_ready w2_loaded0 w2_loaded1 hid_ready "
           "hid_even hid_odd ffn_ready bank_done weighted acc_done ")
HID_BANKS = (2, 3, 7)
HTILES = HID2 // 128


def layer2(nc, c, w, wf, PB):
    with ExitStack() as ctx:
        s = semaphores(nc, ctx, L2_SEMS)
        b = buffers(nc, ctx, "l2", XM=[T], XI=[2, NB, TAPS - 1 + SEQ], XC=[2, T], ZS=[2, T], DL=[2, T], DU=[2, T],
                    EE=[2, T], UU=[2, T], DTL=[T], BC=[T], CN=[2, T], DA=[2, 2, T], DB=[2, 2, T], ST=[2, 2, T],
                    CH=[2, T], YA=[2, T], H=[4, T], YB=[2, T], GS=[2, TT, 128], WB=[2, 2 * HID2],
                    LO=[TT, E2], EX=[TT, E2], OA=[TT, E2], OB=[TT, E2], WK=[TT, E2], M1=[TT], SM=[TT])
        loaded = (s.w2_loaded0, s.w2_loaded1)

        def hid_wait(eng, k):
            if k % 2:
                eng.wait_ge(s.hid_odd, (k + 1) // 2)
            else:
                eng.wait_ge(s.hid_even, k // 2 + 1)

        with nc.Block() as block:
            @block.sync
            def _(sp):
                for e in range(E2):
                    if e >= 2:
                        sp.wait_ge(s.ffn_ready, HTILES * (e - 1))
                    sp.dma_start(b.WB[:, e % 2, :], wf[e, :, :]).then_inc(loaded[e % 2], 16)

            @block.tensor
            def _(pe):
                ln_tensor(nc, pe, s, c, c.X[:], PB)
                pe.wait_ge(s.xn_ready, 1)
                ln_tensor(nc, pe, s, c, c.XN[:], PB, 1)
                for t in range(TT):
                    last = nc.tensor.matmul(PB[:, 4, t * E2:(t + 1) * E2], c.XN[:, t * 128:(t + 1) * 128], w.r,
                                            start=True, stop=True)
                last.then_inc(s.logits_ready, 1)
                pe.wait_ge(s.xm_ready, 1)
                for k in range(4):
                    nc.tensor.matmul(PB[:, k, :], w.win[:, k * 128:(k + 1) * 128], b.XM[:], start=True, stop=True).then_inc(s.xz_ready, 1)
                pe.wait_ge(s.silu_x, 2)
                for k in range(2):
                    last = nc.tensor.matmul(PB[0:DTR, 5, :], w.xp[:, k * 40:k * 40 + DTR], b.XC[:, k, :], start=k == 0, stop=k == 1)
                for k in range(2):
                    last = nc.tensor.matmul(PB[0:32, 6, :], w.xp[:, k * 40 + DTR:k * 40 + 40], b.XC[:, k, :], start=k == 0, stop=k == 1)
                last.then_inc(s.xd_ready, 1)
                pe.wait_ge(s.dtl_copied, 1)
                pe.wait_ge(s.xi_copied, 1)
                pe.wait_ge(s.silu_z, 2)
                for k in range(2):
                    last = nc.tensor.matmul(PB[:, k, :], w.dt[0:DTR, k * 128:(k + 1) * 128], b.DTL[0:DTR, :], start=True, stop=True)
                last.then_inc(s.dt_ready, 1)
                pe.wait_ge(s.bc_copied, 1)
                pe.wait_ge(s.dt_raw, 1)
                pe.wait_ge(s.gates_ready, 1)
                for n in range(NS):
                    if n:
                        pe.wait_ge(s.drive_ready, n)
                    nc.tensor.matmul(PB[:, 0, :], c.ident[0:32, n:n + 1].broadcast_to([32, 128]),
                                     b.BC[0:32, :], start=True, stop=True).then_inc(s.b_ready, 1)
                    if n:
                        pe.wait_ge(s.c_copied, n)
                    nc.tensor.matmul(PB[:, 1, :], c.ident[0:32, NS + n:NS + n + 1].broadcast_to([32, 128]),
                                     b.BC[0:32, :], start=True, stop=True).then_inc(s.c_ready, 1)
                    for i in range(HTILES + 2):
                        if i < HTILES:
                            k = HTILES * n + i
                            if i == 0:
                                pe.wait_ge(loaded[n % 2], 16 * (n // 2 + 1))
                            if k >= 3:
                                hid_wait(pe, k - 3)
                            nc.tensor.matmul(PB[:, HID_BANKS[k % 3], :], b.WB[:, n % 2, i * 128:(i + 1) * 128], c.XN[:],
                                             start=True, stop=True).then_inc(s.hid_ready, 1)
                        if i >= 2:
                            k = HTILES * n + i - 2
                            hid_wait(pe, k)
                            if i == 2 and n >= 2:
                                pe.wait_ge(s.bank_done, n - 1)
                            nc.tensor.matmul(PB[:, 4 + n % 2, :], b.WB[:, n % 2, HID2 + (i - 2) * 128:HID2 + (i - 1) * 128],
                                             b.H[:, k % 4, :], start=i == 2, stop=i == HTILES + 1).then_inc(s.ffn_ready, 1)
                    pe.wait_ge(s.gate_spread, n + 1)
                    if n:
                        pe.wait_ge(s.weighted, n)
                    for t in range(TT):
                        last = nc.tensor.transpose(PB[:, 6, t * 128:(t + 1) * 128], b.GS[:, n % 2, t, :], c.ident)
                    last.then_inc(s.gateT_ready, 1)
                pe.wait_ge(s.y_gated, 1)
                for k in range(2):
                    last = nc.tensor.matmul(PB[:, 0, :], w.out[:, k * 128:(k + 1) * 128], b.EE[:, k, :], start=k == 0, stop=k == 1)
                last.then_inc(s.mamba_ready, 1)

            @block.scalar
            def _(act):
                link = Link(act, s.act_link)
                act.preload_act_table_set(EXP_LN)
                ln_scalar(nc, act, s, c, PB, link)
                ln_scalar(nc, act, s, c, PB, link, 1)
                act.wait_ge(s.logits_shifted, 1)
                nc.scalar.activation(b.EX[:], b.LO[:], ACT.Exp).then_inc(s.route_exp, 1)
                for k in range(2):
                    act.wait_ge(s.xz_ready, 3 + k)
                    nc.scalar.activation(b.ZS[:, k, :], PB[:, 2 + k, :], ACT.Silu).then_inc(s.silu_z, 1)
                for k in range(2):
                    act.wait_ge(s.conv_done, k + 1)
                    nc.scalar.activation(b.XC[:, k, :], b.XC[:, k, :], ACT.Silu).then_inc(s.silu_x, 1)
                act.preload_act_table_set(EXP_LN)
                act.wait_ge(s.xd_ready, 1)
                nc.scalar.activation(b.DTL[0:DTR, :], PB[0:DTR, 5, :], ACT.Copy).then_inc(s.dtl_copied, 1)
                nc.scalar.activation(b.BC[0:32, :], PB[0:32, 6, :], ACT.Copy).then_inc(s.bc_copied, 1)
                act.wait_ge(s.dt_raw, 1)
                link(nc.scalar.activation(b.EE[:], b.DL[:], ACT.Abs))
                nc.scalar.activation(b.EE[:], b.EE[:], ACT.Exp, scale=-1.0).then_inc(s.dt_exp, 1)
                act.preload_act_table_set(LN)
                act.wait_ge(s.dt_u, 1)
                nc.scalar.activation(b.DU[:], b.UU[:], ACT.Ln).then_inc(s.dt_log, 1)
                act.preload_act_table_set(EXP_LN)
                act.wait_ge(s.delta_ready, 1)
                act.wait_ge(s.pads_set, 1)

                def bank_out(e):
                    act.wait_ge(s.ffn_ready, HTILES * (e + 1))
                    if e >= 2:
                        act.wait_ge(s.acc_done, e - 1)
                    nc.scalar.activation(b.YB[:, e % 2, :], PB[:, 4 + e % 2, :], ACT.Identity, bias=w.b2[:, e:e + 1]).then_inc(s.bank_done, 1)

                def hidden(k):
                    act.wait_ge(s.hid_ready, k + 1)
                    if k >= 4:
                        act.wait_ge(s.ffn_ready, k - 3)
                    nc.scalar.activation(b.H[:, k % 4, :], PB[:, HID_BANKS[k % 3], :], ACT.Relu, bias=w.b1[:, k:k + 1]).then_inc(s.hid_even, 1)

                for n in range(NS):
                    if n >= 2:
                        act.wait_ge(s.state_ready, n - 1)
                    for k in range(2):
                        last = nc.scalar.activation(b.DA[:, n % 2, k, :].rearrange("p (s t) -> p s t", t=SEQ)[:, :, 1:SEQ],
                                                    b.DL[:, k, :].rearrange("p (s t) -> p s t", t=SEQ)[:, :, 1:SEQ],
                                                    ACT.Exp, scale=c.aneg[:, k * NS + n:k * NS + n + 1])
                    last.then_inc(s.decay_ready, 1)
                    act.wait_ge(s.c_ready, n + 1)
                    if n >= 2:
                        act.wait_ge(s.part_ready, n - 1)
                    nc.scalar.activation(b.CN[:, n % 2, :], PB[:, 1, :], ACT.Copy).then_inc(s.c_copied, 1)
                    hidden(HTILES * n)
                    hidden(HTILES * n + 2)
                    if n:
                        bank_out(n - 1)
                bank_out(E2 - 1)
                act.wait_ge(s.acc_done, E2)
                gate_scalar(nc, act, s, c, link)

            @block.vector
            def _(dve):
                link = Link(dve, s.dve_link)
                ln_vector(nc, dve, s, c, c.X[:], c.XN[:], PB, link).then_inc(s.xn_ready, 1)
                dve.wait_ge(s.xn_ready, 1)
                link(ln_vector(nc, dve, s, c, c.XN[:], b.XM[:], PB, link, 1))
                nc.vector.tensor_scalar(b.XM[:], b.XM[:], w.g, w.b, ALU.mult, ALU.add).then_inc(s.xm_ready, 1)
                dve.wait_ge(s.logits_ready, 1)
                spread = lambda x, k: x.unsqueeze(2).broadcast_to([128, TT, k])
                rank = c.rank16.unsqueeze(1).broadcast_to([128, TT, E2])
                link(nc.vector.tensor_tensor(b.LO[:], PB[:, 4, 0:TT * E2].rearrange("p (t e) -> p t e", e=E2),
                                             w.br.unsqueeze(1).broadcast_to([128, TT, E2]), ALU.add))
                link(nc.vector.tensor_reduce(b.M1[:], b.LO[:], AX.X, ALU.max))
                nc.vector.tensor_tensor(b.LO[:], b.LO[:], spread(b.M1[:], E2), ALU.subtract).then_inc(s.logits_shifted, 1)
                dve.wait_ge(s.logits_shifted, 1)
                dve.wait_ge(s.pads_set, 1)
                dve.wait_ge(s.xz_ready, 2)
                for k in range(2):
                    last = nc.vector.tensor_copy(b.XI[:, k, :, TAPS - 1:], PB[:, k, :].rearrange("p (s t) -> p s t", t=SEQ))
                last.then_inc(s.xi_copied, 1)
                dve.wait_ge(s.xi_copied, 1)
                for k in range(2):
                    xc = b.XC[:, k, :].rearrange("p (s t) -> p s t", t=SEQ)
                    link(nc.vector.tensor_scalar(xc, b.XI[:, k, :, 0:SEQ], w.conv[:, k * TAPS:k * TAPS + 1], w.cb[:, k:k + 1],
                                                 ALU.mult, ALU.add))
                    for tap in range(1, TAPS):
                        last = nc.vector.scalar_tensor_tensor(out=xc, in0=b.XI[:, k, :, tap:tap + SEQ],
                                                              scalar=w.conv[:, k * TAPS + tap:k * TAPS + tap + 1], in1=xc,
                                                              op0=ALU.mult, op1=ALU.add)
                        if tap < TAPS - 1:
                            link(last)
                    last.then_inc(s.conv_done, 1)
                link(nc.vector.tensor_scalar(b.OA[:], b.LO[:], 0.0, None, ALU.is_equal))
                link(nc.vector.tensor_tensor(b.WK[:], b.OA[:], rank, ALU.mult))
                link(nc.vector.tensor_reduce(b.M1[:], b.WK[:], AX.X, ALU.max))
                link(nc.vector.tensor_tensor(b.OA[:], b.WK[:], spread(b.M1[:], E2), ALU.is_equal))
                link(nc.vector.scalar_tensor_tensor(out=b.WK[:], in0=b.OA[:], scalar=-BIG, in1=b.LO[:], op0=ALU.mult, op1=ALU.add))
                link(nc.vector.tensor_reduce(b.M1[:], b.WK[:], AX.X, ALU.max))
                link(nc.vector.tensor_tensor(b.OB[:], b.WK[:], spread(b.M1[:], E2), ALU.is_equal))
                link(nc.vector.tensor_tensor(b.WK[:], b.OB[:], rank, ALU.mult))
                link(nc.vector.tensor_reduce(b.M1[:], b.WK[:], AX.X, ALU.max))
                link(nc.vector.tensor_tensor(b.OB[:], b.WK[:], spread(b.M1[:], E2), ALU.is_equal))
                link(nc.vector.tensor_tensor(b.OA[:], b.OA[:], b.OB[:], ALU.add))
                dve.wait_ge(s.route_exp, 1)
                link(nc.vector.tensor_tensor(b.OA[:], b.OA[:], b.EX[:], ALU.mult))
                link(nc.vector.tensor_reduce(b.SM[:], b.EX[:], AX.X, ALU.add))
                link(nc.vector.reciprocal(b.SM[:], b.SM[:]))
                nc.vector.tensor_tensor(b.OA[:], b.OA[:], spread(b.SM[:], E2), ALU.mult).then_inc(s.gates_ready, 1)
                dve.wait_ge(s.dt_ready, 1)
                for k in range(2):
                    last = nc.vector.tensor_scalar(b.DL[:, k, :], PB[:, k, :], w.dtb[:, k:k + 1], None, ALU.add)
                last.then_inc(s.dt_raw, 1)
                dve.wait_ge(s.dt_raw, 1)
                dve.wait_ge(s.dt_exp, 1)
                nc.vector.tensor_scalar(b.UU[:], b.EE[:], 1.0, None, ALU.add).then_inc(s.dt_u, 1)
                dve.wait_ge(s.dt_u, 1)
                link(nc.vector.scalar_tensor_tensor(out=b.EE[:], in0=b.UU[:], scalar=-1.0, in1=b.EE[:], op0=ALU.add, op1=ALU.subtract))
                dve.wait_ge(s.dt_log, 1)
                link(nc.vector.tensor_tensor(b.EE[:], b.DU[:], b.EE[:], ALU.subtract))
                nc.vector.scalar_tensor_tensor(out=b.DL[:], in0=b.DL[:], scalar=0.0, in1=b.EE[:], op0=ALU.max,
                                               op1=ALU.add).then_inc(s.delta_ready, 1)
                dve.wait_ge(s.delta_ready, 1)
                dve.wait_ge(s.silu_x, 2)
                link(nc.vector.tensor_tensor(b.DU[:], b.DL[:], b.XC[:], ALU.mult))

                def hidden(k):
                    dve.wait_ge(s.hid_ready, k + 1)
                    if k >= 4:
                        dve.wait_ge(s.ffn_ready, k - 3)
                    nc.vector.tensor_scalar(b.H[:, k % 4, :], PB[:, HID_BANKS[k % 3], :], w.b1[:, k:k + 1], 0.0,
                                            ALU.add, ALU.max).then_inc(s.hid_odd, 1)

                def weigh(e):
                    dve.wait_ge(s.bank_done, e + 1)
                    dve.wait_ge(s.gateT_ready, e + 1)
                    nc.vector.tensor_tensor(b.YB[:, e % 2, :], b.YB[:, e % 2, :], PB[:, 6, :], ALU.mult).then_inc(s.weighted, 1)

                for n in range(NS):
                    dve.wait_ge(s.b_ready, n + 1)
                    nc.vector.tensor_tensor(b.DB[:, n % 2, :, :], b.DU[:], PB[:, 0, :].unsqueeze(1).broadcast_to([128, 2, T]),
                                            ALU.mult).then_inc(s.drive_ready, 1)
                    hidden(HTILES * n + 1)
                    dve.wait_ge(s.drive_ready, n + 1)
                    dve.wait_ge(s.decay_ready, n + 1)
                    if n >= 2:
                        dve.wait_ge(s.part_ready, n - 1)
                    nc.vector.tensor_tensor_scan(b.ST[:, n % 2].rearrange("p k t -> p (k t)"), b.DA[:, n % 2].rearrange("p k t -> p (k t)"),
                                                 b.DB[:, n % 2].rearrange("p k t -> p (k t)"), 0.0, ALU.mult, ALU.add).then_inc(s.state_ready, 1)
                    dve.wait_ge(s.state_ready, n + 1)
                    hidden(HTILES * n + 3)
                    if n:
                        weigh(n - 1)
                dve.wait_ge(s.y_summed, 1)
                for k in range(2):
                    last = nc.vector.scalar_tensor_tensor(out=b.YA[:, k, :], in0=b.XC[:, k, :], scalar=w.dskip[:, k:k + 1],
                                                          in1=b.YA[:, k, :], op0=ALU.mult, op1=ALU.add)
                link(last)
                nc.vector.tensor_tensor(b.EE[:], b.YA[:], b.ZS[:], ALU.mult).then_inc(s.y_gated, 1)
                weigh(E2 - 1)
                dve.wait_ge(s.mamba_ready, 1)
                link(nc.vector.tensor_tensor(c.S[:], PB[:, 0, :], c.XN[:], ALU.add))
                dve.wait_ge(s.acc_done, E2)
                gate_vector(nc, dve, s, c, link)

            @block.gpsimd
            def _(pool):
                link = Link(pool, s.pool_link)
                for k in range(2):
                    nc.gpsimd.memset(b.XI[:, k, :, 0:TAPS - 1], 0.0)
                last = nc.gpsimd.memset(b.DA[:].rearrange("p a k (s t) -> p (a k s) t", t=SEQ)[:, :, 0:1], 0.0)
                last.then_inc(s.pads_set, 1)

                def add_bank(e):
                    pool.wait_ge(s.weighted, e + 1)
                    if e == 0:
                        nc.gpsimd.tensor_copy(c.Y[:], b.YB[:, 0, :]).then_inc(s.acc_done, 1)
                    else:
                        nc.gpsimd.tensor_tensor(c.Y[:], c.Y[:], b.YB[:, e % 2, :], ALU.add).then_inc(s.acc_done, 1)
                    pool.wait_ge(s.acc_done, e + 1)

                pool.wait_ge(s.gates_ready, 1)
                for n in range(NS):
                    if n >= 2:
                        pool.wait_ge(s.gateT_ready, n - 1)
                    nc.gpsimd.tensor_copy(b.GS[:, n % 2], b.OA[:, :, n:n + 1].broadcast_to([128, TT, 128])).then_inc(s.gate_spread, 1)
                    pool.wait_ge(s.state_ready, n + 1)
                    pool.wait_ge(s.c_copied, n + 1)
                    cn = b.CN[:, n % 2, :].unsqueeze(1).broadcast_to([128, 2, T])
                    out = b.CH if n else b.YA
                    nc.gpsimd.tensor_tensor(out[:], b.ST[:, n % 2], cn, ALU.mult).then_inc(s.part_ready, 1)
                    pool.wait_ge(s.part_ready, n + 1)
                    if n:
                        last = nc.gpsimd.tensor_tensor(b.YA[:], b.YA[:], b.CH[:], ALU.add)
                        if n < NS - 1:
                            link(last)
                        else:
                            last.then_inc(s.y_summed, 1)
                        add_bank(n - 1)
                add_bank(E2 - 1)
        clear(nc, s)


L3_SEMS = (LN_SEMS + ATT_SEMS + LINKS + "logpen_ready gate_ready gate_raw gate_exp gate_u "
           "gi_ready penq_ready ")


def layer3_attention(nc, c, w, PB):
    with ExitStack() as ctx:
        s = semaphores(nc, ctx, L3_SEMS)
        s = s._replace(scores_read=s.scores_masked)
        b = att_buffers(nc, ctx, "l3", TS=[TBUFS, 2, SEQ], LP=[TT, SEQ], PQ=[TT, SEQ], T1=[SEQ], T2=[SEQ], GA=[T + TT],
                        GU=[T + TT], GJ=[T], NJ=[T], GI=[TT], AI=[TT], PI=[TT])
        with nc.Block() as block:
            @block.tensor
            def _(pe):
                ln_tensor(nc, pe, s, c, c.X[:], PB)
                pe.wait_ge(s.xn_ready, 1)
                nc.tensor.matmul(PB[:, 2, :], w.grow, c.XN[:], start=True, stop=True)
                for t in range(TT):
                    last = nc.tensor.matmul(PB[:, 3, t:t + 1], c.XN[:, t * 128:(t + 1) * 128], w.gcol, start=True, stop=True)
                last.then_inc(s.gate_ready, 1)
                pe.wait_ge(s.gate_raw, 1)
                att_tensor(nc, pe, s, c, w, b, PB, c.unpad)

            @block.scalar
            def _(act):
                link = Link(act, s.act_link)
                act.preload_act_table_set(EXP_LN)
                ln_scalar(nc, act, s, c, PB, link)
                act.wait_ge(s.gate_raw, 1)
                link(nc.scalar.activation(b.GU[:], b.GA[:], ACT.Abs))
                link(nc.scalar.activation(b.GU[:], b.GU[:], ACT.Exp, scale=-1.0))
                act.preload_act_table_set(LN)
                nc.scalar.activation(b.GU[:], b.GU[:], ACT.Ln, bias=c.one).then_inc(s.gate_exp, 1)
                act.preload_act_table_set(EXP_LN)
                act.wait_ge(s.gate_u, 1)
                link(nc.scalar.activation(b.GJ[:], b.GU[:, 0:T], ACT.Exp))
                nc.scalar.activation(b.GI[:], b.GU[:, T:T + TT], ACT.Exp).then_inc(s.gi_ready, 1)
                act.wait_ge(s.gi_ready, 1)
                link(nc.scalar.activation(b.PI[:], b.GI[:], ACT.Exp, scale=-float(np.log(SEQ - 2)), bias=c.pow))
                act.sem_inc(s.gi_ready, 1)
                act.wait_ge(s.penq_ready, 1)
                act.preload_act_table_set(LN)
                link(nc.scalar.activation(b.LP[:], b.PQ[:], ACT.Ln, scale=PEN_SCALE))
                act.preload_act_table_set(EXP_LN)
                nc.scalar.activation(b.LP[:], b.LP[:], ACT.Identity, bias=c.lnpen).then_inc(s.logpen_ready, 1)
                att_scalar(nc, act, s, c, b, PB, link, c.bqs, True)

            @block.vector
            def _(dve):
                link = Link(dve, s.dve_link)
                ln_vector(nc, dve, s, c, c.X[:], c.XN[:], PB, link).then_inc(s.xn_ready, 1)
                dve.wait_ge(s.gate_ready, 1)
                nc.vector.tensor_scalar(b.GA[:, 0:T], PB[:, 2, :], w.bg, None, ALU.add)
                nc.vector.tensor_scalar(b.GA[:, T:T + TT], PB[:, 3, 0:TT], w.bg, None, ALU.add).then_inc(s.gate_raw, 1)
                dve.wait_ge(s.gate_raw, 1)
                dve.wait_ge(s.gate_exp, 1)
                nc.vector.scalar_tensor_tensor(out=b.GU[:], in0=b.GA[:], scalar=0.0, in1=b.GU[:], op0=ALU.min,
                                               op1=ALU.subtract).then_inc(s.gate_u, 1)
                dve.wait_ge(s.gi_ready, 2)
                link(nc.vector.tensor_scalar(b.NJ[:], b.GJ[:], -1.0, None, ALU.mult))
                link(nc.vector.tensor_scalar(b.AI[:], b.GI[:], -1.0, 1.0, ALU.mult, ALU.add))
                for t in range(TT):
                    gj = slice(t // 2 * SEQ, (t // 2 + 1) * SEQ)
                    ai, gi, pi = b.AI[:, t:t + 1], b.GI[:, t:t + 1], b.PI[:, t:t + 1]
                    nc.vector.tensor_scalar(b.T2[:], b.GJ[:, gj], ai, 1.0, ALU.add, ALU.min)
                    link(nc.vector.tensor_scalar(b.T1[:], b.NJ[:, gj], ai, 0.0, ALU.add, ALU.max))
                    link(nc.vector.tensor_scalar(b.T1[:], b.T1[:], ai, None, ALU.mult))
                    link(nc.vector.scalar_tensor_tensor(out=b.T1[:], in0=b.T2[:], scalar=gi, in1=b.T1[:], op0=ALU.mult, op1=ALU.add))
                    link(nc.vector.tensor_scalar(b.T2[:], c.dist[:, t % 2 * SEQ:(t % 2 + 1) * SEQ], pi, 1.0, ALU.add, ALU.min))
                    link(nc.vector.scalar_tensor_tensor(out=b.T1[:], in0=b.T2[:], scalar=1e-32, in1=b.T1[:], op0=ALU.max, op1=ALU.mult))
                    last = nc.vector.tensor_scalar(b.PQ[:, t, :], b.T1[:], 1e-32, None, ALU.max)
                    if t < TT - 1:
                        link(last)
                last.then_inc(s.penq_ready, 1)
                att_vector(nc, dve, s, c, w, b, PB, link, True)
                dve.wait_ge(s.att_ready, 1)
                link(nc.vector.tensor_copy(c.S[:], PB[:, 0, :]))

            @block.gpsimd
            def _(pool):
                att_gpsimd(nc, pool, s, b, Link(pool, s.pool_link))
        clear(nc, s)


L3F_SEMS = (LN_SEMS + GATE_SEMS + LINKS + "pad_set shift_done raw_ready raw_copied squared norm_ready norm_taken norm_guarded rot_ready "
            "cos_done sin_done rnorm_ready rot_summed qk_ready v_ready v_copied win_ready win_shifted prob_ready probT_ready "
            "probT_copied ctx_ready ctx_recip ctx_scaled o_ready x_added hn_ready gate_in_ready gelu_done val_ready hid_ready "
            "out_ready layer_done ")
NW = SEQ // WIN
NT = LI // 128
FT = [(0, 128), (128, 128), (256, HIDL - 256)]


def layer3_ffn(nc, c, ws, PB):
    with ExitStack() as ctx:
        s = semaphores(nc, ctx, L3F_SEMS)
        b = buffers(nc, ctx, "l3f", HS=[NB, SEQ], HN=[T], RW=[2, T], SQ=[2, T], C1=[2, T], C2=[2, T], NR=[2, T], RN=[2, T],
                    QK=[2 * NT, T], VL=[NB, 3, LI], MX=[NW], SH=[2, T], PP=[2, T], PT=[2, T], OF=[NT, T], LG=[T], DT=[T],
                    RG=[2, T], G=[3, T], HH=[3, T])
        F = c.XN
        U, A = 2 * NT, NT * NB

        with nc.Block() as block:
            @block.tensor
            def _(pe):
                for l in range(DEPTH):
                    w, u0, a0 = ws[l], l * U, l * A
                    pe.wait_ge(s.shift_done, 2 * l + 1)
                    hs = b.HS[:].rearrange("p s t -> p (s t)")
                    for u in range(U + 1):
                        if u < U:
                            if u >= 2:
                                pe.wait_ge(s.raw_copied, u0 + u - 1)
                            nc.tensor.matmul(PB[:, u % 2, :], w.qkv[:, u * 128:(u + 1) * 128], hs, start=True, stop=True).then_inc(s.raw_ready, 1)
                        if u < NB * 3:
                            sq, o = divmod(u, 3)
                            if u >= 2:
                                pe.wait_ge(s.v_copied, NB * 3 * l + u - 1)
                            t0 = sq * SEQ + o * WIN
                            nc.tensor.matmul(PB[:, 6 + u % 2, :], hs[:, t0:t0 + 128], w.qkv[:, 2 * LI:3 * LI], start=True, stop=True).then_inc(s.v_ready, 1)
                        if u:
                            v = u - 1
                            if v >= 2:
                                pe.wait_ge(s.norm_taken, u0 + v - 1)
                                pe.wait_ge(s.sin_done, u0 + v - 1)
                            pe.wait_ge(s.raw_copied, u0 + v + 1)
                            nc.tensor.matmul(PB[:, 4 + v % 2, :], c.rotq[l] if v < NT else c.rotk[l], b.RW[:, v % 2, :],
                                             start=True, stop=True).then_inc(s.rot_ready, 1)
                            pe.wait_ge(s.squared, u0 + v + 1)
                            nc.tensor.matmul(PB[:, 2 + v % 2, :], c.bd64, b.SQ[:, v % 2, :], start=True, stop=True).then_inc(s.norm_ready, 1)
                    pe.wait_ge(s.v_copied, NB * 3 * (l + 1))
                    pe.wait_ge(s.norm_taken, u0 + U)
                    pe.wait_ge(s.sin_done, u0 + U)
                    pe.wait_ge(s.qk_ready, u0 + U)
                    for m in range(A + 3):
                        if m < A:
                            hp, sq = divmod(m, NB)
                            if m >= 2:
                                pe.wait_ge(s.win_shifted, a0 + m - 1)
                            for win in range(NW):
                                q0 = sq * SEQ + win * WIN
                                k0 = q0 - WIN if win else q0
                                for h in range(2):
                                    r = slice(LD * h, LD * h + LD)
                                    last = nc.tensor.matmul(PB[r, m % 2, win * 128:win * 128 + 2 * WIN], b.QK[r, hp, q0:q0 + WIN],
                                                            b.QK[r, NT + hp, k0:k0 + 2 * WIN], start=win == 0, stop=False,
                                                            skip_group_check=True)
                            last = nc.tensor.matmul(PB[:, m % 2, :], c.identb, c.windowb, start=False, stop=True, skip_group_check=True)
                            last.then_inc(s.win_ready, 1)
                        v = m - 2
                        if 0 <= v < A:
                            pe.wait_ge(s.prob_ready, a0 + v + 1)
                            if v >= 2:
                                pe.wait_ge(s.probT_copied, a0 + v - 1)
                            for win in range(NW):
                                last = nc.tensor.transpose(PB[:, 2 + v % 2, win * 128:(win + 1) * 128],
                                                           b.PP[:, v % 2, win * 128:(win + 1) * 128], c.ident)
                            last.then_inc(s.probT_ready, 1)
                        v = m - 3
                        if 0 <= v < A:
                            hp, sq = divmod(v, NB)
                            if sq == 0 and hp >= 2:
                                pe.wait_ge(s.ctx_scaled, l * NT + hp - 1)
                            pe.wait_ge(s.probT_copied, a0 + v + 1)
                            k = 4 + 2 * (hp % 2)
                            for win in range(NW):
                                o0 = sq * SEQ + win * WIN
                                for h in range(2):
                                    r = slice(LD * h, LD * h + LD)
                                    p = b.PT[:, v % 2, win * 128 + h * WIN:win * 128 + h * WIN + WIN]
                                    f0 = (2 * hp + h) * LD
                                    nc.tensor.matmul(PB[r, k, o0:o0 + WIN], b.VL[:, sq, max(win - 1, 0), f0:f0 + LD], p,
                                                     start=True, stop=True, tile_position=(0, LD * h))
                                    last = nc.tensor.matmul(PB[r, k + 1, o0:o0 + WIN], c.ones[:, 0:LD], p,
                                                            start=True, stop=True, tile_position=(0, LD * h))
                            last.then_inc(s.ctx_ready, 1)
                    for t in range(NT):
                        pe.wait_ge(s.ctx_scaled, l * NT + t + 1)
                        last = nc.tensor.matmul(PB[:, 2, :], w.o[:, t * 128:(t + 1) * 128], b.OF[:, t, :], start=t == 0, stop=t == NT - 1)
                    last.then_inc(s.o_ready, 1)
                    pe.wait_ge(s.shift_done, 2 * l + 2)
                    ln_tensor(nc, pe, s, c, hs, PB, l)
                    pe.wait_ge(s.hn_ready, l + 1)
                    for i, (f0, fn) in enumerate(FT):
                        nc.tensor.matmul(PB[0:fn, 2 + i, :], w.wg[:, f0:f0 + fn], b.HN[:], start=True, stop=True).then_inc(s.gate_in_ready, 1)
                        nc.tensor.matmul(PB[0:fn, 5 + i, :], w.wa[:, f0:f0 + fn], b.HN[:], start=True, stop=True).then_inc(s.val_ready, 1)
                    for i, (f0, fn) in enumerate(FT):
                        pe.wait_ge(s.hid_ready, 3 * l + i + 1)
                        last = nc.tensor.matmul(PB[:, 0, :], w.w2[0:fn, i * 128:(i + 1) * 128], b.HH[0:fn, i, :], start=i == 0, stop=i == 2)
                    last.then_inc(s.out_ready, 1)

            @block.scalar
            def _(act):
                link = Link(act, s.act_link)
                act.preload_act_table_set(EXP_LN)
                for l in range(DEPTH):
                    w, u0, a0 = ws[l], l * U, l * A
                    for u in range(U + 1):
                        if u < U:
                            act.wait_ge(s.raw_ready, u0 + u + 1)
                            if u >= 2:
                                act.wait_ge(s.squared, u0 + u - 1)
                                act.wait_ge(s.rot_ready, u0 + u - 1)
                                act.wait_ge(s.cos_done, u0 + u - 1)
                            nc.scalar.activation(b.RW[:, u % 2, :], PB[:, u % 2, :], ACT.Copy).then_inc(s.raw_copied, 1)
                        if u < NB * 3:
                            sq, o = divmod(u, 3)
                            act.wait_ge(s.v_ready, NB * 3 * l + u + 1)
                            nc.scalar.activation(b.VL[:, sq, o, :], PB[:, 6 + u % 2, :], ACT.Copy).then_inc(s.v_copied, 1)
                        if u:
                            v = u - 1
                            act.wait_ge(s.norm_guarded, u0 + v + 1)
                            link(nc.scalar.activation(b.NR[:, v % 2, :], b.NR[:, v % 2, :], ACT.Ln, scale=NORM_SCALE))
                            if v >= 2:
                                act.wait_ge(s.qk_ready, u0 + v - 1)
                            nc.scalar.activation(b.RN[:, v % 2, :], b.NR[:, v % 2, :], ACT.Exp, scale=-0.5, bias=c.lnnorm).then_inc(s.rnorm_ready, 1)
                    for m in range(A + 4):
                        if m < A:
                            act.wait_ge(s.win_shifted, a0 + m + 1)
                            if m >= 2:
                                act.wait_ge(s.probT_ready, a0 + m - 1)
                            nc.scalar.activation(b.PP[:, m % 2, :], b.SH[:, m % 2, :], ACT.Exp, scale=8.0).then_inc(s.prob_ready, 1)
                        v = m - 2
                        if 0 <= v < A:
                            act.wait_ge(s.probT_ready, a0 + v + 1)
                            if v >= 2:
                                act.wait_ge(s.ctx_ready, a0 + v - 1)
                            nc.scalar.activation(b.PT[:, v % 2, :], PB[:, 2 + v % 2, :], ACT.Copy).then_inc(s.probT_copied, 1)
                        v = m - 4
                        if 0 <= v and v % NB == NB - 1:
                            hp = v // NB
                            act.wait_ge(s.ctx_ready, a0 + v + 1)
                            link(nc.scalar.activation(b.LG[:], PB[:, 5 + 2 * (hp % 2), :], ACT.Ln))
                            if l or hp >= 2:
                                act.wait_ge(s.ctx_scaled, l * NT + hp - 1)
                            nc.scalar.activation(b.RG[:, hp % 2, :], b.LG[:], ACT.Exp, scale=-1.0).then_inc(s.ctx_recip, 1)
                            act.wait_ge(s.ctx_recip, l * NT + hp + 1)
                    ln_scalar(nc, act, s, c, PB, link, l)
                    for i, (f0, fn) in enumerate(FT):
                        act.wait_ge(s.gate_in_ready, 3 * l + i + 1)
                        nc.scalar.activation(b.G[0:fn, i, :], PB[0:fn, 2 + i, :], ACT.Gelu, bias=w.bgl[0:fn, i:i + 1]).then_inc(s.gelu_done, 1)
                    act.preload_act_table_set(EXP_LN)
                act.wait_ge(s.layer_done, DEPTH)
                gate_scalar(nc, act, s, c, link)

            @block.vector
            def _(dve):
                link = Link(dve, s.dve_link)

                def shift():
                    nc.vector.tensor_copy(b.HS[0:64, :, :], F[0:64, :].rearrange("p (s t) -> p s t", t=SEQ))
                    nc.vector.tensor_copy(b.HS[64:128, :, 1:SEQ],
                                          F[64:128, :].rearrange("p (s t) -> p s t", t=SEQ)[:, :, 0:SEQ - 1]).then_inc(s.shift_done, 1)

                dve.wait_ge(s.pad_set, 1)
                two = lambda x: x.unsqueeze(1).broadcast_to([128, NB, SEQ])
                for l in range(DEPTH):
                    w, u0, a0 = ws[l], l * U, l * A
                    shift()
                    dve.wait_ge(s.shift_done, 2 * l + 1)
                    for u in range(U + 1):
                        seq = lambda x: x.rearrange("p (s t) -> p s t", t=SEQ)
                        if u < U:
                            cos, sin = (c.qcos, c.qsin) if u < NT else (c.kcos, c.ksin)
                            dve.wait_ge(s.raw_copied, u0 + u + 1)
                            if u >= 2:
                                dve.wait_ge(s.rot_summed, u0 + u - 1)
                                dve.wait_ge(s.qk_ready, u0 + u - 1)
                            nc.vector.scalar_tensor_tensor(out=seq(b.C1[:, u % 2, :]), in0=seq(b.RW[:, u % 2, :]),
                                                           scalar=w.qs if u < NT else w.ks, in1=two(cos),
                                                           op0=ALU.mult, op1=ALU.mult).then_inc(s.cos_done, 1)
                            dve.wait_ge(s.rot_ready, u0 + u + 1)
                            nc.vector.tensor_tensor(seq(b.C2[:, u % 2, :]), seq(PB[:, 4 + u % 2, :]), two(sin), ALU.mult).then_inc(s.sin_done, 1)
                            dve.wait_ge(s.norm_ready, u0 + u + 1)
                            if u >= 2:
                                dve.wait_ge(s.rnorm_ready, u0 + u - 1)
                            nc.vector.tensor_scalar(b.NR[:, u % 2, :], PB[:, 2 + u % 2, :], 1e-24, None, ALU.max).then_inc(s.norm_taken, 1)
                            dve.wait_ge(s.norm_taken, u0 + u + 1)
                            dve.sem_inc(s.norm_guarded, 1)
                        if u:
                            v = u - 1
                            dve.wait_ge(s.rnorm_ready, u0 + v + 1)
                            dve.wait_ge(s.rot_summed, u0 + v + 1)
                            nc.vector.tensor_tensor(b.QK[:, v, :], b.C1[:, v % 2, :], b.RN[:, v % 2, :], ALU.mult).then_inc(s.qk_ready, 1)
                    dve.wait_ge(s.qk_ready, u0 + U)
                    for m in range(A + 5):
                        if m < A:
                            dve.wait_ge(s.win_ready, a0 + m + 1)
                            pw = PB[:, m % 2, :].rearrange("p (w k) -> p w k", k=128)
                            link(nc.vector.tensor_reduce(b.MX[:], pw, AX.X, ALU.max))
                            if m >= 2:
                                dve.wait_ge(s.prob_ready, a0 + m - 1)
                            nc.vector.tensor_tensor(b.SH[:, m % 2, :].rearrange("p (w k) -> p w k", k=128), pw,
                                                    b.MX[:].unsqueeze(2).broadcast_to([128, NW, 128]), ALU.subtract).then_inc(s.win_shifted, 1)
                            dve.wait_ge(s.win_shifted, a0 + m + 1)
                        v = m - 5
                        if 0 <= v and v % NB == NB - 1:
                            hp = v // NB
                            dve.wait_ge(s.ctx_recip, l * NT + hp + 1)
                            k = 4 + 2 * (hp % 2)
                            divide(nc, b.OF[:, hp, :], PB[:, k, :], PB[:, k + 1, :], b.RG[:, hp % 2, :], b.DT[:], link).then_inc(s.ctx_scaled, 1)
                            dve.wait_ge(s.ctx_scaled, l * NT + hp + 1)
                    dve.wait_ge(s.o_ready, l + 1)
                    link(nc.vector.tensor_tensor(F[:], F[:], PB[:, 2, :], ALU.add))
                    shift()
                    dve.wait_ge(s.shift_done, 2 * l + 2)
                    link(ln_vector(nc, dve, s, c, b.HS[:].rearrange("p s t -> p (s t)"), b.HN[:], PB, link, l))
                    nc.vector.tensor_scalar(b.HN[:], b.HN[:], w.lg, w.lb, ALU.mult, ALU.add).then_inc(s.hn_ready, 1)
                    for i, (f0, fn) in enumerate(FT):
                        dve.wait_ge(s.gelu_done, 3 * l + i + 1)
                        dve.wait_ge(s.val_ready, 3 * l + i + 1)
                        nc.vector.scalar_tensor_tensor(out=b.HH[0:fn, i, :], in0=PB[0:fn, 5 + i, :], scalar=w.ba[0:fn, i:i + 1],
                                                       in1=b.G[0:fn, i, :], op0=ALU.add, op1=ALU.mult).then_inc(s.hid_ready, 1)
                    dve.wait_ge(s.out_ready, l + 1)
                    out = F if l < DEPTH - 1 else c.Y
                    nc.vector.scalar_tensor_tensor(out=out[:], in0=PB[:, 0, :], scalar=w.b2, in1=F[:],
                                                   op0=ALU.add, op1=ALU.add).then_inc(s.layer_done, 1)
                    dve.wait_ge(s.layer_done, l + 1)
                gate_vector(nc, dve, s, c, link)

            @block.gpsimd
            def _(pool):
                nc.gpsimd.memset(b.HS[64:128, :, 0:1], 0.0).then_inc(s.pad_set, 1)
                for l in range(DEPTH):
                    u0 = l * U
                    for u in range(U):
                        pool.wait_ge(s.raw_copied, u0 + u + 1)
                        if u >= 2:
                            pool.wait_ge(s.norm_ready, u0 + u - 1)
                        nc.gpsimd.tensor_tensor(b.SQ[:, u % 2, :], b.RW[:, u % 2, :], b.RW[:, u % 2, :], ALU.mult).then_inc(s.squared, 1)
                        pool.wait_ge(s.cos_done, u0 + u + 1)
                        pool.wait_ge(s.sin_done, u0 + u + 1)
                        nc.gpsimd.tensor_tensor(b.C1[:, u % 2, :], b.C1[:, u % 2, :], b.C2[:, u % 2, :], ALU.add).then_inc(s.rot_summed, 1)
        clear(nc, s)


def network(nc, x, consts, w0, w1, w2, w2f, w3, w3f, out, layers):
    tokens = x.shape[0]
    chunks = tokens // T
    with ExitStack() as ctx:
        def sb(name, parts):
            return ctx.enter_context(nc.sbuf_tensor(name, [128, columns(parts)[1]], F32))

        pieces = [("consts", CONSTS, consts), ("w0s", W0, w0), ("w1s", W1, w1), ("w2s", W2, w2), ("w3s", W3, w3), ("w3fs", W3F, w3f)]
        tiles = {n: sb(n, parts) for n, parts, _ in pieces}
        c = view(tiles["consts"], CONSTS)
        v0, v1, v2, v3 = view(tiles["w0s"], W0), view(tiles["w1s"], W1), view(tiles["w2s"], W2), view(tiles["w3s"], W3)
        per_layer = columns(W3F)[1] // DEPTH
        ws = [view(tiles["w3fs"][:, l * per_layer:(l + 1) * per_layer], W3F_LAYER) for l in range(DEPTH)]
        keep = buffers(nc, ctx, "keep", X=[T], XN=[T], S=[T], Y=[T], lnc=[T], lnsq=[T], lnr=[T], lnt=[T], ga=[T], gb=[T],
                       aneg=[2 * NS], bqs=[4], XI0=[TT, 128])
        identb = ctx.enter_context(nc.sbuf_tensor("identb", [128, 128], BF16))
        windowb = ctx.enter_context(nc.sbuf_tensor("windowb", [128, 512], BF16))
        rots = ctx.enter_context(nc.sbuf_tensor("rots", [128, 2 * DEPTH, 128], F32))
        c = record(**c._asdict(), **keep._asdict(), identb=identb[:], windowb=windowb[:],
                   rotq=[rots[:, 2 * l, :] for l in range(DEPTH)], rotk=[rots[:, 2 * l + 1, :] for l in range(DEPTH)])
        PB = ctx.enter_context(nc.psum_tensor("PB", [128, 8, 512], F32))

        with ExitStack() as pro:
            s = semaphores(nc, pro, "loaded exped folded fold_ready dve_link")
            with nc.Block() as block:
                @block.sync
                def _(sp):
                    for n, _, src in pieces:
                        sp.dma_start(tiles[n][:], src).then_inc(s.loaded, 16)

                @block.scalar
                def _(act):
                    act.wait_ge(s.loaded, 16 * len(pieces))
                    nc.scalar.activation(c.aneg[:], v2.alog, ACT.Exp).then_inc(s.exped, 1)

                @block.tensor
                def _(pe):
                    pe.wait_ge(s.loaded, 16 * len(pieces))
                    nc.tensor.matmul(PB[:, 0, 0:1], v0.woutm[0:64, :], v0.b2m[0:64, :], start=True, stop=True).then_inc(s.folded, 1)

                @block.vector
                def _(dve):
                    link = Link(dve, s.dve_link)
                    dve.wait_ge(s.loaded, 16 * len(pieces))
                    win = v0.win.unsqueeze(2).broadcast_to([128, 64, 16])
                    w1 = v0.w1.rearrange("p (m h) -> p m h", h=16)
                    nc.vector.tensor_tensor(w1, w1, win, ALU.mult)
                    w2 = v0.w2.rearrange("p (i d) -> p i d", d=128)
                    nc.vector.tensor_tensor(w2, w2, v0.w2c.unsqueeze(2).broadcast_to([128, 8, 128]), ALU.mult)
                    link(nc.vector.tensor_tensor(v0.w1c, v0.w1c, v0.binc, ALU.mult))
                    nc.vector.tensor_tensor(v0.b1c, v0.b1c, v0.w1c, ALU.add)
                    dve.wait_ge(s.folded, 1)
                    nc.vector.tensor_tensor(v0.bout, v0.bout, PB[:, 0, 0:1], ALU.add)
                    dve.wait_ge(s.exped, 1)
                    nc.vector.tensor_scalar(c.aneg[:], c.aneg[:], -1.0, None, ALU.mult)
                    nc.vector.tensor_scalar(c.bqs[:], v3.bq, float(DH) ** -0.5, None, ALU.mult)
                    nc.vector.tensor_copy(c.identb, c.ident)
                    nc.vector.tensor_copy(c.windowb, c.window)
                    for l in range(DEPTH):
                        nc.vector.tensor_scalar(c.rotq[l], c.rot, ws[l].qs, None, ALU.mult)
                        nc.vector.tensor_scalar(c.rotk[l], c.rot, ws[l].ks, None, ALU.mult)
            clear(nc, s)

        x_mid = nc.dram_tensor("x_mid", (chunks * 128, T), F32, kind="Internal").ap()
        s_mid = nc.dram_tensor("s_mid", (chunks * 128, T), F32, kind="Internal").ap()
        y_mid = nc.dram_tensor("y_mid", (tokens, D), F32, kind="Internal").ap()

        with ExitStack() as first:
            r = record(base=first.enter_context(nc.sbuf_tensor("base", [128, E1], F32)),
                                rank=first.enter_context(nc.sbuf_tensor("rank", [128, tokens // 128], F32)),
                                route=first.enter_context(nc.sbuf_tensor("route", [128, tokens // 128, E1], F32)),
                                y=first.enter_context(nc.sbuf_tensor("y", [128, tokens // 128, D], F32)))
            with nc.Block() as block:
                @block.vector
                def _(dve):
                    nc.vector.memset(r.base[:], 0.0)
            with nc.Fori(0, chunks) as it:
                with ExitStack() as io:
                    s = semaphores(nc, io, "x_loaded xT_ready ")
                    with nc.Block() as block:
                        @block.sync
                        def _(sp):
                            sp.dma_start(c.XI0[:], x[bass.ts(it, T), :].rearrange("(t p) d -> p t d", p=128)).then_inc(s.x_loaded, 16)

                        @block.tensor
                        def _(pe):
                            pe.wait_ge(s.x_loaded, 16)
                            for t in range(TT):
                                last = nc.tensor.transpose(PB[:, 0, t * 128:(t + 1) * 128], c.XI0[:, t, :], c.ident)
                            last.then_inc(s.xT_ready, 1)

                        @block.vector
                        def _(dve):
                            dve.wait_ge(s.xT_ready, 1)
                            nc.vector.tensor_copy(c.X[:], PB[:, 0, :])
                    clear(nc, s)
                layer0(nc, c, v0, PB)
                layer1(nc, c, v1, r, it, x_mid, s_mid, PB)
            place_tokens(nc, r, tokens // 128, y_mid)

        with nc.Fori(0, chunks) as it:
            with ExitStack() as io:
                s = semaphores(nc, io, GATE_SEMS + "x_loaded s_loaded y_loaded yT_ready y_ready act_link dve_link ")
                with nc.Block() as block:
                    @block.sync
                    def _(sp):
                        sp.dma_start(c.XI0[:], y_mid[bass.ts(it, T), :].rearrange("(t p) d -> p t d", p=128)).then_inc(s.y_loaded, 16)
                        sp.dma_start(c.S[:], s_mid[bass.ts(it, 128), :]).then_inc(s.s_loaded, 16)
                        sp.dma_start(c.X[:], x_mid[bass.ts(it, 128), :]).then_inc(s.x_loaded, 16)

                    @block.tensor
                    def _(pe):
                        pe.wait_ge(s.y_loaded, 16)
                        for t in range(TT):
                            last = nc.tensor.transpose(PB[:, 0, t * 128:(t + 1) * 128], c.XI0[:, t, :], c.ident)
                        last.then_inc(s.yT_ready, 1)

                    @block.scalar
                    def _(act):
                        act.preload_act_table_set(EXP_LN)
                        act.wait_ge(s.y_ready, 1)
                        gate_scalar(nc, act, s, c, Link(act, s.act_link))

                    @block.vector
                    def _(dve):
                        dve.wait_ge(s.yT_ready, 1)
                        nc.vector.tensor_copy(c.Y[:], PB[:, 0, :]).then_inc(s.y_ready, 1)
                        dve.wait_ge(s.y_ready, 1)
                        dve.wait_ge(s.s_loaded, 16)
                        dve.wait_ge(s.x_loaded, 16)
                        gate_vector(nc, dve, s, c, Link(dve, s.dve_link))
                clear(nc, s)
            if layers > 2:
                layer2(nc, c, v2, w2f, PB)
            if layers > 3:
                layer3_attention(nc, c, v3, PB)
                layer3_ffn(nc, c, ws, PB)
            with ExitStack() as io:
                s = semaphores(nc, io, "xT_ready x_copied x_stored")
                with nc.Block() as block:
                    @block.tensor
                    def _(pe):
                        for t in range(TT):
                            last = nc.tensor.transpose(PB[:, 0, t * 128:(t + 1) * 128], c.X[:, t * 128:(t + 1) * 128], c.ident)
                        last.then_inc(s.xT_ready, 1)

                    @block.vector
                    def _(dve):
                        dve.wait_ge(s.xT_ready, 1)
                        nc.vector.tensor_copy(c.XI0[:].rearrange("p t d -> p (t d)"), PB[:, 0, :]).then_inc(s.x_copied, 1)

                    @block.sync
                    def _(sp):
                        sp.wait_ge(s.x_copied, 1)
                        sp.dma_start(out[bass.ts(it, T), :].rearrange("(t p) d -> p t d", p=128), c.XI0[:]).then_inc(s.x_stored, 16)
                        sp.wait_ge(s.x_stored, 16)
                clear(nc, s)


def constants():
    p = np.arange(128)
    k = {}
    k["ident"] = np.eye(128)
    k["mean"] = np.full((128, 128), 1.0 / D)
    k["ones"] = np.ones((128, 128))
    k["before"] = p[:, None] < p[None, :]
    k["sumsel"] = (p[:, None] == p[None, :] // 32 * 32 + DH)
    k["bd8"] = p[:, None] // DH == p[None, :] // DH
    k["bd64"] = p[:, None] // LD == p[None, :] // LD
    un = np.zeros((128, 4, 128))
    for g in range(4):
        for j in range(4):
            for d in range(DH):
                un[32 * j + d, g, (4 * g + j) * DH + d] = 1
    k["unpad"] = un.reshape(128, 512)
    dec = np.exp(-np.arange(SEQ, dtype=np.float32) / np.float32(SEQ))
    k["decrow"] = np.broadcast_to(dec, (128, SEQ))
    k["dectok"] = dec.reshape(2, 128).T
    k["rank8"] = np.broadcast_to(np.arange(E1, 0, -1), (128, E1))
    k["rank16"] = np.broadcast_to(np.arange(E2, 0, -1), (128, E2))
    q = np.arange(2)[None, :, None] * 128 + p[:, None, None]
    k["dist"] = (2.0 - np.abs(q - np.arange(SEQ)[None, None, :])).reshape(128, 2 * SEQ)
    f = np.float32
    half = np.arange(0, LD, 2, dtype=f)
    inv = f(1.0) / f(10000.0) ** (half / f(LD))
    t = np.arange(SEQ, dtype=f)
    fr = (t[:, None] * inv[None, :]).astype(f)
    base = (half + f(0.4 * LD)) / f(1.4 * LD)
    scale = base[None, :] ** ((t - SEQ // 2) / f(WIN // 2))[:, None]
    rep = lambda a: np.tile(a.T, (4, 1))
    cos, sin = np.cos(fr), np.sin(fr)
    k["qcos"], k["qsin"], k["kcos"], k["ksin"] = rep(cos * scale), rep(sin * scale), rep(cos / scale), rep(sin / scale)
    rot = np.zeros((128, 128))
    for m in range(128):
        if m % LD < LD // 2:
            rot[m + LD // 2, m] = -1
        else:
            rot[m - LD // 2, m] = 1
    k["rot"] = rot
    a, cc, win = p[:, None, None] % WIN, np.arange(128)[None, None, :], np.arange(NW)[None, :, None]
    ok = np.where(win == 0, (cc < WIN) & (cc <= a), (cc - WIN <= a) & (a <= cc))
    k["window"] = np.where(ok, 0.0, -1.0e30).reshape(128, NW * 128)
    one = np.ones((128, 1))
    k["eps"], k["one"], k["aeps"] = one * 1e-5, one, one * 1e-6
    k["kone"] = (p % 32 == DH)[:, None]
    k["pow"] = one * np.log(SEQ - 2)
    k["lnpen"] = one * -np.log(PEN_SCALE)
    k["lnnorm"] = one * 0.5 * np.log(NORM_SCALE)
    return pack(CONSTS, k)


def pack(parts, arrays):
    at, width = columns(parts)
    out = np.zeros((128, width), np.float32)
    for n, (a, w) in at.items():
        out[:arrays[n].shape[0], a:a + w] = arrays[n]
    return out


def heads_apart(a):
    out = np.zeros((a.shape[0], NG, 4, 32), a.dtype)
    out[:, :, :, :DH] = a.reshape(a.shape[0], NG, 4, DH)
    return out.reshape(a.shape[0], 512)


def layouts(i):
    rep = lambda a: np.broadcast_to(a, (128, a.size))
    cols = lambda a: a.reshape(-1, 128).T
    out0 = heads_apart(i["L0_attn_Wout"].T).reshape(D, NG, 128).transpose(2, 1, 0).reshape(128, 512)
    w0 = dict(q=heads_apart(i["L0_attn_Wq"]), k=heads_apart(i["L0_attn_Wk"]), v=i["L0_attn_Wv"], out=out0,
              w1=rep(i["L0_ffn_W1"].reshape(-1)), win=i["L0_ffn_Win"],
              w2=np.repeat(i["L0_ffn_Wout"], 16, axis=0).reshape(8, 128, 128).transpose(1, 0, 2).reshape(128, 1024),
              w1c=cols(i["L0_ffn_W1"]), b1c=cols(i["L0_ffn_b1"]), binc=cols(np.repeat(i["L0_ffn_bin_"], 16)),
              w2c=cols(i["L0_ffn_W2"]), woutm=i["L0_ffn_Wout"], b2m=i["L0_ffn_b2"][:, None], bout=i["L0_ffn_bout"][:, None])
    side = lambda a: a.transpose(1, 0, 2).reshape(a.shape[1], -1)
    w1 = dict(q=i["L1_attn_W_q"].T, kv=np.concatenate([i["L1_attn_W_k"].T, i["L1_attn_W_v"].T], 1), o=i["L1_attn_W_o"].T,
              bq=i["L1_attn_b_q"][:, None], bkv=rep(np.concatenate([i["L1_attn_b_k"], i["L1_attn_b_v"]])),
              bo=i["L1_attn_b_o"][:, None], s=i["L1_ffn_Ws"].T, bs=rep(i["L1_ffn_bs"]), w1=side(i["L1_ffn_W1"]),
              b1=i["L1_ffn_b1"].T, w2=side(i["L1_ffn_W2"]), b2=i["L1_ffn_b2"])
    halves = lambda a: side(a.reshape(2, 128, -1))
    w2 = dict(g=i["L2_attn_ln_g"][:, None], b=i["L2_attn_ln_b"][:, None], win=i["L2_attn_W_in"],
              conv=halves(i["L2_attn_conv_w"]), cb=cols(i["L2_attn_conv_b"]), xp=halves(i["L2_attn_W_xp"]), dt=i["L2_attn_W_dt"],
              dtb=cols(i["L2_attn_dt_bias"]), alog=halves(i["L2_attn_A_log"]), dskip=cols(i["L2_attn_D_skip"]),
              out=halves(i["L2_attn_W_out"]), r=i["L2_ffn_Wr"], br=rep(i["L2_ffn_br"]), b1=cols(i["L2_ffn_b1"]), b2=i["L2_ffn_b2"].T)
    w2f = np.concatenate([i["L2_ffn_W1"], i["L2_ffn_W2"].reshape(E2, 4, 128, D).transpose(0, 2, 1, 3).reshape(E2, 128, 512)], 2)
    w3 = dict(q=heads_apart(i["L3_attn_Wq"]), k=heads_apart(i["L3_attn_Wk"]), v=i["L3_attn_Wv"], bv=rep(i["L3_attn_bv"]),
              bq=heads_apart(i["L3_attn_bq"][None]).reshape(NG, 128).T, bk=heads_apart(i["L3_attn_bk"][None]).reshape(NG, 128).T.copy(),
              gcol=i["L3_attn_Wg"], grow=np.broadcast_to(i["L3_attn_Wg"], (D, 128)), bg=rep(i["L3_attn_bg"]))
    w3["bk"][DH::32, :] = 1.0
    w3f = {}
    for l in range(DEPTH):
        p = lambda n: i["L3_ffn_" + n][l]
        tail = lambda a: np.concatenate([a, np.zeros((384 - HIDL, *a.shape[1:]), a.dtype)])
        w3f |= {f"qkv{l}": p("wqkv"), f"qs{l}": np.tile(p("q_scale"), 2)[:, None], f"ks{l}": np.tile(p("k_scale"), 2)[:, None],
                f"o{l}": side(p("wo").reshape(NT, 128, D)), f"lg{l}": p("ln_g")[:, None], f"lb{l}": p("ln_b")[:, None],
                f"wa{l}": p("w1")[:, :HIDL], f"wg{l}": p("w1")[:, HIDL:], f"ba{l}": cols(tail(p("b1")[:HIDL])),
                f"bgl{l}": cols(tail(p("b1")[HIDL:])), f"w2{l}": side(tail(p("w2")).reshape(3, 128, D)), f"b2{l}": p("b2")[:, None]}
    return dict(x=i["L0_attn_x"].reshape(-1, D), consts=constants(), w0=pack(W0, w0), w1=pack(W1, w1), w2=pack(W2, w2), w2f=w2f,
                w3=pack(W3, w3), w3f=pack(W3F, w3f))


LAYERS = 4


def kernel(**inputs):
    import concourse.bacc as _bacc
    from concourse.bass_utils import run_bass_kernel_spmd as _run

    nc = _bacc.Bacc("TRN2", target_bir_lowering=False, num_devices=1)
    i = {n: np.asarray(a) for n, a in inputs.items()}
    shape = i["L0_attn_x"].shape
    arrays, args = {}, []
    for name, a in layouts(i).items():
        a = np.ascontiguousarray(a)
        arrays[f"in_{name}_dram"] = a
        args.append(nc.dram_tensor(f"in_{name}_dram", a.shape, mybir.dt.from_np(a.dtype), kind="ExternalInput").ap())
    out = nc.dram_tensor("out_0_dram", (shape[0] * shape[1], D), F32, kind="ExternalOutput").ap()
    network(nc, *args, out, LAYERS)
    r = _run(nc, [arrays], core_ids=[0])
    return r.results[0]["out_0_dram"].reshape(shape)
```

```python
import concourse.bass as bass
from concourse import mybir
from contextlib import ExitStack
from collections import namedtuple
import numpy as np

F32 = mybir.dt.float32
BF16 = mybir.dt.bfloat16
ALU = mybir.AluOpType
ACT = mybir.ActivationFunctionType
AX = mybir.AxisListType

D = 128
SEQ = 256
NB = 2
T = NB * SEQ
TT = T // 128
NH, DH = 16, 8
NG = 4
E1 = 8
E2, HID2 = 16, 512
DI, NS, DTR, TAPS = 256, 16, 8, 4
DEPTH, LH, LD, WIN = 2, 8, 64, 64
LI = LH * LD
HIDL = int(D * 4 * 2 / 3)
BIG = 3.0e38
EXP_LN = "natural_log_exp_and_others"
LN = "natural_log"
LN_PEN_SCALE = float(np.log(1.0e16))
PEN_SCALE = 1.0e16
NORM_SCALE = float(2 ** 16)


def record(**fields):
    return namedtuple("Record", list(fields))(**fields)


def columns(parts):
    at, out = 0, {}
    for name, width in parts:
        out[name] = (at, width)
        at += width
    return out, at


CONSTS = [("ident", 128), ("mean", 128), ("centre", 128), ("ones", 128), ("before", 128), ("sumsel", 128), ("bd8", 128), ("bd64", 128),
          ("unpad", 4 * 128), ("decrow", SEQ), ("dectok", 2), ("rank8", E1), ("rank16", E2),
          ("dist", 2 * SEQ), ("qcos", SEQ), ("qsin", SEQ), ("kcos", SEQ), ("ksin", SEQ), ("rot", 128),
          ("window", 4 * 128), ("eps", 1), ("one", 1), ("aeps", 1), ("pow", 1), ("lnnorm", 1)]
W0 = [("q", 512), ("k", 512), ("v", 128), ("out", 512), ("w1", 1024), ("w2", 1024), ("win", 64), ("w1c", 8),
      ("b1c", 8), ("binc", 8), ("w2c", 8), ("woutm", 128), ("b2m", 1), ("bout", 1)]
W1 = [("q", 128), ("kv", 256), ("o", 128), ("bq", 1), ("bkv", 256), ("bo", 1), ("s", E1), ("bs", E1),
      ("w1", E1 * 128), ("b1", E1), ("w2", E1 * 128), ("b2", 128)]
W2 = [("g", 1), ("b", 1), ("win", 2 * 2 * 128), ("conv", 2 * TAPS), ("cb", 2), ("xp", 2 * (DTR + 2 * NS)), ("dt", DI),
      ("dtb", 2), ("alog", 2 * NS), ("dskip", 2), ("out", 2 * 128), ("r", E2), ("br", E2), ("b1", E2 * 4), ("b2", E2)]
W2F = [("w1", E2 * HID2), ("w2", E2 * 4 * 128)]
W3 = [("q", 512), ("k", 512), ("v", 128), ("bq", 4), ("bk", 4), ("bv", 128), ("gcol", 1), ("grow", 128), ("bg", 1)]
W3F_LAYER = [("qkv", 3 * LI), ("qs", 1), ("ks", 1), ("o", 4 * 128), ("lg", 1), ("lb", 1), ("wa", HIDL), ("wg", HIDL),
       ("ba", 3), ("bgl", 3), ("w2", 3 * 128), ("b2", 1)]
W3F = [(f"{n}{l}", w) for l in range(DEPTH) for n, w in W3F_LAYER]


def view(tensor, parts):
    at, _ = columns(parts)
    return record(**{n: tensor[:, a:a + w] for n, (a, w) in at.items()})


class Link:

    def __init__(self, eng, sem):
        self.eng, self.sem, self.n = eng, sem, 0

    def __call__(self, ins):
        self.n += 1
        ins.then_inc(self.sem, 1)
        self.eng.wait_ge(self.sem, self.n)
        return ins


def semaphores(nc, ctx, names):
    return record(**{n: ctx.enter_context(nc.semaphore(n)) for n in names.split()})


def buffers(nc, ctx, tag, **shapes):
    return record(**{n: ctx.enter_context(nc.sbuf_tensor(f"{tag}_{n}", [128, *s[:-1]] if s[-1] is BF16 else [128, *s],
                                                                  BF16 if s[-1] is BF16 else F32))
                              for n, s in shapes.items()})


def clear(nc, s):
    nums = sorted({x.num for x in s})
    start = nums[0]
    for a, b in zip(nums, nums[1:] + [None]):
        if b != a + 1:
            nc.gpsimd.sem_clear(range(start, a + 1))
            start = b
    nc.all_engine_barrier(sem_only=True)


LN_SEMS = "ln_centred ln_square ln_var ln_rstd xn_ready "
GATE_SEMS = "gate_log gate_arg gate_sigmoid "
LINKS = "act_link dve_link pool_link "


HALVES = [(h, slice(h * T // 2, (h + 1) * T // 2)) for h in range(2)]


def ln_tensor(nc, pe, s, c, src, PB, n=0):
    for h, half in HALVES:
        nc.tensor.matmul(PB[:, h, 0:T // 2], c.centre, src[:, half], start=True, stop=True).then_inc(s.ln_centred, 1)
    for h, half in HALVES:
        pe.wait_ge(s.ln_square, 2 * n + h + 1)
        nc.tensor.matmul(PB[:, 2 + h, 0:T // 2], c.mean, c.lnsq[:, half], start=True, stop=True).then_inc(s.ln_var, 1)


def ln_scalar(nc, act, s, c, PB, link, n=0):
    for h, half in HALVES:
        act.wait_ge(s.ln_centred, 2 * n + h + 1)
        nc.scalar.activation(c.lnsq[:, half], PB[:, h, 0:T // 2], ACT.Square).then_inc(s.ln_square, 1)
    for h, half in HALVES:
        act.wait_ge(s.ln_var, 2 * n + h + 1)
        link(nc.scalar.activation(c.lnr[:, half], PB[:, 2 + h, 0:T // 2], ACT.Ln, bias=c.eps))
        nc.scalar.activation(c.lnr[:, half], c.lnr[:, half], ACT.Exp, scale=-0.5).then_inc(s.ln_rstd, 1)


def ln_vector(nc, dve, s, c, dst, PB, link, n=0):
    for h, half in HALVES:
        dve.wait_ge(s.ln_rstd, 2 * n + h + 1)
        r, u = c.lnr[:, half], c.lnt[:, half]
        link(nc.vector.tensor_tensor(u, r, r, ALU.mult))
        link(nc.vector.scalar_tensor_tensor(out=u, in0=PB[:, 2 + h, 0:T // 2], scalar=c.eps, in1=u, op0=ALU.add, op1=ALU.mult))
        link(nc.vector.scalar_tensor_tensor(out=u, in0=u, scalar=-3.0, in1=r, op0=ALU.add, op1=ALU.mult))
        last = nc.vector.scalar_tensor_tensor(out=dst[:, half], in0=PB[:, h, 0:T // 2], scalar=-0.5, in1=u, op0=ALU.mult, op1=ALU.mult)
    return last


def divide(nc, dst, num, den, recip, tmp, link):
    link(nc.vector.tensor_tensor(tmp, den, recip, ALU.mult))
    link(nc.vector.scalar_tensor_tensor(out=tmp, in0=tmp, scalar=-2.0, in1=recip, op0=ALU.add, op1=ALU.mult))
    return nc.vector.scalar_tensor_tensor(out=dst, in0=num, scalar=-1.0, in1=tmp, op0=ALU.mult, op1=ALU.mult)


def gate_scalar(nc, act, s, c, link, n=0):
    for h, half in HALVES:
        link(nc.scalar.activation(c.ga[:, half], c.Y[:, half], ACT.Abs))
        link(nc.scalar.activation(c.ga[:, half], c.ga[:, half], ACT.Exp, scale=-1.0))
        nc.scalar.activation(c.ga[:, half], c.ga[:, half], ACT.Ln, bias=c.one).then_inc(s.gate_log, 1)
    for h, half in HALVES:
        act.wait_ge(s.gate_arg, 2 * n + h + 1)
        nc.scalar.activation(c.gb[:, half], c.gb[:, half], ACT.Exp).then_inc(s.gate_sigmoid, 1)


def gate_vector(nc, dve, s, c, link, n=0):
    link(nc.vector.tensor_tensor(c.lnc[:], c.S[:], c.Y[:], ALU.mult))
    for h, half in HALVES:
        dve.wait_ge(s.gate_log, 2 * n + h + 1)
        nc.vector.scalar_tensor_tensor(out=c.gb[:, half], in0=c.Y[:, half], scalar=0.0, in1=c.ga[:, half],
                                       op0=ALU.min, op1=ALU.subtract).then_inc(s.gate_arg, 1)
    for h, half in HALVES:
        dve.wait_ge(s.gate_sigmoid, 2 * n + h + 1)
        link(nc.vector.tensor_tensor(c.lnc[:, half], c.lnc[:, half], c.gb[:, half], ALU.mult))
        link(nc.vector.tensor_tensor(c.X[:, half], c.X[:, half], c.lnc[:, half], ALU.add))


ATT_SEMS = ("scores_read q_ready k_ready v_ready q_copied k_copied v_copied scores_ready scores_masked max_taken exp_done "
            "probT_ready probT_even probT_odd ctx_ready ctx_copied den_ready den_logged den_taken recip_ready "
            "ctx_scaled att_ready att_done zeroed ")
UNITS = NH * NB
GU = UNITS // NG
LAG_T, LAG_P, LAG_V, LAG_O, LAG_D = 4, 5, 7, GU + 6, GU + 9
STEPS = UNITS - GU + LAG_D + 1
SBANKS, TBANKS = 4, 2
BUFS = 4
TBUFS = 3


def unit(m):
    return m // GU, m % GU // 4, m % 4


def group_at(i, lag):
    g, r = divmod(i - lag, GU)
    return g if r == 0 and 0 <= g < NG else None


def turned_done(s, m):
    return (s.probT_odd if m % 2 else s.probT_even), m // 2 + 1


def turned_on_scalar(m, masked):
    return masked or m % 2 == 1


def att_buffers(nc, ctx, tag, **more):
    return buffers(nc, ctx, tag, QP=[NG, T], KP=[NG, T], VT=[TT, NH, 32], MX=[BUFS, 2], PP=[BUFS, 2, SEQ], PT=[BUFS, 2, SEQ],
                   OS=[2, T], LG=[T], RG=[2, T], DT=[T], Z=[NG, T], **more)


def att_tensor(nc, pe, s, c, w, b, PB, w_out, fill=None):
    pe.wait_ge(s.xn_ready, 1)
    for g in range(NG):
        nc.tensor.matmul(PB[:, g, :], w.q[:, g * 128:(g + 1) * 128], c.XN[:], start=True, stop=True).then_inc(s.q_ready, 1)
    for g in range(NG):
        nc.tensor.matmul(PB[:, 4 + g, :], w.k[:, g * 128:(g + 1) * 128], c.XN[:], start=True, stop=True).then_inc(s.k_ready, 1)
    pe.wait_ge(s.q_copied, 1)
    for t in range(TT):
        last = nc.tensor.matmul(PB[:, 0, t * 128:(t + 1) * 128], c.XN[:, t * 128:(t + 1) * 128], w.v,
                                start=True, stop=True)
    last.then_inc(s.v_ready, 1)
    pe.wait_ge(s.q_copied, NG)
    pe.wait_ge(s.k_copied, NG)
    pe.wait_ge(s.v_copied, 1)
    for i in range(STEPS):
        if i < UNITS and i % 2 == 0:
            if i + 2 > SBANKS:
                pe.wait_ge(s.scores_read, i + 2 - SBANKS)
            for qt in range(2):
                for u in (i, i + 1):
                    g, sq, j = unit(u)
                    q0 = sq * SEQ + qt * 128
                    last = nc.tensor.matmul(PB[:, u % SBANKS, qt * SEQ:(qt + 1) * SEQ], b.QP[32 * j:32 * j + 32, g, q0:q0 + 128],
                                            b.KP[32 * j:32 * j + 32, g, sq * SEQ:(sq + 1) * SEQ], start=True, stop=True)
            last.then_inc(s.scores_ready, 2)
        m = i - LAG_T
        if 0 <= m < UNITS:
            pe.wait_ge(s.exp_done, m + 1)
            if m >= TBANKS:
                pe.wait_ge(*turned_done(s, m - TBANKS))
            for kt in range(2):
                for qt in range(2):
                    last = nc.tensor.transpose(PB[:, SBANKS + m % TBANKS, kt * SEQ + qt * 128:kt * SEQ + qt * 128 + 128],
                                               b.PP[:, m % BUFS, qt, kt * 128:(kt + 1) * 128], c.ident)
            last.then_inc(s.probT_ready, 1)
        m = i - LAG_V
        if 0 <= m < UNITS and m % 2 == 0:
            pe.wait_ge(*turned_done(s, m))
            pe.wait_ge(*turned_done(s, m + 1))
            if m % GU == 0 and m >= 2 * GU:
                pe.wait_ge(s.den_taken, m // GU - 1)
            for kt in range(2):
                for u in (m, m + 1):
                    g, sq, j = unit(u)
                    last = nc.tensor.matmul(PB[32 * j:32 * j + 32, 6 + g % 2, sq * SEQ:(sq + 1) * SEQ],
                                            b.VT[:, 2 * sq + kt, 4 * g + j, :], b.PT[:, u % BUFS, kt, :],
                                            start=kt == 0, stop=kt == 1, tile_position=(0, 32 * j))
            last.then_inc(s.ctx_ready, 2)
        g = group_at(i, LAG_D)
        if g is not None:
            pe.wait_ge(s.ctx_copied, g + 1)
            nc.tensor.matmul(PB[:, 6 + g % 2, :], c.sumsel, b.OS[:, g % 2, :], start=True, stop=True).then_inc(s.den_ready, 1)
        if fill and i >= UNITS + LAG_T:
            fill(i - UNITS - LAG_T)
    if fill:
        for k in range(STEPS - UNITS - LAG_T, 9):
            fill(k)
    for g in range(NG):
        pe.wait_ge(s.ctx_scaled, g + 1)
        last = nc.tensor.matmul(PB[:, 0, :], w_out[:, g * 128:(g + 1) * 128], b.Z[:, g, :], start=g == 0, stop=g == NG - 1)
    last.then_inc(s.att_ready, 1)


def copy_queries(nc, act, s, b, PB, bias, masked):
    for g in range(NG):
        act.wait_ge(s.q_ready, g + 1)
        nc.scalar.activation(b.QP[:, g, :], PB[:, g, :], ACT.Identity, scale=float(DH) ** -0.5,
                             bias=bias[:, g:g + 1] if masked else 0.0).then_inc(s.q_copied, 1)


def att_scalar(nc, act, s, c, b, PB, link, masked, fill=None):
    for i in range(STEPS):
        m = i - LAG_T
        if 0 <= m < UNITS and turned_on_scalar(m, masked):
            act.wait_ge(s.probT_ready, m + 1)
            if m >= BUFS:
                act.wait_ge(s.ctx_ready, m - BUFS + 1)
            nc.scalar.activation(b.PT[:, m % BUFS].rearrange("p k q -> p (k q)"), PB[:, SBANKS + m % TBANKS, :],
                                 ACT.Copy).then_inc(turned_done(s, m)[0], 1)
        if i < UNITS:
            act.wait_ge(s.max_taken, i + 1)
            if i >= BUFS:
                act.wait_ge(s.probT_ready, i - BUFS + 1)
            for qt in range(2):
                src = b.TS[:, i % TBUFS, qt, :] if masked else PB[:, i % SBANKS, qt * SEQ:(qt + 1) * SEQ]
                last = nc.scalar.activation(b.PP[:, i % BUFS, qt, :], src, ACT.Exp, scale=-1.0, bias=b.MX[:, i % BUFS, qt:qt + 1])
            last.then_inc(s.exp_done, 1)
        g = group_at(i, LAG_O)
        if g is not None:
            act.wait_ge(s.ctx_ready, GU * (g + 1))
            if g >= 2:
                act.wait_ge(s.ctx_scaled, g - 1)
            nc.scalar.activation(b.OS[:, g % 2, :], PB[:, 6 + g % 2, :], ACT.Copy).then_inc(s.ctx_copied, 1)
        g = group_at(i, LAG_D)
        if g is not None:
            act.wait_ge(s.den_ready, g + 1)
            nc.scalar.activation(b.LG[:], PB[:, 6 + g % 2, :], ACT.Ln).then_inc(s.den_logged, 1)
            act.wait_ge(s.den_logged, g + 1)
            if g >= 2:
                act.wait_ge(s.ctx_scaled, g - 1)
            nc.scalar.activation(b.RG[:, g % 2, :], b.LG[:], ACT.Exp, scale=-1.0).then_inc(s.recip_ready, 1)
            act.wait_ge(s.recip_ready, g + 1)
        if fill and i >= UNITS + LAG_T:
            fill(i - UNITS - LAG_T)
    if fill:
        for k in range(STEPS - UNITS - LAG_T, 9):
            fill(k)


def copy_keys_values(nc, dve, s, w, b, PB, masked):
    for g in range(NG):
        dve.wait_ge(s.k_ready, g + 1)
        if masked:
            nc.vector.tensor_scalar(b.KP[:, g, :], PB[:, 4 + g, :], w.bk[:, g:g + 1], -1.0, ALU.add, ALU.mult).then_inc(s.k_copied, 1)
        else:
            nc.vector.tensor_scalar(b.KP[:, g, :], PB[:, 4 + g, :], -1.0, None, ALU.mult).then_inc(s.k_copied, 1)
    dve.wait_ge(s.zeroed, 1)
    dve.wait_ge(s.v_ready, 1)
    vt = b.VT[:].rearrange("p t h c -> p (t h) c")[:, :, 0:DH]
    vp = PB[:, 0, :].rearrange("p (a c) -> p a c", c=DH)
    if masked:
        for t in range(TT):
            last = nc.vector.tensor_tensor(b.VT[:, t, :, 0:DH], PB[:, 0, t * 128:(t + 1) * 128].rearrange("p (h c) -> p h c", c=DH),
                                           w.bv.rearrange("p (h c) -> p h c", c=DH), ALU.add)
        last.then_inc(s.v_copied, 1)
    else:
        nc.vector.tensor_copy(vt, vp).then_inc(s.v_copied, 1)


def att_vector(nc, dve, s, c, b, PB, link, masked):
    for i in range(STEPS + 1):
        m = i - LAG_P
        if 0 <= m < UNITS and not turned_on_scalar(m, masked):
            dve.wait_ge(s.probT_ready, m + 1)
            if m >= BUFS:
                dve.wait_ge(s.ctx_ready, m - BUFS + 1)
            nc.vector.tensor_copy(b.PT[:, m % BUFS].rearrange("p k q -> p (k q)"),
                                  PB[:, SBANKS + m % TBANKS, :]).then_inc(turned_done(s, m)[0], 1)
        if i < UNITS:
            g, sq, j = unit(i)
            dve.wait_ge(s.scores_ready, i + 1)
            src = PB[:, i % SBANKS, :].rearrange("p (t k) -> p t k", k=SEQ)
            if masked:
                if i >= TBUFS:
                    dve.wait_ge(s.exp_done, i - TBUFS + 1)
                if i in (0, 4):
                    dve.wait_ge(s.logpen_ready, sq + 1)
                nc.vector.scalar_tensor_tensor(out=b.TS[:, i % TBUFS], in0=src, scalar=LN_PEN_SCALE, in1=b.LP[:, 2 * sq:2 * sq + 2, :],
                                               op0=ALU.add, op1=ALU.subtract).then_inc(s.scores_masked, 1)
                dve.wait_ge(s.scores_masked, i + 1)
                src = b.TS[:, i % TBUFS]
            nc.vector.tensor_reduce(b.MX[:, i % BUFS, :], src, AX.X, ALU.min).then_inc(s.max_taken, 1)
        g = group_at(i, LAG_D + 1)
        if g is not None:
            dve.wait_ge(s.recip_ready, g + 1)
            if g:
                dve.wait_ge(s.ctx_scaled, g)
            nc.vector.tensor_tensor(b.DT[:], PB[:, 6 + g % 2, :], b.RG[:, g % 2, :], ALU.mult).then_inc(s.den_taken, 1)


def pad_values(nc, s, b, link):
    link(nc.gpsimd.memset(b.VT[:], 0.0))
    nc.gpsimd.memset(b.VT[:, :, :, DH:DH + 1].rearrange("p t h c -> p (t h) c"), 1.0).then_inc(s.zeroed, 1)


def att_gpsimd(nc, pool, s, b, link):
    for g in range(NG):
        pool.wait_ge(s.den_taken, g + 1)
        link(nc.gpsimd.tensor_scalar(b.DT[:], b.DT[:], -1.0, 2.0, ALU.mult, ALU.add))
        link(nc.gpsimd.tensor_tensor(b.DT[:], b.DT[:], b.RG[:, g % 2, :], ALU.mult))
        nc.gpsimd.tensor_tensor(b.Z[:, g, :], b.OS[:, g % 2, :], b.DT[:], ALU.mult).then_inc(s.ctx_scaled, 1)


L0_SEMS = LN_SEMS + ATT_SEMS + GATE_SEMS + LINKS + "hid_ready hid_done ffn_ready y_ready xT_ready x_ready "


def layer0(nc, c, w, PB):
    with ExitStack() as ctx:
        s = semaphores(nc, ctx, L0_SEMS)
        s = s._replace(scores_read=s.exp_done)
        b = att_buffers(nc, ctx, "l0", H=[2, T])
        with nc.Block() as block:
            @block.tensor
            def _(pe):
                for t in range(TT):
                    last = nc.tensor.transpose(PB[:, 2, t * 128:(t + 1) * 128], c.XI0[:, t, :], c.ident)
                last.then_inc(s.xT_ready, 1)
                pe.wait_ge(s.x_ready, 1)
                ln_tensor(nc, pe, s, c, c.X[:], PB)

                def hidden_layer(i):
                    if i > 8:
                        return
                    if i < 8:
                        if i >= 2:
                            pe.wait_ge(s.hid_done, i - 1)
                        else:
                            pe.wait_ge(s.exp_done, UNITS)
                        nc.tensor.matmul(PB[:, 2 + i % 2, :], w.w1[:, i * 128:(i + 1) * 128], c.XN[:],
                                         start=True, stop=True).then_inc(s.hid_ready, 1)
                    if i:
                        pe.wait_ge(s.hid_done, i)
                        nc.tensor.matmul(PB[:, 1, :], w.w2[:, (i - 1) * 128:i * 128], b.H[:, (i - 1) % 2, :],
                                         start=i == 1, stop=i == 8).then_inc(s.ffn_ready, 1)

                att_tensor(nc, pe, s, c, w, b, PB, w.out, hidden_layer)

            @block.scalar
            def _(act):
                link = Link(act, s.act_link)
                act.preload_act_table_set(EXP_LN)
                ln_scalar(nc, act, s, c, PB, link)

                def hidden_layer(i):
                    if i < 8:
                        act.wait_ge(s.hid_ready, i + 1)
                        if i >= 2:
                            act.wait_ge(s.ffn_ready, i - 1)
                        nc.scalar.activation(b.H[:, i % 2, :], PB[:, 2 + i % 2, :], ACT.Relu, bias=w.b1c[:, i:i + 1]).then_inc(s.hid_done, 1)

                copy_queries(nc, act, s, b, PB, None, False)
                att_scalar(nc, act, s, c, b, PB, link, False, hidden_layer)
                act.wait_ge(s.y_ready, 1)
                gate_scalar(nc, act, s, c, link)

            @block.vector
            def _(dve):
                link = Link(dve, s.dve_link)
                dve.wait_ge(s.xT_ready, 1)
                nc.vector.tensor_copy(c.X[:], PB[:, 2, :]).then_inc(s.x_ready, 1)
                dve.wait_ge(s.x_ready, 1)
                ln_vector(nc, dve, s, c, c.XN[:], PB, link).then_inc(s.xn_ready, 1)
                copy_keys_values(nc, dve, s, w, b, PB, False)
                att_vector(nc, dve, s, c, b, PB, link, False)
                dve.wait_ge(s.att_ready, 1)
                dve.wait_ge(s.xn_ready, 1)
                link(nc.vector.tensor_tensor(c.S[:], PB[:, 0, :], c.XN[:], ALU.add))
                dve.wait_ge(s.ffn_ready, 8)
                nc.vector.tensor_scalar(c.Y[:], PB[:, 1, :], w.bout, None, ALU.add).then_inc(s.y_ready, 1)
                dve.wait_ge(s.y_ready, 1)
                gate_vector(nc, dve, s, c, link)

            @block.gpsimd
            def _(pool):
                link = Link(pool, s.pool_link)
                pad_values(nc, s, b, link)
                att_gpsimd(nc, pool, s, b, link)
        clear(nc, s)


L1_SEMS = (LN_SEMS + LINKS + "q_ready qf_relu qf_ready kv_ready kv_biased kf_ready kvsum_ready "
           "kvsum_masked num_ready den_ready recip_ready ctx_scaled att_ready att_done ones_set "
           "logits_ready logits_shifted route_exp pmax_ready route_ready pmaxT_ready routeT_ready xp_ready "
           "routeT_copied keep_ready hid_ready hid_done ffn_ready y_ready count_ready count_taken yT_ready saved next_loaded ")


def layer1(nc, c, w, r, it, x, x_mid, s_mid, PB):
    with ExitStack() as ctx:
        s = semaphores(nc, ctx, L1_SEMS)
        b = buffers(nc, ctx, "l1", QF=[T], KV=[TT, 257], KM=[NB, 128], KS=[NB, 128], RG=[T], LG=[T], CT=[T], DN=[T],
                    LO=[TT, E1], EX=[TT, E1], OH=[TT, E1], WK=[TT, E1], M1=[TT], SM=[TT], PX=[TT, 128],
                    XP=[T], OT=[T], PEN=[T, BF16], H=[2, T])
        with nc.Block() as block:
            @block.tensor
            def _(pe):
                ln_tensor(nc, pe, s, c, c.X[:], PB)
                pe.wait_ge(s.xn_ready, 1)
                for t in range(TT):
                    last = nc.tensor.matmul(PB[:, 0, t * E1:(t + 1) * E1], c.XN[:, t * 128:(t + 1) * 128], w.s,
                                            start=True, stop=True)
                last.then_inc(s.logits_ready, 1)
                for t in range(TT):
                    last = nc.tensor.matmul(PB[:, 2 + t // 2, t % 2 * 256:t % 2 * 256 + 256],
                                            c.XN[:, t * 128:(t + 1) * 128], w.kv, start=True, stop=True)
                last.then_inc(s.kv_ready, 1)
                nc.tensor.matmul(PB[:, 1, :], w.q, c.XN[:], start=True, stop=True).then_inc(s.q_ready, 1)
                pe.wait_ge(s.kf_ready, 1)
                for sq in range(NB):
                    for t in range(2):
                        last = nc.tensor.matmul(PB[:, 4 + sq, 0:129], b.KV[:, 2 * sq + t, 0:128], b.KV[:, 2 * sq + t, 128:257],
                                                start=t == 0, stop=t == 1)
                last.then_inc(s.kvsum_ready, 1)
                pe.wait_ge(s.pmax_ready, 1)
                pe.wait_ge(s.route_ready, 1)
                for t in range(TT):
                    last = nc.tensor.transpose(PB[:, 0, t * 128:(t + 1) * 128], b.PX[:, t, :], c.ident)
                last.then_inc(s.pmaxT_ready, 1)
                for t in range(TT):
                    last = nc.tensor.transpose(PB[0:E1, 2, t * 128:(t + 1) * 128], b.OH[:, t, :], c.ident)
                last.then_inc(s.routeT_ready, 1)
                pe.wait_ge(s.qf_relu, 1)
                for t in range(TT):
                    o = PB[:, 1, t * E1:(t + 1) * E1]
                    nc.tensor.matmul(o, c.before, b.OH[:, t, :], start=True, stop=t == 0)
                    for u in range(t):
                        nc.tensor.matmul(o, c.ones, b.OH[:, u, :], start=False, stop=u == t - 1)
                for t in range(TT):
                    last = nc.tensor.matmul(PB[:, 1, TT * E1:TT * E1 + E1], c.ones, b.OH[:, t, :], start=t == 0, stop=t == TT - 1)
                last.then_inc(s.count_ready, 1)
                pe.wait_ge(s.kvsum_masked, 1)
                pe.wait_ge(s.qf_ready, 1)
                for sq in range(NB):
                    last = nc.tensor.matmul(PB[:, 6, sq * SEQ:(sq + 1) * SEQ], b.KM[:, sq, :], b.QF[:, sq * SEQ:(sq + 1) * SEQ],
                                            start=True, stop=True)
                last.then_inc(s.num_ready, 1)
                for sq in range(NB):
                    last = nc.tensor.matmul(PB[:, 7, sq * SEQ:(sq + 1) * SEQ], b.KS[:, sq, :], b.QF[:, sq * SEQ:(sq + 1) * SEQ],
                                            start=True, stop=True)
                last.then_inc(s.den_ready, 1)
                pe.wait_ge(s.xp_ready, 1)
                pe.wait_ge(s.keep_ready, 1)
                for e in range(E1 + 1):
                    if e == E1 - 2:
                        pe.wait_ge(s.ctx_scaled, 1)
                        pe.wait_ge(s.count_taken, 1)
                        nc.tensor.matmul(PB[:, 1, :], w.o, b.CT[:], start=True, stop=True).then_inc(s.att_ready, 1)
                    if e < E1:
                        if e >= 2:
                            pe.wait_ge(s.hid_done, e - 1)
                        nc.tensor.matmul(PB[:, 4 + e % 2, :], w.w1[:, e * 128:(e + 1) * 128], b.XP[:], start=True, stop=False)
                        nc.tensor.matmul(PB[:, 4 + e % 2, :], c.identb[0:E1, e:e + 1].broadcast_to([E1, 128]), b.PEN[0:E1, :],
                                         start=False, stop=True).then_inc(s.hid_ready, 1)
                    if e:
                        pe.wait_ge(s.hid_done, e)
                        nc.tensor.matmul(PB[:, 3, :], w.w2[:, (e - 1) * 128:e * 128], b.H[:, (e - 1) % 2, :],
                                         start=e == 1, stop=False).then_inc(s.ffn_ready, 1)
                nc.tensor.matmul(PB[:, 3, :], w.b2[0:E1, :], b.OT[0:E1, :], start=False, stop=True).then_inc(s.ffn_ready, 1)
                pe.wait_ge(s.y_ready, 1)
                for t in range(TT):
                    last = nc.tensor.transpose(PB[:, 0, t * 128:(t + 1) * 128], c.Y[:, t * 128:(t + 1) * 128], c.ident)
                last.then_inc(s.yT_ready, 1)

            @block.scalar
            def _(act):
                link = Link(act, s.act_link)
                act.preload_act_table_set(EXP_LN)
                ln_scalar(nc, act, s, c, PB, link)
                act.wait_ge(s.logits_shifted, 1)
                nc.scalar.activation(b.EX[:], b.LO[:], ACT.Exp).then_inc(s.route_exp, 1)
                act.wait_ge(s.q_ready, 1)
                nc.scalar.activation(b.QF[:], PB[:, 1, :], ACT.Relu, bias=w.bq).then_inc(s.qf_relu, 1)
                act.wait_ge(s.routeT_ready, 1)
                nc.scalar.activation(b.OT[0:E1, :], PB[0:E1, 2, :], ACT.Copy).then_inc(s.routeT_copied, 1)
                act.wait_ge(s.den_ready, 1)
                link(nc.scalar.activation(b.LG[:], PB[:, 7, :], ACT.Ln, bias=c.aeps))
                nc.scalar.activation(b.RG[:], b.LG[:], ACT.Exp, scale=-1.0).then_inc(s.recip_ready, 1)
                for e in range(E1):
                    act.wait_ge(s.hid_ready, e + 1)
                    if e >= 2:
                        act.wait_ge(s.ffn_ready, e - 1)
                    nc.scalar.activation(b.H[:, e % 2, :], PB[:, 4 + e % 2, :], ACT.Relu, bias=w.b1[:, e:e + 1]).then_inc(s.hid_done, 1)

            @block.vector
            def _(dve):
                link = Link(dve, s.dve_link)
                ln_vector(nc, dve, s, c, c.XN[:], PB, link).then_inc(s.xn_ready, 1)
                dve.wait_ge(s.logits_ready, 1)
                link(nc.vector.tensor_tensor(b.LO[:], PB[:, 0, 0:TT * E1].rearrange("p (t e) -> p t e", e=E1),
                                             w.bs.unsqueeze(1).broadcast_to([128, TT, E1]), ALU.add))
                link(nc.vector.tensor_reduce(b.M1[:], b.LO[:], AX.X, ALU.max))
                nc.vector.tensor_tensor(b.LO[:], b.LO[:], b.M1[:].unsqueeze(2).broadcast_to([128, TT, E1]),
                                        ALU.subtract).then_inc(s.logits_shifted, 1)
                dve.wait_ge(s.logits_shifted, 1)
                link(nc.vector.tensor_scalar(b.OH[:], b.LO[:], 0.0, None, ALU.is_equal))
                link(nc.vector.tensor_tensor(b.WK[:], b.OH[:], c.rank8.unsqueeze(1).broadcast_to([128, TT, E1]), ALU.mult))
                link(nc.vector.tensor_reduce(b.M1[:], b.WK[:], AX.X, ALU.max))
                nc.vector.tensor_tensor(b.OH[:], b.WK[:], b.M1[:].unsqueeze(2).broadcast_to([128, TT, E1]),
                                        ALU.is_equal).then_inc(s.route_ready, 1)
                dve.wait_ge(s.kv_ready, 1)
                dve.wait_ge(s.ones_set, 1)
                link(nc.vector.tensor_tensor(b.KV[:, :, 0:256], PB[:, 2:4, :].rearrange("p a (t k) -> p (a t) k", k=256),
                                             w.bkv.unsqueeze(1).broadcast_to([128, TT, 256]), ALU.add))
                for par in range(2):
                    last = nc.vector.tensor_scalar(b.KV[:, par:TT:2, 0:128], b.KV[:, par:TT:2, 0:128], 0.0,
                                                   c.dectok[:, par:par + 1], ALU.max, ALU.mult)
                last.then_inc(s.kf_ready, 1)
                dve.wait_ge(s.route_exp, 1)
                link(nc.vector.tensor_reduce(b.SM[:], b.EX[:], AX.X, ALU.add))
                link(nc.vector.reciprocal(b.SM[:], b.SM[:]))
                nc.vector.tensor_copy(b.PX[:], b.SM[:].unsqueeze(2).broadcast_to([128, TT, 128])).then_inc(s.pmax_ready, 1)
                dve.wait_ge(s.kvsum_ready, 1)
                for sq in range(NB):
                    nc.vector.tensor_tensor(b.KM[:, sq, :], PB[:, 4 + sq, 0:128], c.bd8, ALU.mult)
                    last = nc.vector.tensor_scalar(b.KS[:, sq, :], c.bd8, PB[:, 4 + sq, 128:129], None, ALU.mult)
                last.then_inc(s.kvsum_masked, 1)
                dve.wait_ge(s.pmaxT_ready, 1)
                nc.vector.tensor_tensor(b.XP[:], c.XN[:], PB[:, 0, :], ALU.mult).then_inc(s.xp_ready, 1)
                dve.wait_ge(s.routeT_copied, 1)
                nc.vector.tensor_scalar(b.PEN[0:E1, :], b.OT[0:E1, :], -1.0, BIG, ALU.add, ALU.mult).then_inc(s.keep_ready, 1)
                dve.wait_ge(s.count_ready, 1)
                link(nc.vector.tensor_tensor(b.WK[:], PB[:, 1, 0:TT * E1].rearrange("p (t e) -> p t e", e=E1),
                                             r.base[:].unsqueeze(1).broadcast_to([128, TT, E1]), ALU.add))
                nc.vector.tensor_tensor(r.base[:], r.base[:], PB[:, 1, TT * E1:TT * E1 + E1], ALU.add).then_inc(s.count_taken, 1)
                link(nc.vector.tensor_tensor(b.WK[:], b.WK[:], b.OH[:], ALU.mult))
                nc.vector.tensor_reduce(r.rank[:, bass.ts(it, TT)], b.WK[:], AX.X, ALU.add)
                nc.vector.tensor_copy(r.route[:, bass.ts(it, TT), :], b.OH[:])
                dve.wait_ge(s.recip_ready, 1)
                dve.wait_ge(s.num_ready, 1)
                link(nc.vector.tensor_scalar(b.DN[:], PB[:, 7, :], c.aeps, None, ALU.add))
                divide(nc, b.CT[:], PB[:, 6, :], b.DN[:], b.RG[:], b.LG[:], link).then_inc(s.ctx_scaled, 1)
                dve.wait_ge(s.att_ready, 1)
                nc.vector.tensor_scalar(c.S[:], PB[:, 1, :], w.bo, None, ALU.add).then_inc(s.att_done, 1)
                dve.wait_ge(s.ffn_ready, E1 + 1)
                nc.vector.tensor_copy(c.Y[:], PB[:, 3, :]).then_inc(s.y_ready, 1)
                dve.wait_ge(s.yT_ready, 1)
                nc.vector.tensor_copy(r.y[:, bass.ts(it, TT), :], PB[:, 0, :].rearrange("p (t d) -> p t d", d=D))

            @block.sync
            def _(sp):
                sp.dma_start(c.XI0[:], x[bass.ts(it + 1, T), :].rearrange("(t p) d -> p t d", p=128)).then_inc(s.next_loaded, 16)
                sp.dma_start(x_mid[bass.ts(it, 128), :], c.X[:]).then_inc(s.saved, 16)
                sp.wait_ge(s.att_done, 1)
                sp.dma_start(s_mid[bass.ts(it, 128), :], c.S[:]).then_inc(s.saved, 16)
                sp.wait_ge(s.saved, 32)
                sp.wait_ge(s.next_loaded, 16)

            @block.gpsimd
            def _(pool):
                nc.gpsimd.memset(b.KV[:, :, 256:257].rearrange("p t o -> p (t o)"), 1.0).then_inc(s.ones_set, 1)
                pool.wait_ge(s.qf_relu, 1)
                nc.gpsimd.tensor_tensor(b.QF[:].rearrange("p (s n) -> p s n", n=SEQ), b.QF[:].rearrange("p (s n) -> p s n", n=SEQ),
                                        c.decrow.unsqueeze(1).broadcast_to([128, NB, SEQ]), ALU.mult).then_inc(s.qf_ready, 1)
        clear(nc, s)


def place_tokens(nc, c, r, tiles, x_mid, s_mid, y_mid):
    with ExitStack() as ctx:
        s = semaphores(nc, ctx, "dve_link places_ready scattered padded")
        off = ctx.enter_context(nc.sbuf_tensor("off", [128, E1], F32))
        pos = ctx.enter_context(nc.sbuf_tensor("pos", [128, tiles], F32))
        idx = ctx.enter_context(nc.sbuf_tensor("idx", [128, tiles], mybir.dt.int32))
        with nc.Block() as block:
            @block.vector
            def _(dve):
                link = Link(dve, s.dve_link)
                link(nc.vector.memset(off[:, 0:1], 0.0))
                for e in range(1, E1):
                    link(nc.vector.tensor_tensor(off[:, e:e + 1], off[:, e - 1:e], r.base[:, e - 1:e], ALU.add))
                link(nc.vector.tensor_tensor(r.route[:], r.route[:], off[:].unsqueeze(1).broadcast_to([128, tiles, E1]), ALU.mult))
                link(nc.vector.tensor_reduce(pos[:], r.route[:], AX.X, ALU.add))
                nc.vector.tensor_tensor(idx[:], pos[:], r.rank[:], ALU.add).then_inc(s.places_ready, 1)

            @block.sync
            def _(sp):
                sp.dma_start(x_mid[tiles // TT * 128:, :], c.X[:]).then_inc(s.padded, 16)
                sp.dma_start(s_mid[tiles // TT * 128:, :], c.S[:]).then_inc(s.padded, 16)
                sp.dma_start(y_mid[tiles * 128:, :].rearrange("(t p) d -> p t d", p=128), r.y[:, 0:TT, :]).then_inc(s.padded, 16)
                sp.wait_ge(s.padded, 48)

            @block.gpsimd
            def _(pool):
                pool.wait_ge(s.places_ready, 1)
                for t in range(tiles):
                    pool.indirect_dma_start(out=y_mid, out_offset=bass.IndirectOffsetOnAxis(ap=idx[:, t:t + 1], axis=0),
                                            in_=r.y[:, t, :], in_offset=None).then_inc(s.scattered, 16)
                pool.wait_ge(s.scattered, 16 * tiles)
        clear(nc, s)


L2_SEMS = (LN_SEMS + GATE_SEMS + LINKS + "yT_ready y_taken taken_over next_loaded xm_ready xz_ready xi_copied conv_done silu_x silu_z xd_ready dtl_copied "
           "bc_copied dt_ready dt_raw dt_exp dt_u dt_log delta_ready decay_ready b_ready c_ready drive_ready "
           "c_copied state_ready part_ready y_summed y_gated mamba_ready pads_set "
           "logits_ready logits_shifted route_exp gates_ready gate_spread gateT_ready w2_loaded0 w2_loaded1 hid_ready "
           "hid_even hid_odd ffn_ready bank_done weighted acc_done ")
HID_BANKS = (2, 3, 7)
HTILES = HID2 // 128


def load_middle(nc, sp, c, chunk, x_mid, s_mid, y_mid, loaded):
    sp.dma_start(c.XI0[:], y_mid[bass.ts(chunk, T), :].rearrange("(t p) d -> p t d", p=128)).then_inc(loaded, 16)
    sp.dma_start(c.SI0[:], s_mid[bass.ts(chunk, 128), :]).then_inc(loaded, 16)
    sp.dma_start(c.X1[:], x_mid[bass.ts(chunk, 128), :]).then_inc(loaded, 16)


def layer2(nc, c, w, wf, it, x_mid, s_mid, y_mid, PB):
    with ExitStack() as ctx:
        s = semaphores(nc, ctx, L2_SEMS)
        b = buffers(nc, ctx, "l2", XM=[T], XI=[2, NB, TAPS - 1 + SEQ], XC=[2, T], ZS=[2, T], DL=[2, T], DU=[2, T],
                    EE=[2, T], UU=[2, T], DTL=[T], BC=[T], CN=[2, T], DA=[2, 2, T], DB=[2, 2, T], ST=[2, 2, T],
                    CH=[2, T], YA=[2, T], H=[4, T], YB=[2, T], GS=[2, TT, 128], WB=[2, 2 * HID2],
                    LO=[TT, E2], EX=[TT, E2], OA=[TT, E2], OB=[TT, E2], WK=[TT, E2], M1=[TT], SM=[TT])
        loaded = (s.w2_loaded0, s.w2_loaded1)

        def hid_wait(eng, k):
            if k % 2:
                eng.wait_ge(s.hid_odd, (k + 1) // 2)
            else:
                eng.wait_ge(s.hid_even, k // 2 + 1)

        with nc.Block() as block:
            @block.sync
            def _(sp):
                for e in range(E2):
                    if e >= 2:
                        sp.wait_ge(s.ffn_ready, HTILES * (e - 1))
                    sp.dma_start(b.WB[:, e % 2, :], wf[e, :, :]).then_inc(loaded[e % 2], 16)
                    if e == 2:
                        sp.wait_ge(s.taken_over, 1)
                        load_middle(nc, sp, c, it + 1, x_mid, s_mid, y_mid, s.next_loaded)
                sp.wait_ge(s.next_loaded, 48)

            @block.tensor
            def _(pe):
                for t in range(TT):
                    last = nc.tensor.transpose(PB[:, 2, t * 128:(t + 1) * 128], c.XI0[:, t, :], c.ident)
                last.then_inc(s.yT_ready, 1)
                pe.wait_ge(s.taken_over, 1)
                ln_tensor(nc, pe, s, c, c.X[:], PB)
                pe.wait_ge(s.xn_ready, 1)
                ln_tensor(nc, pe, s, c, c.XN[:], PB, 1)
                for t in range(TT):
                    last = nc.tensor.matmul(PB[:, 4, t * E2:(t + 1) * E2], c.XN[:, t * 128:(t + 1) * 128], w.r,
                                            start=True, stop=True)
                last.then_inc(s.logits_ready, 1)
                pe.wait_ge(s.xm_ready, 1)
                for k in range(4):
                    nc.tensor.matmul(PB[:, k, :], w.win[:, k * 128:(k + 1) * 128], b.XM[:], start=True, stop=True).then_inc(s.xz_ready, 1)
                pe.wait_ge(s.silu_x, 2)
                for k in range(2):
                    last = nc.tensor.matmul(PB[0:DTR, 5, :], w.xp[:, k * 40:k * 40 + DTR], b.XC[:, k, :], start=k == 0, stop=k == 1)
                for k in range(2):
                    last = nc.tensor.matmul(PB[0:32, 6, :], w.xp[:, k * 40 + DTR:k * 40 + 40], b.XC[:, k, :], start=k == 0, stop=k == 1)
                last.then_inc(s.xd_ready, 1)
                pe.wait_ge(s.dtl_copied, 1)
                pe.wait_ge(s.xi_copied, 1)
                pe.wait_ge(s.silu_z, 2)
                for k in range(2):
                    last = nc.tensor.matmul(PB[:, k, :], w.dt[0:DTR, k * 128:(k + 1) * 128], b.DTL[0:DTR, :], start=True, stop=True)
                last.then_inc(s.dt_ready, 1)
                pe.wait_ge(s.bc_copied, 1)
                pe.wait_ge(s.dt_raw, 1)
                pe.wait_ge(s.gates_ready, 1)
                for n in range(NS):
                    if n:
                        pe.wait_ge(s.drive_ready, n)
                    nc.tensor.matmul(PB[:, 0, :], c.ident[0:32, n:n + 1].broadcast_to([32, 128]),
                                     b.BC[0:32, :], start=True, stop=True).then_inc(s.b_ready, 1)
                    if n:
                        pe.wait_ge(s.c_copied, n)
                    nc.tensor.matmul(PB[:, 1, :], c.ident[0:32, NS + n:NS + n + 1].broadcast_to([32, 128]),
                                     b.BC[0:32, :], start=True, stop=True).then_inc(s.c_ready, 1)
                    for i in range(HTILES + 2):
                        if i < HTILES:
                            k = HTILES * n + i
                            if i == 0:
                                pe.wait_ge(loaded[n % 2], 16 * (n // 2 + 1))
                            if k >= 3:
                                hid_wait(pe, k - 3)
                            nc.tensor.matmul(PB[:, HID_BANKS[k % 3], :], b.WB[:, n % 2, i * 128:(i + 1) * 128], c.XN[:],
                                             start=True, stop=True).then_inc(s.hid_ready, 1)
                        if i >= 2:
                            k = HTILES * n + i - 2
                            hid_wait(pe, k)
                            if i == 2 and n >= 2:
                                pe.wait_ge(s.bank_done, n - 1)
                            nc.tensor.matmul(PB[:, 4 + n % 2, :], b.WB[:, n % 2, HID2 + (i - 2) * 128:HID2 + (i - 1) * 128],
                                             b.H[:, k % 4, :], start=i == 2, stop=i == HTILES + 1).then_inc(s.ffn_ready, 1)
                    pe.wait_ge(s.gate_spread, n + 1)
                    if n:
                        pe.wait_ge(s.weighted, n)
                    for t in range(TT):
                        last = nc.tensor.transpose(PB[:, 6, t * 128:(t + 1) * 128], b.GS[:, n % 2, t, :], c.ident)
                    last.then_inc(s.gateT_ready, 1)
                pe.wait_ge(s.y_gated, 1)
                for k in range(2):
                    last = nc.tensor.matmul(PB[:, 0, :], w.out[:, k * 128:(k + 1) * 128], b.EE[:, k, :], start=k == 0, stop=k == 1)
                last.then_inc(s.mamba_ready, 1)

            @block.scalar
            def _(act):
                link = Link(act, s.act_link)
                act.preload_act_table_set(EXP_LN)
                act.wait_ge(s.y_taken, 1)
                gate_scalar(nc, act, s, c, link)
                ln_scalar(nc, act, s, c, PB, link)
                ln_scalar(nc, act, s, c, PB, link, 1)
                act.wait_ge(s.logits_shifted, 1)
                nc.scalar.activation(b.EX[:], b.LO[:], ACT.Exp).then_inc(s.route_exp, 1)
                for k in range(2):
                    act.wait_ge(s.xz_ready, 3 + k)
                    nc.scalar.activation(b.ZS[:, k, :], PB[:, 2 + k, :], ACT.Silu).then_inc(s.silu_z, 1)
                for k in range(2):
                    act.wait_ge(s.conv_done, k + 1)
                    nc.scalar.activation(b.XC[:, k, :], b.XC[:, k, :], ACT.Silu).then_inc(s.silu_x, 1)
                act.preload_act_table_set(EXP_LN)
                act.wait_ge(s.xd_ready, 1)
                nc.scalar.activation(b.DTL[0:DTR, :], PB[0:DTR, 5, :], ACT.Copy).then_inc(s.dtl_copied, 1)
                nc.scalar.activation(b.BC[0:32, :], PB[0:32, 6, :], ACT.Copy).then_inc(s.bc_copied, 1)
                act.wait_ge(s.dt_raw, 1)
                link(nc.scalar.activation(b.EE[:], b.DL[:], ACT.Abs))
                nc.scalar.activation(b.EE[:], b.EE[:], ACT.Exp, scale=-1.0).then_inc(s.dt_exp, 1)
                act.preload_act_table_set(LN)
                act.wait_ge(s.dt_u, 1)
                nc.scalar.activation(b.DU[:], b.UU[:], ACT.Ln).then_inc(s.dt_log, 1)
                act.preload_act_table_set(EXP_LN)
                act.wait_ge(s.delta_ready, 1)
                act.wait_ge(s.pads_set, 1)

                def bank_out(e):
                    act.wait_ge(s.ffn_ready, HTILES * (e + 1))
                    if e >= 2:
                        act.wait_ge(s.acc_done, e - 1)
                    nc.scalar.activation(b.YB[:, e % 2, :], PB[:, 4 + e % 2, :], ACT.Identity, bias=w.b2[:, e:e + 1]).then_inc(s.bank_done, 1)

                def hidden(k):
                    act.wait_ge(s.hid_ready, k + 1)
                    if k >= 4:
                        act.wait_ge(s.ffn_ready, k - 3)
                    nc.scalar.activation(b.H[:, k % 4, :], PB[:, HID_BANKS[k % 3], :], ACT.Relu, bias=w.b1[:, k:k + 1]).then_inc(s.hid_even, 1)

                for n in range(NS):
                    if n >= 2:
                        act.wait_ge(s.state_ready, n - 1)
                    for k in range(2):
                        last = nc.scalar.activation(b.DA[:, n % 2, k, :].rearrange("p (s t) -> p s t", t=SEQ)[:, :, 1:SEQ],
                                                    b.DL[:, k, :].rearrange("p (s t) -> p s t", t=SEQ)[:, :, 1:SEQ],
                                                    ACT.Exp, scale=c.aneg[:, k * NS + n:k * NS + n + 1])
                    last.then_inc(s.decay_ready, 1)
                    act.wait_ge(s.c_ready, n + 1)
                    if n >= 2:
                        act.wait_ge(s.part_ready, n - 1)
                    nc.scalar.activation(b.CN[:, n % 2, :], PB[:, 1, :], ACT.Copy).then_inc(s.c_copied, 1)
                    hidden(HTILES * n)
                    hidden(HTILES * n + 2)
                    if n:
                        bank_out(n - 1)
                bank_out(E2 - 1)
                act.wait_ge(s.acc_done, E2)
                gate_scalar(nc, act, s, c, link, 1)

            @block.vector
            def _(dve):
                link = Link(dve, s.dve_link)
                nc.vector.tensor_copy(c.X[:], c.X1[:])
                dve.wait_ge(s.yT_ready, 1)
                nc.vector.tensor_copy(c.Y[:], PB[:, 2, :]).then_inc(s.y_taken, 1)
                dve.wait_ge(s.y_taken, 1)
                gate_vector(nc, dve, s, c._replace(S=c.SI0), link)
                dve.sem_inc(s.taken_over, 1)
                ln_vector(nc, dve, s, c, c.XN[:], PB, link).then_inc(s.xn_ready, 1)
                dve.wait_ge(s.xn_ready, 1)
                link(ln_vector(nc, dve, s, c, b.XM[:], PB, link, 1))
                nc.vector.tensor_scalar(b.XM[:], b.XM[:], w.g, w.b, ALU.mult, ALU.add).then_inc(s.xm_ready, 1)
                dve.wait_ge(s.logits_ready, 1)
                spread = lambda x, k: x.unsqueeze(2).broadcast_to([128, TT, k])
                rank = c.rank16.unsqueeze(1).broadcast_to([128, TT, E2])
                link(nc.vector.tensor_tensor(b.LO[:], PB[:, 4, 0:TT * E2].rearrange("p (t e) -> p t e", e=E2),
                                             w.br.unsqueeze(1).broadcast_to([128, TT, E2]), ALU.add))
                link(nc.vector.tensor_reduce(b.M1[:], b.LO[:], AX.X, ALU.max))
                nc.vector.tensor_tensor(b.LO[:], b.LO[:], spread(b.M1[:], E2), ALU.subtract).then_inc(s.logits_shifted, 1)
                dve.wait_ge(s.logits_shifted, 1)
                dve.wait_ge(s.pads_set, 1)
                dve.wait_ge(s.xz_ready, 2)
                for k in range(2):
                    last = nc.vector.tensor_copy(b.XI[:, k, :, TAPS - 1:], PB[:, k, :].rearrange("p (s t) -> p s t", t=SEQ))
                last.then_inc(s.xi_copied, 1)
                dve.wait_ge(s.xi_copied, 1)
                for k in range(2):
                    xc = b.XC[:, k, :].rearrange("p (s t) -> p s t", t=SEQ)
                    link(nc.vector.tensor_scalar(xc, b.XI[:, k, :, 0:SEQ], w.conv[:, k * TAPS:k * TAPS + 1], w.cb[:, k:k + 1],
                                                 ALU.mult, ALU.add))
                    for tap in range(1, TAPS):
                        last = nc.vector.scalar_tensor_tensor(out=xc, in0=b.XI[:, k, :, tap:tap + SEQ],
                                                              scalar=w.conv[:, k * TAPS + tap:k * TAPS + tap + 1], in1=xc,
                                                              op0=ALU.mult, op1=ALU.add)
                        if tap < TAPS - 1:
                            link(last)
                    last.then_inc(s.conv_done, 1)
                link(nc.vector.tensor_scalar(b.OA[:], b.LO[:], 0.0, None, ALU.is_equal))
                link(nc.vector.tensor_tensor(b.WK[:], b.OA[:], rank, ALU.mult))
                link(nc.vector.tensor_reduce(b.M1[:], b.WK[:], AX.X, ALU.max))
                link(nc.vector.tensor_tensor(b.OA[:], b.WK[:], spread(b.M1[:], E2), ALU.is_equal))
                link(nc.vector.scalar_tensor_tensor(out=b.WK[:], in0=b.OA[:], scalar=-BIG, in1=b.LO[:], op0=ALU.mult, op1=ALU.add))
                link(nc.vector.tensor_reduce(b.M1[:], b.WK[:], AX.X, ALU.max))
                link(nc.vector.tensor_tensor(b.OB[:], b.WK[:], spread(b.M1[:], E2), ALU.is_equal))
                link(nc.vector.tensor_tensor(b.WK[:], b.OB[:], rank, ALU.mult))
                link(nc.vector.tensor_reduce(b.M1[:], b.WK[:], AX.X, ALU.max))
                link(nc.vector.tensor_tensor(b.OB[:], b.WK[:], spread(b.M1[:], E2), ALU.is_equal))
                link(nc.vector.tensor_tensor(b.OA[:], b.OA[:], b.OB[:], ALU.add))
                dve.wait_ge(s.route_exp, 1)
                link(nc.vector.tensor_tensor(b.OA[:], b.OA[:], b.EX[:], ALU.mult))
                link(nc.vector.tensor_reduce(b.SM[:], b.EX[:], AX.X, ALU.add))
                link(nc.vector.reciprocal(b.SM[:], b.SM[:]))
                nc.vector.tensor_tensor(b.OA[:], b.OA[:], spread(b.SM[:], E2), ALU.mult).then_inc(s.gates_ready, 1)
                dve.wait_ge(s.dt_ready, 1)
                for k in range(2):
                    last = nc.vector.tensor_scalar(b.DL[:, k, :], PB[:, k, :], w.dtb[:, k:k + 1], None, ALU.add)
                last.then_inc(s.dt_raw, 1)
                dve.wait_ge(s.dt_raw, 1)
                dve.wait_ge(s.dt_exp, 1)
                nc.vector.tensor_scalar(b.UU[:], b.EE[:], 1.0, None, ALU.add).then_inc(s.dt_u, 1)
                dve.wait_ge(s.dt_u, 1)
                link(nc.vector.scalar_tensor_tensor(out=b.EE[:], in0=b.UU[:], scalar=-1.0, in1=b.EE[:], op0=ALU.add, op1=ALU.subtract))
                dve.wait_ge(s.dt_log, 1)
                link(nc.vector.tensor_tensor(b.EE[:], b.DU[:], b.EE[:], ALU.subtract))
                nc.vector.scalar_tensor_tensor(out=b.DL[:], in0=b.DL[:], scalar=0.0, in1=b.EE[:], op0=ALU.max,
                                               op1=ALU.add).then_inc(s.delta_ready, 1)
                dve.wait_ge(s.delta_ready, 1)
                dve.wait_ge(s.silu_x, 2)
                link(nc.vector.tensor_tensor(b.DU[:], b.DL[:], b.XC[:], ALU.mult))

                def hidden(k):
                    dve.wait_ge(s.hid_ready, k + 1)
                    if k >= 4:
                        dve.wait_ge(s.ffn_ready, k - 3)
                    nc.vector.tensor_scalar(b.H[:, k % 4, :], PB[:, HID_BANKS[k % 3], :], w.b1[:, k:k + 1], 0.0,
                                            ALU.add, ALU.max).then_inc(s.hid_odd, 1)

                def weigh(e):
                    dve.wait_ge(s.bank_done, e + 1)
                    dve.wait_ge(s.gateT_ready, e + 1)
                    nc.vector.tensor_tensor(b.YB[:, e % 2, :], b.YB[:, e % 2, :], PB[:, 6, :], ALU.mult).then_inc(s.weighted, 1)

                for n in range(NS):
                    dve.wait_ge(s.b_ready, n + 1)
                    nc.vector.tensor_tensor(b.DB[:, n % 2, :, :], b.DU[:], PB[:, 0, :].unsqueeze(1).broadcast_to([128, 2, T]),
                                            ALU.mult).then_inc(s.drive_ready, 1)
                    hidden(HTILES * n + 1)
                    dve.wait_ge(s.drive_ready, n + 1)
                    dve.wait_ge(s.decay_ready, n + 1)
                    if n >= 2:
                        dve.wait_ge(s.part_ready, n - 1)
                    nc.vector.tensor_tensor_scan(b.ST[:, n % 2].rearrange("p k t -> p (k t)"), b.DA[:, n % 2].rearrange("p k t -> p (k t)"),
                                                 b.DB[:, n % 2].rearrange("p k t -> p (k t)"), 0.0, ALU.mult, ALU.add).then_inc(s.state_ready, 1)
                    dve.wait_ge(s.state_ready, n + 1)
                    hidden(HTILES * n + 3)
                    if n:
                        weigh(n - 1)
                dve.wait_ge(s.y_summed, 1)
                for k in range(2):
                    last = nc.vector.scalar_tensor_tensor(out=b.YA[:, k, :], in0=b.XC[:, k, :], scalar=w.dskip[:, k:k + 1],
                                                          in1=b.YA[:, k, :], op0=ALU.mult, op1=ALU.add)
                link(last)
                nc.vector.tensor_tensor(b.EE[:], b.YA[:], b.ZS[:], ALU.mult).then_inc(s.y_gated, 1)
                weigh(E2 - 1)
                dve.wait_ge(s.mamba_ready, 1)
                link(nc.vector.tensor_tensor(c.S[:], PB[:, 0, :], c.XN[:], ALU.add))
                dve.wait_ge(s.acc_done, E2)
                gate_vector(nc, dve, s, c, link, 1)

            @block.gpsimd
            def _(pool):
                link = Link(pool, s.pool_link)
                for k in range(2):
                    nc.gpsimd.memset(b.XI[:, k, :, 0:TAPS - 1], 0.0)
                last = nc.gpsimd.memset(b.DA[:].rearrange("p a k (s t) -> p (a k s) t", t=SEQ)[:, :, 0:1], 0.0)
                last.then_inc(s.pads_set, 1)

                def add_bank(e):
                    pool.wait_ge(s.weighted, e + 1)
                    if e == 0:
                        nc.gpsimd.tensor_copy(c.Y[:], b.YB[:, 0, :]).then_inc(s.acc_done, 1)
                    else:
                        nc.gpsimd.tensor_tensor(c.Y[:], c.Y[:], b.YB[:, e % 2, :], ALU.add).then_inc(s.acc_done, 1)
                    pool.wait_ge(s.acc_done, e + 1)

                pool.wait_ge(s.gates_ready, 1)
                for n in range(NS):
                    if n >= 2:
                        pool.wait_ge(s.gateT_ready, n - 1)
                    nc.gpsimd.tensor_copy(b.GS[:, n % 2], b.OA[:, :, n:n + 1].broadcast_to([128, TT, 128])).then_inc(s.gate_spread, 1)
                    pool.wait_ge(s.state_ready, n + 1)
                    pool.wait_ge(s.c_copied, n + 1)
                    cn = b.CN[:, n % 2, :].unsqueeze(1).broadcast_to([128, 2, T])
                    out = b.CH if n else b.YA
                    nc.gpsimd.tensor_tensor(out[:], b.ST[:, n % 2], cn, ALU.mult).then_inc(s.part_ready, 1)
                    pool.wait_ge(s.part_ready, n + 1)
                    if n:
                        last = nc.gpsimd.tensor_tensor(b.YA[:], b.YA[:], b.CH[:], ALU.add)
                        if n < NS - 1:
                            link(last)
                        else:
                            last.then_inc(s.y_summed, 1)
                        add_bank(n - 1)
                add_bank(E2 - 1)
        clear(nc, s)


L3_SEMS = (LN_SEMS + ATT_SEMS + LINKS + "logpen_ready gate_ready gate_raw gate_exp gate_u "
           "gi_ready pen_ready ")


def layer3_attention(nc, c, w, PB):
    with ExitStack() as ctx:
        s = semaphores(nc, ctx, L3_SEMS)
        s = s._replace(scores_read=s.scores_masked)
        b = att_buffers(nc, ctx, "l3", TS=[TBUFS, 2, SEQ], LP=[TT, SEQ], PQ=[TT, SEQ], T1=[TT, SEQ], T2=[TT, SEQ], GA=[T + TT],
                        GU=[T + TT], GJ=[T], NJ=[T], GI=[TT], AI=[TT], PI=[TT])

        def penalties(sq, link):
            tiles = (2 * sq, 2 * sq + 1)
            gates = slice(sq * SEQ, (sq + 1) * SEQ)
            ai = lambda t: b.AI[:, t:t + 1]
            for t in tiles:
                nc.vector.tensor_scalar(b.T2[:, t, :], b.GJ[:, gates], ai(t), 1.0, ALU.add, ALU.min)
                last = nc.vector.tensor_scalar(b.T1[:, t, :], b.NJ[:, gates], ai(t), 0.0, ALU.add, ALU.max)
            link(last)
            for t in tiles:
                nc.vector.tensor_scalar(b.T1[:, t, :], b.T1[:, t, :], ai(t), None, ALU.mult)
                last = nc.vector.tensor_scalar(b.T2[:, t, :], b.T2[:, t, :], b.GI[:, t:t + 1], None, ALU.mult)
            link(last)
            both = slice(2 * sq, 2 * sq + 2)
            link(nc.vector.tensor_tensor(b.T1[:, both], b.T1[:, both], b.T2[:, both], ALU.add))
            for t in tiles:
                last = nc.vector.tensor_scalar(b.T2[:, t, :], c.dist[:, t % 2 * SEQ:(t % 2 + 1) * SEQ], b.PI[:, t:t + 1], 1.0, ALU.add, ALU.min)
            link(last)
            link(nc.vector.tensor_scalar(b.T2[:, both], b.T2[:, both], 1e-32, None, ALU.max))
            link(nc.vector.tensor_tensor(b.T1[:, both], b.T1[:, both], b.T2[:, both], ALU.mult))
            return nc.vector.tensor_scalar(b.PQ[:, both], b.T1[:, both], 1e-32, None, ALU.max)

        with nc.Block() as block:
            @block.tensor
            def _(pe):
                ln_tensor(nc, pe, s, c, c.X[:], PB)
                pe.wait_ge(s.xn_ready, 1)
                nc.tensor.matmul(PB[:, 2, :], w.grow, c.XN[:], start=True, stop=True)
                for t in range(TT):
                    last = nc.tensor.matmul(PB[:, 3, t:t + 1], c.XN[:, t * 128:(t + 1) * 128], w.gcol, start=True, stop=True)
                last.then_inc(s.gate_ready, 1)
                pe.wait_ge(s.gate_raw, 1)
                att_tensor(nc, pe, s, c, w, b, PB, c.unpad)

            @block.scalar
            def _(act):
                link = Link(act, s.act_link)
                act.preload_act_table_set(EXP_LN)
                ln_scalar(nc, act, s, c, PB, link)
                act.wait_ge(s.gate_raw, 1)
                link(nc.scalar.activation(b.GU[:], b.GA[:], ACT.Abs))
                link(nc.scalar.activation(b.GU[:], b.GU[:], ACT.Exp, scale=-1.0))
                act.preload_act_table_set(LN)
                nc.scalar.activation(b.GU[:], b.GU[:], ACT.Ln, bias=c.one).then_inc(s.gate_exp, 1)
                act.preload_act_table_set(EXP_LN)
                act.wait_ge(s.gate_u, 1)
                link(nc.scalar.activation(b.GJ[:], b.GU[:, 0:T], ACT.Exp))
                nc.scalar.activation(b.GI[:], b.GU[:, T:T + TT], ACT.Exp).then_inc(s.gi_ready, 1)
                act.wait_ge(s.gi_ready, 1)
                link(nc.scalar.activation(b.PI[:], b.GI[:], ACT.Exp, scale=-float(np.log(SEQ - 2)), bias=c.pow))
                act.sem_inc(s.gi_ready, 1)
                act.preload_act_table_set(LN)
                copy_queries(nc, act, s, b, PB, c.bqs, True)
                for sq in range(NB):
                    act.wait_ge(s.pen_ready, sq + 1)
                    nc.scalar.activation(b.LP[:, 2 * sq:2 * sq + 2], b.PQ[:, 2 * sq:2 * sq + 2], ACT.Ln, scale=PEN_SCALE).then_inc(s.logpen_ready, 1)
                act.preload_act_table_set(EXP_LN)
                att_scalar(nc, act, s, c, b, PB, link, True)

            @block.vector
            def _(dve):
                link = Link(dve, s.dve_link)
                ln_vector(nc, dve, s, c, c.XN[:], PB, link).then_inc(s.xn_ready, 1)
                dve.wait_ge(s.gate_ready, 1)
                nc.vector.tensor_scalar(b.GA[:, 0:T], PB[:, 2, :], w.bg, None, ALU.add)
                nc.vector.tensor_scalar(b.GA[:, T:T + TT], PB[:, 3, 0:TT], w.bg, None, ALU.add).then_inc(s.gate_raw, 1)
                dve.wait_ge(s.gate_raw, 1)
                dve.wait_ge(s.gate_exp, 1)
                nc.vector.scalar_tensor_tensor(out=b.GU[:], in0=b.GA[:], scalar=0.0, in1=b.GU[:], op0=ALU.min,
                                               op1=ALU.subtract).then_inc(s.gate_u, 1)
                copy_keys_values(nc, dve, s, w, b, PB, True)
                dve.wait_ge(s.gi_ready, 2)
                link(nc.vector.tensor_scalar(b.NJ[:], b.GJ[:], -1.0, None, ALU.mult))
                link(nc.vector.tensor_scalar(b.AI[:], b.GI[:], -1.0, 1.0, ALU.mult, ALU.add))
                for sq in range(NB):
                    penalties(sq, link).then_inc(s.pen_ready, 1)
                att_vector(nc, dve, s, c, b, PB, link, True)
                dve.wait_ge(s.att_ready, 1)
                link(nc.vector.tensor_copy(c.S[:], PB[:, 0, :]))

            @block.gpsimd
            def _(pool):
                link = Link(pool, s.pool_link)
                pad_values(nc, s, b, link)
                att_gpsimd(nc, pool, s, b, link)
        clear(nc, s)


L3F_SEMS = (LN_SEMS + GATE_SEMS + LINKS + "pad_set shift_done raw_ready raw_copied squared norm_ready norm_taken norm_guarded rot_ready "
            "cos_done sin_done rnorm_ready rot_summed qk_ready v_ready v_copied win_ready win_max win_exped win_recip prob_ready probT_ready "
            "probT_copied ctx_ready ctx_copied o_ready x_added hn_ready gate_in_ready gelu_done val_ready hid_ready "
            "out_ready layer_done x_done xT_ready x_copied x_stored ")
NW = SEQ // WIN
SCORES = 4
SCORE_BANKS = (0, 1, 5, 7)
NT = LI // 128
FT = [(0, 128), (128, 128), (256, HIDL - 256)]


def layer3_ffn(nc, c, ws, it, out, PB):
    with ExitStack() as ctx:
        s = semaphores(nc, ctx, L3F_SEMS)
        b = buffers(nc, ctx, "l3f", HS=[NB, SEQ], HN=[T], RW=[2, T], SQ=[2, T], C1=[2, T], C2=[2, T], NR=[2, T], RN=[2, T],
                    QK=[2 * NT, T], VL=[NB, 3, LI], MX=[NW], MN=[SCORES, NW], SM=[NW], RS=[SCORES, NW], PP=[SCORES, T], PT=[2, T], OF=[NT, T],
                    G=[3, T], HH=[3, T])
        F = c.XN
        U, A = 2 * NT, NT * NB

        with nc.Block() as block:
            @block.tensor
            def _(pe):
                for l in range(DEPTH):
                    w, u0, a0 = ws[l], l * U, l * A
                    pe.wait_ge(s.shift_done, 2 * l + 1)
                    hs = b.HS[:].rearrange("p s t -> p (s t)")
                    for u in range(U + 1):
                        if u < U:
                            if u >= 2:
                                pe.wait_ge(s.raw_copied, u0 + u - 1)
                            nc.tensor.matmul(PB[:, u % 2, :], w.qkv[:, u * 128:(u + 1) * 128], hs, start=True, stop=True).then_inc(s.raw_ready, 1)
                        if u < NB * 3:
                            sq, o = divmod(u, 3)
                            if u >= 2:
                                pe.wait_ge(s.v_copied, NB * 3 * l + u - 1)
                            t0 = sq * SEQ + o * WIN
                            nc.tensor.matmul(PB[:, 6 + u % 2, :], hs[:, t0:t0 + 128], w.qkv[:, 2 * LI:3 * LI], start=True, stop=True).then_inc(s.v_ready, 1)
                        if u:
                            v = u - 1
                            if v >= 2:
                                pe.wait_ge(s.norm_taken, u0 + v - 1)
                                pe.wait_ge(s.sin_done, u0 + v - 1)
                            pe.wait_ge(s.raw_copied, u0 + v + 1)
                            nc.tensor.matmul(PB[:, 4 + v % 2, :], c.rotq[l] if v < NT else c.rotk[l], b.RW[:, v % 2, :],
                                             start=True, stop=True).then_inc(s.rot_ready, 1)
                            pe.wait_ge(s.squared, u0 + v + 1)
                            nc.tensor.matmul(PB[:, 2 + v % 2, :], c.bd64, b.SQ[:, v % 2, :], start=True, stop=True).then_inc(s.norm_ready, 1)
                    pe.wait_ge(s.v_copied, NB * 3 * (l + 1))
                    pe.wait_ge(s.norm_taken, u0 + U)
                    pe.wait_ge(s.sin_done, u0 + U)
                    pe.wait_ge(s.qk_ready, u0 + U)
                    for m in range(A + 4):
                        if m < A:
                            hp, sq = divmod(m, NB)
                            k = SCORE_BANKS[m % SCORES]
                            if m >= SCORES:
                                pe.wait_ge(s.win_exped, a0 + m - SCORES + 1)
                            for h in range(2):
                                r = slice(LD * h, LD * h + LD)
                                for win in range(NW):
                                    q0 = sq * SEQ + win * WIN
                                    k0 = q0 - WIN if win else q0
                                    nc.tensor.matmul(PB[r, k, win * 128:win * 128 + 2 * WIN], b.QK[r, hp, q0:q0 + WIN],
                                                     b.QK[r, NT + hp, k0:k0 + 2 * WIN], start=win == 0, stop=False,
                                                     skip_group_check=True)
                            last = nc.tensor.matmul(PB[:, k, :], c.identb, c.windowb, start=False, stop=True, skip_group_check=True)
                            last.then_inc(s.win_ready, 1)
                        v = m - 3
                        if 0 <= v < A:
                            pe.wait_ge(s.prob_ready, a0 + v + 1)
                            if v >= 2:
                                pe.wait_ge(s.probT_copied, a0 + v - 1)
                            for win in range(NW):
                                last = nc.tensor.transpose(PB[:, 2 + v % 2, win * 128:(win + 1) * 128],
                                                           b.PP[:, v % SCORES, win * 128:(win + 1) * 128], c.ident)
                            last.then_inc(s.probT_ready, 1)
                        v = m - 4
                        if 0 <= v < A:
                            hp, sq = divmod(v, NB)
                            if sq == 0 and hp >= 2:
                                pe.wait_ge(s.ctx_copied, l * NT + hp - 1)
                            pe.wait_ge(s.probT_copied, a0 + v + 1)
                            k = 4 + 2 * (hp % 2)
                            for h in range(2):
                                f0 = (2 * hp + h) * LD
                                for win in range(NW):
                                    o0 = sq * SEQ + win * WIN
                                    last = nc.tensor.matmul(PB[LD * h:LD * h + LD, k, o0:o0 + WIN], b.VL[:, sq, max(win - 1, 0), f0:f0 + LD],
                                                            b.PT[:, v % 2, win * 128 + h * WIN:win * 128 + h * WIN + WIN],
                                                            start=True, stop=True, tile_position=(0, LD * h))
                            last.then_inc(s.ctx_ready, 1)
                    for t in range(NT):
                        pe.wait_ge(s.ctx_copied, l * NT + t + 1)
                        last = nc.tensor.matmul(PB[:, 2, :], w.o[:, t * 128:(t + 1) * 128], b.OF[:, t, :], start=t == 0, stop=t == NT - 1)
                    last.then_inc(s.o_ready, 1)
                    pe.wait_ge(s.shift_done, 2 * l + 2)
                    ln_tensor(nc, pe, s, c, hs, PB, l)
                    pe.wait_ge(s.hn_ready, l + 1)
                    for i, (f0, fn) in enumerate(FT):
                        nc.tensor.matmul(PB[0:fn, 2 + i, :], w.wg[:, f0:f0 + fn], b.HN[:], start=True, stop=True).then_inc(s.gate_in_ready, 1)
                        nc.tensor.matmul(PB[0:fn, 5 + i, :], w.wa[:, f0:f0 + fn], b.HN[:], start=True, stop=True).then_inc(s.val_ready, 1)
                    for i, (f0, fn) in enumerate(FT):
                        pe.wait_ge(s.hid_ready, 3 * l + i + 1)
                        last = nc.tensor.matmul(PB[:, 0, :], w.w2[0:fn, i * 128:(i + 1) * 128], b.HH[0:fn, i, :], start=i == 0, stop=i == 2)
                    last.then_inc(s.out_ready, 1)
                pe.wait_ge(s.x_done, 1)
                for t in range(TT):
                    last = nc.tensor.transpose(PB[:, 1, t * 128:(t + 1) * 128], c.X[:, t * 128:(t + 1) * 128], c.ident)
                last.then_inc(s.xT_ready, 1)

            @block.scalar
            def _(act):
                link = Link(act, s.act_link)
                act.preload_act_table_set(EXP_LN)
                for l in range(DEPTH):
                    w, u0, a0 = ws[l], l * U, l * A
                    for u in range(U + 1):
                        if u < U:
                            act.wait_ge(s.raw_ready, u0 + u + 1)
                            if u >= 2:
                                act.wait_ge(s.squared, u0 + u - 1)
                                act.wait_ge(s.rot_ready, u0 + u - 1)
                                act.wait_ge(s.cos_done, u0 + u - 1)
                            nc.scalar.activation(b.RW[:, u % 2, :], PB[:, u % 2, :], ACT.Copy).then_inc(s.raw_copied, 1)
                        if u < NB * 3:
                            sq, o = divmod(u, 3)
                            act.wait_ge(s.v_ready, NB * 3 * l + u + 1)
                            nc.scalar.activation(b.VL[:, sq, o, :], PB[:, 6 + u % 2, :], ACT.Copy).then_inc(s.v_copied, 1)
                        if u:
                            v = u - 1
                            act.wait_ge(s.norm_guarded, u0 + v + 1)
                            link(nc.scalar.activation(b.NR[:, v % 2, :], b.NR[:, v % 2, :], ACT.Ln, scale=NORM_SCALE))
                            if v >= 2:
                                act.wait_ge(s.qk_ready, u0 + v - 1)
                            nc.scalar.activation(b.RN[:, v % 2, :], b.NR[:, v % 2, :], ACT.Exp, scale=-0.5, bias=c.lnnorm).then_inc(s.rnorm_ready, 1)
                    for m in range(A + 4):
                        v = m - 4
                        if v >= 0:
                            act.wait_ge(s.probT_ready, a0 + v + 1)
                            if v >= 2:
                                act.wait_ge(s.ctx_ready, a0 + v - 1)
                            nc.scalar.activation(b.PT[:, v % 2, :], PB[:, 2 + v % 2, :], ACT.Copy).then_inc(s.probT_copied, 1)
                        if m < A:
                            act.wait_ge(s.win_max, a0 + m + 1)
                            if m >= SCORES:
                                act.wait_ge(s.probT_ready, a0 + m - SCORES + 1)
                            for win in range(NW):
                                w0 = slice(win * 128, (win + 1) * 128)
                                last = nc.scalar.activation(b.PP[:, m % SCORES, w0], PB[:, SCORE_BANKS[m % SCORES], w0], ACT.Exp,
                                                            scale=8.0, bias=b.MN[:, m % SCORES, win:win + 1])
                            last.then_inc(s.win_exped, 1)
                    ln_scalar(nc, act, s, c, PB, link, l)
                    for i, (f0, fn) in enumerate(FT):
                        act.wait_ge(s.gate_in_ready, 3 * l + i + 1)
                        nc.scalar.activation(b.G[0:fn, i, :], PB[0:fn, 2 + i, :], ACT.Gelu, bias=w.bgl[0:fn, i:i + 1]).then_inc(s.gelu_done, 1)
                    act.preload_act_table_set(EXP_LN)
                act.wait_ge(s.layer_done, DEPTH)
                gate_scalar(nc, act, s, c, link)

            @block.vector
            def _(dve):
                link = Link(dve, s.dve_link)

                def shift():
                    nc.vector.tensor_copy(b.HS[0:64, :, :], F[0:64, :].rearrange("p (s t) -> p s t", t=SEQ))
                    nc.vector.tensor_copy(b.HS[64:128, :, 1:SEQ],
                                          F[64:128, :].rearrange("p (s t) -> p s t", t=SEQ)[:, :, 0:SEQ - 1]).then_inc(s.shift_done, 1)

                dve.wait_ge(s.pad_set, 1)
                two = lambda x: x.unsqueeze(1).broadcast_to([128, NB, SEQ])
                for l in range(DEPTH):
                    w, u0, a0 = ws[l], l * U, l * A
                    shift()
                    dve.wait_ge(s.shift_done, 2 * l + 1)
                    for u in range(U + 1):
                        seq = lambda x: x.rearrange("p (s t) -> p s t", t=SEQ)
                        if u < U:
                            cos, sin = (c.qcos, c.qsin) if u < NT else (c.kcos, c.ksin)
                            dve.wait_ge(s.raw_copied, u0 + u + 1)
                            if u >= 2:
                                dve.wait_ge(s.rot_summed, u0 + u - 1)
                                dve.wait_ge(s.qk_ready, u0 + u - 1)
                            nc.vector.scalar_tensor_tensor(out=seq(b.C1[:, u % 2, :]), in0=seq(b.RW[:, u % 2, :]),
                                                           scalar=w.qs if u < NT else w.ks, in1=two(cos),
                                                           op0=ALU.mult, op1=ALU.mult).then_inc(s.cos_done, 1)
                            dve.wait_ge(s.rot_ready, u0 + u + 1)
                            nc.vector.tensor_tensor(seq(b.C2[:, u % 2, :]), seq(PB[:, 4 + u % 2, :]), two(sin), ALU.mult).then_inc(s.sin_done, 1)
                            dve.wait_ge(s.norm_ready, u0 + u + 1)
                            if u >= 2:
                                dve.wait_ge(s.rnorm_ready, u0 + u - 1)
                            nc.vector.tensor_scalar(b.NR[:, u % 2, :], PB[:, 2 + u % 2, :], 1e-24, None, ALU.max).then_inc(s.norm_taken, 1)
                            dve.wait_ge(s.norm_taken, u0 + u + 1)
                            dve.sem_inc(s.norm_guarded, 1)
                        if u:
                            v = u - 1
                            dve.wait_ge(s.rnorm_ready, u0 + v + 1)
                            dve.wait_ge(s.rot_summed, u0 + v + 1)
                            nc.vector.tensor_tensor(b.QK[:, v, :], b.C1[:, v % 2, :], b.RN[:, v % 2, :], ALU.mult).then_inc(s.qk_ready, 1)
                    dve.wait_ge(s.qk_ready, u0 + U)
                    for m in range(A + 5):
                        v = m - 5
                        if 0 <= v and v % NB == NB - 1:
                            hp = v // NB
                            dve.wait_ge(s.ctx_ready, a0 + v + 1)
                            nc.vector.tensor_copy(b.OF[:, hp, :], PB[:, 4 + 2 * (hp % 2), :]).then_inc(s.ctx_copied, 1)
                        if m < A:
                            dve.wait_ge(s.win_ready, a0 + m + 1)
                            link(nc.vector.tensor_reduce(b.MX[:], PB[:, SCORE_BANKS[m % SCORES], :].rearrange("p (w k) -> p w k", k=128),
                                                         AX.X, ALU.max))
                            nc.vector.tensor_scalar(b.MN[:, m % SCORES, :], b.MX[:], -8.0, None, ALU.mult).then_inc(s.win_max, 1)
                            dve.wait_ge(s.win_max, a0 + m + 1)
                        v = m - 1
                        if 0 <= v < A:
                            dve.wait_ge(s.win_exped, a0 + v + 1)
                            link(nc.vector.tensor_reduce(b.SM[:], b.PP[:, v % SCORES, :].rearrange("p (w k) -> p w k", k=128), AX.X, ALU.add))
                            nc.vector.reciprocal(b.RS[:, v % SCORES, :], b.SM[:]).then_inc(s.win_recip, 1)
                            dve.wait_ge(s.win_recip, a0 + v + 1)
                    dve.wait_ge(s.o_ready, l + 1)
                    link(nc.vector.tensor_tensor(F[:], F[:], PB[:, 2, :], ALU.add))
                    shift()
                    dve.wait_ge(s.shift_done, 2 * l + 2)
                    link(ln_vector(nc, dve, s, c, b.HN[:], PB, link, l))
                    nc.vector.tensor_scalar(b.HN[:], b.HN[:], w.lg, w.lb, ALU.mult, ALU.add).then_inc(s.hn_ready, 1)
                    for i, (f0, fn) in enumerate(FT):
                        dve.wait_ge(s.gelu_done, 3 * l + i + 1)
                        dve.wait_ge(s.val_ready, 3 * l + i + 1)
                        nc.vector.scalar_tensor_tensor(out=b.HH[0:fn, i, :], in0=PB[0:fn, 5 + i, :], scalar=w.ba[0:fn, i:i + 1],
                                                       in1=b.G[0:fn, i, :], op0=ALU.add, op1=ALU.mult).then_inc(s.hid_ready, 1)
                    dve.wait_ge(s.out_ready, l + 1)
                    dst = F if l < DEPTH - 1 else c.Y
                    nc.vector.scalar_tensor_tensor(out=dst[:], in0=PB[:, 0, :], scalar=w.b2, in1=F[:],
                                                   op0=ALU.add, op1=ALU.add).then_inc(s.layer_done, 1)
                    dve.wait_ge(s.layer_done, l + 1)
                gate_vector(nc, dve, s, c, link)
                dve.sem_inc(s.x_done, 1)
                dve.wait_ge(s.xT_ready, 1)
                nc.vector.tensor_copy(b.G[:, 0, :], PB[:, 1, :]).then_inc(s.x_copied, 1)

            @block.sync
            def _(sp):
                sp.wait_ge(s.x_copied, 1)
                sp.dma_start(out[bass.ts(it, T), :].rearrange("(t p) d -> p t d", p=128),
                             b.G[:, 0, :].rearrange("p (t d) -> p t d", d=D)).then_inc(s.x_stored, 16)
                sp.wait_ge(s.x_stored, 16)

            @block.gpsimd
            def _(pool):
                nc.gpsimd.memset(b.HS[64:128, :, 0:1], 0.0).then_inc(s.pad_set, 1)
                for l in range(DEPTH):
                    u0 = l * U
                    for u in range(U + 1):
                        if u < U:
                            pool.wait_ge(s.raw_copied, u0 + u + 1)
                            if u >= 2:
                                pool.wait_ge(s.norm_ready, u0 + u - 1)
                            nc.gpsimd.tensor_tensor(b.SQ[:, u % 2, :], b.RW[:, u % 2, :], b.RW[:, u % 2, :], ALU.mult).then_inc(s.squared, 1)
                        if u:
                            v = u - 1
                            pool.wait_ge(s.cos_done, u0 + v + 1)
                            pool.wait_ge(s.sin_done, u0 + v + 1)
                            nc.gpsimd.tensor_tensor(b.C1[:, v % 2, :], b.C1[:, v % 2, :], b.C2[:, v % 2, :], ALU.add).then_inc(s.rot_summed, 1)
                    for m in range(A):
                        pool.wait_ge(s.win_recip, l * A + m + 1)
                        pp = b.PP[:, m % SCORES, :].rearrange("p (w k) -> p w k", k=128)
                        nc.gpsimd.tensor_tensor(pp, pp, b.RS[:, m % SCORES, :].unsqueeze(2).broadcast_to([128, NW, 128]),
                                                ALU.mult).then_inc(s.prob_ready, 1)
        clear(nc, s)


def network(nc, x, consts, w0, w1, w2, w2f, w3, w3f, out):
    tokens = out.shape[0]
    chunks = tokens // T
    with ExitStack() as ctx:
        def sb(name, parts):
            return ctx.enter_context(nc.sbuf_tensor(name, [128, columns(parts)[1]], F32))

        pieces = [("consts", CONSTS, consts), ("w0s", W0, w0), ("w1s", W1, w1), ("w2s", W2, w2), ("w3s", W3, w3), ("w3fs", W3F, w3f)]
        tiles = {n: sb(n, parts) for n, parts, _ in pieces}
        c = view(tiles["consts"], CONSTS)
        v0, v1, v2, v3 = view(tiles["w0s"], W0), view(tiles["w1s"], W1), view(tiles["w2s"], W2), view(tiles["w3s"], W3)
        per_layer = columns(W3F)[1] // DEPTH
        ws = [view(tiles["w3fs"][:, l * per_layer:(l + 1) * per_layer], W3F_LAYER) for l in range(DEPTH)]
        keep = buffers(nc, ctx, "keep", X=[T], XN=[T], S=[T], Y=[T], lnc=[T], lnsq=[T], lnr=[T], lnt=[T], ga=[T], gb=[T],
                       aneg=[2 * NS], bqs=[4], XI0=[TT, 128], SI0=[T], X1=[T])
        identb = ctx.enter_context(nc.sbuf_tensor("identb", [128, 128], BF16))
        windowb = ctx.enter_context(nc.sbuf_tensor("windowb", [128, 512], BF16))
        rots = ctx.enter_context(nc.sbuf_tensor("rots", [128, 2 * DEPTH, 128], F32))
        c = record(**c._asdict(), **keep._asdict(), identb=identb[:], windowb=windowb[:],
                   rotq=[rots[:, 2 * l, :] for l in range(DEPTH)], rotk=[rots[:, 2 * l + 1, :] for l in range(DEPTH)])
        PB = ctx.enter_context(nc.psum_tensor("PB", [128, 8, 512], F32))

        with ExitStack() as pro:
            s = semaphores(nc, pro, "x_loaded loaded exped folded fold_ready dve_link")
            with nc.Block() as block:
                @block.sync
                def _(sp):
                    sp.dma_start(c.XI0[:], x[0:T, :].rearrange("(t p) d -> p t d", p=128)).then_inc(s.x_loaded, 16)
                    for n, _, src in pieces:
                        sp.dma_start(tiles[n][:], src).then_inc(s.loaded, 16)
                    sp.wait_ge(s.x_loaded, 16)

                @block.scalar
                def _(act):
                    act.wait_ge(s.loaded, 16 * len(pieces))
                    nc.scalar.activation(c.aneg[:], v2.alog, ACT.Exp).then_inc(s.exped, 1)

                @block.tensor
                def _(pe):
                    pe.wait_ge(s.loaded, 16 * len(pieces))
                    nc.tensor.matmul(PB[:, 0, 0:1], v0.woutm[0:64, :], v0.b2m[0:64, :], start=True, stop=True).then_inc(s.folded, 1)

                @block.vector
                def _(dve):
                    link = Link(dve, s.dve_link)
                    dve.wait_ge(s.loaded, 16 * len(pieces))
                    win = v0.win.unsqueeze(2).broadcast_to([128, 64, 16])
                    w1 = v0.w1.rearrange("p (m h) -> p m h", h=16)
                    nc.vector.tensor_tensor(w1, w1, win, ALU.mult)
                    w2 = v0.w2.rearrange("p (i d) -> p i d", d=128)
                    nc.vector.tensor_tensor(w2, w2, v0.w2c.unsqueeze(2).broadcast_to([128, 8, 128]), ALU.mult)
                    link(nc.vector.tensor_tensor(v0.w1c, v0.w1c, v0.binc, ALU.mult))
                    nc.vector.tensor_tensor(v0.b1c, v0.b1c, v0.w1c, ALU.add)
                    dve.wait_ge(s.folded, 1)
                    nc.vector.tensor_tensor(v0.bout, v0.bout, PB[:, 0, 0:1], ALU.add)
                    dve.wait_ge(s.exped, 1)
                    nc.vector.tensor_scalar(c.aneg[:], c.aneg[:], -1.0, None, ALU.mult)
                    nc.vector.tensor_scalar(c.bqs[:], v3.bq, float(DH) ** -0.5, None, ALU.mult)
                    nc.vector.tensor_copy(c.identb, c.ident)
                    nc.vector.tensor_copy(c.windowb, c.window)
                    for l in range(DEPTH):
                        nc.vector.tensor_scalar(c.rotq[l], c.rot, ws[l].qs, None, ALU.mult)
                        nc.vector.tensor_scalar(c.rotk[l], c.rot, ws[l].ks, None, ALU.mult)
            clear(nc, s)

        x_mid = nc.dram_tensor("x_mid", ((chunks + 1) * 128, T), F32, kind="Internal").ap()
        s_mid = nc.dram_tensor("s_mid", ((chunks + 1) * 128, T), F32, kind="Internal").ap()
        y_mid = nc.dram_tensor("y_mid", (tokens + T, D), F32, kind="Internal").ap()

        with ExitStack() as first:
            r = record(base=first.enter_context(nc.sbuf_tensor("base", [128, E1], F32)),
                                rank=first.enter_context(nc.sbuf_tensor("rank", [128, tokens // 128], F32)),
                                route=first.enter_context(nc.sbuf_tensor("route", [128, tokens // 128, E1], F32)),
                                y=first.enter_context(nc.sbuf_tensor("y", [128, tokens // 128, D], F32)))
            with nc.Block() as block:
                @block.vector
                def _(dve):
                    nc.vector.memset(r.base[:], 0.0)
            with nc.Fori(0, chunks) as it:
                layer0(nc, c, v0, PB)
                layer1(nc, c, v1, r, it, x, x_mid, s_mid, PB)
            place_tokens(nc, c, r, tokens // 128, x_mid, s_mid, y_mid)

        with ExitStack() as io:
            s = semaphores(nc, io, "first_loaded")
            with nc.Block() as block:
                @block.sync
                def _(sp):
                    load_middle(nc, sp, c, 0, x_mid, s_mid, y_mid, s.first_loaded)
                    sp.wait_ge(s.first_loaded, 48)
            clear(nc, s)
        with nc.Fori(0, chunks) as it:
            layer2(nc, c, v2, w2f, it, x_mid, s_mid, y_mid, PB)
            layer3_attention(nc, c, v3, PB)
            layer3_ffn(nc, c, ws, it, out, PB)


def constants():
    p = np.arange(128)
    k = {}
    k["ident"] = np.eye(128)
    k["mean"] = np.full((128, 128), 1.0 / D)
    k["centre"] = np.eye(128) - 1.0 / D
    k["ones"] = np.ones((128, 128))
    k["before"] = p[:, None] < p[None, :]
    k["sumsel"] = (p[:, None] == p[None, :] // 32 * 32 + DH)
    k["bd8"] = p[:, None] // DH == p[None, :] // DH
    k["bd64"] = p[:, None] // LD == p[None, :] // LD
    un = np.zeros((128, 4, 128))
    for g in range(4):
        for j in range(4):
            for d in range(DH):
                un[32 * j + d, g, (4 * g + j) * DH + d] = 1
    k["unpad"] = un.reshape(128, 512)
    dec = np.exp(-np.arange(SEQ, dtype=np.float32) / np.float32(SEQ))
    k["decrow"] = np.broadcast_to(dec, (128, SEQ))
    k["dectok"] = dec.reshape(2, 128).T
    k["rank8"] = np.broadcast_to(np.arange(E1, 0, -1), (128, E1))
    k["rank16"] = np.broadcast_to(np.arange(E2, 0, -1), (128, E2))
    q = np.arange(2)[None, :, None] * 128 + p[:, None, None]
    k["dist"] = (2.0 - np.abs(q - np.arange(SEQ)[None, None, :])).reshape(128, 2 * SEQ)
    f = np.float32
    half = np.arange(0, LD, 2, dtype=f)
    inv = f(1.0) / f(10000.0) ** (half / f(LD))
    t = np.arange(SEQ, dtype=f)
    fr = (t[:, None] * inv[None, :]).astype(f)
    base = (half + f(0.4 * LD)) / f(1.4 * LD)
    scale = base[None, :] ** ((t - SEQ // 2) / f(WIN // 2))[:, None]
    rep = lambda a: np.tile(a.T, (4, 1))
    cos, sin = np.cos(fr), np.sin(fr)
    k["qcos"], k["qsin"], k["kcos"], k["ksin"] = rep(cos * scale), rep(sin * scale), rep(cos / scale), rep(sin / scale)
    rot = np.zeros((128, 128))
    for m in range(128):
        if m % LD < LD // 2:
            rot[m + LD // 2, m] = -1
        else:
            rot[m - LD // 2, m] = 1
    k["rot"] = rot
    a, cc, win = p[:, None, None] % WIN, np.arange(128)[None, None, :], np.arange(NW)[None, :, None]
    ok = np.where(win == 0, (cc < WIN) & (cc <= a), (cc - WIN <= a) & (a <= cc))
    k["window"] = np.where(ok, 0.0, -1.0e30).reshape(128, NW * 128)
    one = np.ones((128, 1))
    k["eps"], k["one"], k["aeps"] = one * 1e-5, one, one * 1e-6
    k["pow"] = one * np.log(SEQ - 2)
    k["lnnorm"] = one * 0.5 * np.log(NORM_SCALE)
    return pack(CONSTS, k)


def pack(parts, arrays):
    at, width = columns(parts)
    out = np.zeros((128, width), np.float32)
    for n, (a, w) in at.items():
        out[:arrays[n].shape[0], a:a + w] = arrays[n]
    return out


def heads_apart(a):
    out = np.zeros((a.shape[0], NG, 4, 32), a.dtype)
    out[:, :, :, :DH] = a.reshape(a.shape[0], NG, 4, DH)
    return out.reshape(a.shape[0], 512)


def layouts(i):
    rep = lambda a: np.broadcast_to(a, (128, a.size))
    cols = lambda a: a.reshape(-1, 128).T
    out0 = heads_apart(i["L0_attn_Wout"].T).reshape(D, NG, 128).transpose(2, 1, 0).reshape(128, 512)
    w0 = dict(q=heads_apart(i["L0_attn_Wq"]), k=heads_apart(i["L0_attn_Wk"]), v=i["L0_attn_Wv"], out=out0,
              w1=rep(i["L0_ffn_W1"].reshape(-1)), win=i["L0_ffn_Win"],
              w2=np.repeat(i["L0_ffn_Wout"], 16, axis=0).reshape(8, 128, 128).transpose(1, 0, 2).reshape(128, 1024),
              w1c=cols(i["L0_ffn_W1"]), b1c=cols(i["L0_ffn_b1"]), binc=cols(np.repeat(i["L0_ffn_bin_"], 16)),
              w2c=cols(i["L0_ffn_W2"]), woutm=i["L0_ffn_Wout"], b2m=i["L0_ffn_b2"][:, None], bout=i["L0_ffn_bout"][:, None])
    side = lambda a: a.transpose(1, 0, 2).reshape(a.shape[1], -1)
    w1 = dict(q=i["L1_attn_W_q"].T, kv=np.concatenate([i["L1_attn_W_k"].T, i["L1_attn_W_v"].T], 1), o=i["L1_attn_W_o"].T,
              bq=i["L1_attn_b_q"][:, None], bkv=rep(np.concatenate([i["L1_attn_b_k"], i["L1_attn_b_v"]])),
              bo=i["L1_attn_b_o"][:, None], s=i["L1_ffn_Ws"].T, bs=rep(i["L1_ffn_bs"]), w1=side(i["L1_ffn_W1"]),
              b1=i["L1_ffn_b1"].T, w2=side(i["L1_ffn_W2"]), b2=i["L1_ffn_b2"])
    halves = lambda a: side(a.reshape(2, 128, -1))
    w2 = dict(g=i["L2_attn_ln_g"][:, None], b=i["L2_attn_ln_b"][:, None], win=i["L2_attn_W_in"],
              conv=halves(i["L2_attn_conv_w"]), cb=cols(i["L2_attn_conv_b"]), xp=halves(i["L2_attn_W_xp"]), dt=i["L2_attn_W_dt"],
              dtb=cols(i["L2_attn_dt_bias"]), alog=halves(i["L2_attn_A_log"]), dskip=cols(i["L2_attn_D_skip"]),
              out=halves(i["L2_attn_W_out"]), r=i["L2_ffn_Wr"], br=rep(i["L2_ffn_br"]), b1=cols(i["L2_ffn_b1"]), b2=i["L2_ffn_b2"].T)
    w2f = np.concatenate([i["L2_ffn_W1"], i["L2_ffn_W2"].reshape(E2, 4, 128, D).transpose(0, 2, 1, 3).reshape(E2, 128, 512)], 2)
    w3 = dict(q=heads_apart(i["L3_attn_Wq"]), k=heads_apart(i["L3_attn_Wk"]), v=i["L3_attn_Wv"], bv=rep(i["L3_attn_bv"]),
              bq=heads_apart(i["L3_attn_bq"][None]).reshape(NG, 128).T, bk=heads_apart(i["L3_attn_bk"][None]).reshape(NG, 128).T.copy(),
              gcol=i["L3_attn_Wg"], grow=np.broadcast_to(i["L3_attn_Wg"], (D, 128)), bg=rep(i["L3_attn_bg"]))
    w3["bk"][DH::32, :] = 1.0
    w3f = {}
    for l in range(DEPTH):
        p = lambda n: i["L3_ffn_" + n][l]
        tail = lambda a: np.concatenate([a, np.zeros((384 - HIDL, *a.shape[1:]), a.dtype)])
        w3f |= {f"qkv{l}": p("wqkv"), f"qs{l}": np.tile(p("q_scale"), 2)[:, None], f"ks{l}": np.tile(p("k_scale"), 2)[:, None],
                f"o{l}": side(p("wo").reshape(NT, 128, D)), f"lg{l}": p("ln_g")[:, None], f"lb{l}": p("ln_b")[:, None],
                f"wa{l}": p("w1")[:, :HIDL], f"wg{l}": p("w1")[:, HIDL:], f"ba{l}": cols(tail(p("b1")[:HIDL])),
                f"bgl{l}": cols(tail(p("b1")[HIDL:])), f"w2{l}": side(tail(p("w2")).reshape(3, 128, D)), f"b2{l}": p("b2")[:, None]}
    x = i["L0_attn_x"].reshape(-1, D)
    x = np.concatenate([x, np.zeros((T, D), x.dtype)])
    return dict(x=x, consts=constants(), w0=pack(W0, w0), w1=pack(W1, w1), w2=pack(W2, w2), w2f=w2f,
                w3=pack(W3, w3), w3f=pack(W3F, w3f))



def kernel(**inputs):
    import concourse.bacc as _bacc
    from concourse.bass_utils import run_bass_kernel_spmd as _run

    nc = _bacc.Bacc("TRN2", target_bir_lowering=False, num_devices=1)
    i = {n: np.asarray(a) for n, a in inputs.items()}
    shape = i["L0_attn_x"].shape
    arrays, args = {}, []
    for name, a in layouts(i).items():
        a = np.ascontiguousarray(a)
        arrays[f"in_{name}_dram"] = a
        args.append(nc.dram_tensor(f"in_{name}_dram", a.shape, mybir.dt.from_np(a.dtype), kind="ExternalInput").ap())
    out = nc.dram_tensor("out_0_dram", (shape[0] * shape[1], D), F32, kind="ExternalOutput").ap()
    network(nc, *args, out)
    r = _run(nc, [arrays], core_ids=[0])
    return r.results[0]["out_0_dram"].reshape(shape)
```
